# Optimizing a Trainium2 kernel written in Bass

```python
import numpy as np
import jax
import jax.numpy as jnp

def _softmax(x, axis=-1):
    return jax.nn.softmax(x, axis=axis)

def _gelu(x):
    return jax.nn.gelu(x, approximate=True)

def _silu(x):
    return jax.nn.silu(x)

def _sigmoid(x):
    return jax.nn.sigmoid(x)

def _layernorm(x, axis=-1, eps=1e-05):
    m = jnp.mean(x, axis=axis, keepdims=True)
    v = jnp.var(x, axis=axis, keepdims=True)
    return (x - m) / jnp.sqrt(v + eps)

def _scatter_add(tgt, idx, src, axis=0):
    return tgt.at[idx].add(src)

def _segment_sum(src, seg, n):
    return jax.ops.segment_sum(src, seg, n)
kernel_name = 'mk_decoder_postln_d2_seqx_r8_18190d'

def setup_inputs(seed: int=0):
    np.random.seed(seed)
    _w = jnp.asarray

    def _rec_inputs():
        import jax
        import jax.numpy as jnp
        _rk = jax.random.key(seed)
        x = 7.22e-05 + 1 * jax.random.normal(jax.random.fold_in(_rk, 1), (16, 128, 256), jnp.float32)
        _lenS = 128 - jax.random.randint(jax.random.fold_in(_rk, 7), (16,), 0, max(1, 128 // 4) + 1, jnp.int32)
        _lenS2 = 128 - jax.random.randint(jax.random.fold_in(_rk, 8), (16,), 0, max(1, 128 // 4) + 1, jnp.int32)
        _ctx_2048P = jax.random.normal(jax.random.fold_in(_rk, 11), (16, 16, 256), jnp.float32)
        _ctx_2048c = jax.random.dirichlet(jax.random.fold_in(_rk, 511), 0.3 * jnp.ones((16,), jnp.float32), (16, 128))
        _ctx_2048t = jnp.einsum('bsk,bkd->bsd', _ctx_2048c, _ctx_2048P)
        _ctx_2048t = _ctx_2048t * jax.lax.rsqrt(jnp.mean(jnp.square(_ctx_2048t)) + 1e-12) * 0.953939
        ctx_2048 = 4.13588e-05 + 0.999923 * (_ctx_2048t + 0.3 * jax.random.normal(jax.random.fold_in(_rk, 611), (16, 128, 256), jnp.float32))
        return (x, ctx_2048)
    x, ctx_2048 = _rec_inputs()

    def _L0_attn_setup():
        import jax, jax.numpy as jnp
        import numpy as np
        D_MODEL = 256
        N_HEADS = 16
        HEAD_DIM = 128
        WINDOW = 64
        ROPE_BASE = 10000.0
        B, N = (2, 256)
        INNER = N_HEADS * HEAD_DIM

        def _rotate_half(t):
            t1, t2 = jnp.split(t, 2, axis=-1)
            return jnp.concatenate([-t2, t1], axis=-1)

        def _rope(q, k, offset=0):
            D = q.shape[-1]
            inv_freq = 1.0 / ROPE_BASE ** (jnp.arange(0, D, 2, dtype=jnp.float32) / D)
            pos = jnp.arange(q.shape[2], dtype=jnp.float32) + offset
            ang = pos[:, None] * inv_freq[None, :]
            cos = jnp.concatenate([jnp.cos(ang), jnp.cos(ang)], axis=-1)
            sin = jnp.concatenate([jnp.sin(ang), jnp.sin(ang)], axis=-1)
            q_r = q * cos + _rotate_half(q) * sin
            k_r = k * cos + _rotate_half(k) * sin
            return (q_r, k_r)
        key = jax.random.key(seed)
        k1, k2, k3 = jax.random.split(key, 3)
        x = jax.random.normal(k1, (B, N, D_MODEL), dtype=jnp.float32)
        w_qkv = jax.random.normal(k2, (3 * INNER, D_MODEL), dtype=jnp.float32) / np.sqrt(D_MODEL)
        w_o = jax.random.normal(k3, (D_MODEL, INNER), dtype=jnp.float32) / np.sqrt(INNER)
        return {'x': x, 'w_qkv': w_qkv, 'w_o': w_o}
    _L0_attn_all = _L0_attn_setup()
    _L0_attn_in = {k: v for k, v in _L0_attn_all.items() if k in ('w_qkv', 'w_o')}
    del _L0_attn_all

    def _L0_xattn_setup():
        import jax, jax.numpy as jnp
        import numpy as np
        NUM_FEATURES = 128
        NUM_HEADS = 16
        HEAD_DIM = NUM_FEATURES // NUM_HEADS
        B, SQ, SKV = (4, 256, 256)

        def _split_heads(x):
            b, s, _ = x.shape
            return x.reshape(b, s, NUM_HEADS, HEAD_DIM).transpose(0, 2, 1, 3)
        key = jax.random.key(seed)
        ks = jax.random.split(key, 8)
        w_scale = 1.0 / np.sqrt(NUM_FEATURES)
        return {'query': jax.random.normal(ks[0], (B, NUM_FEATURES, SQ), dtype=jnp.float32), 'key': jax.random.normal(ks[1], (B, NUM_FEATURES, SKV), dtype=jnp.float32), 'value': jax.random.normal(ks[2], (B, NUM_FEATURES, SKV), dtype=jnp.float32), 'Wq': jax.random.normal(ks[3], (NUM_FEATURES, NUM_FEATURES), dtype=jnp.float32) * w_scale, 'bq': jnp.zeros((NUM_FEATURES,), dtype=jnp.float32), 'Wk': jax.random.normal(ks[4], (NUM_FEATURES, NUM_FEATURES), dtype=jnp.float32) * w_scale, 'bk': jnp.zeros((NUM_FEATURES,), dtype=jnp.float32), 'Wv': jax.random.normal(ks[5], (NUM_FEATURES, NUM_FEATURES), dtype=jnp.float32) * w_scale, 'bv': jnp.zeros((NUM_FEATURES,), dtype=jnp.float32), 'Wo': jax.random.normal(ks[6], (NUM_FEATURES, NUM_FEATURES), dtype=jnp.float32) * w_scale, 'bo': jnp.zeros((NUM_FEATURES,), dtype=jnp.float32)}
    _L0_xattn_all = _L0_xattn_setup()
    _L0_xattn_in = {k: v for k, v in _L0_xattn_all.items() if k in ('Wq', 'bq', 'Wk', 'bk', 'Wv', 'bv', 'Wo', 'bo')}
    del _L0_xattn_all

    def _L0_ffn_setup():
        import jax, jax.numpy as jnp
        import numpy as np
        HIDDEN = 256
        NUM_EXPERTS = 8
        TOP_K = 2
        MOE_INTER = 176
        SHARED_INTER = 704

        def _silu_and_mul(gu):
            i = gu.shape[-1] // 2
            return jax.nn.silu(gu[:, :i]) * gu[:, i:]
        key = jax.random.key(seed)
        ks = jax.random.split(key, 7)
        s = 0.02
        return {'hidden_states': jax.random.normal(ks[0], (2, 256, HIDDEN), dtype=jnp.float32), 'gate_w': jax.random.normal(ks[1], (NUM_EXPERTS, HIDDEN), dtype=jnp.float32) * s, 'shared_gate_w': jax.random.normal(ks[2], (1, HIDDEN), dtype=jnp.float32) * s, 'shared_gate_up_w': jax.random.normal(ks[3], (2 * SHARED_INTER, HIDDEN), dtype=jnp.float32) * s, 'shared_down_w': jax.random.normal(ks[4], (HIDDEN, SHARED_INTER), dtype=jnp.float32) * s, 'w13': jax.random.normal(ks[5], (NUM_EXPERTS, 2 * MOE_INTER, HIDDEN), dtype=jnp.float32) * s, 'w2': jax.random.normal(ks[6], (NUM_EXPERTS, HIDDEN, MOE_INTER), dtype=jnp.float32) * s}
    _L0_ffn_all = _L0_ffn_setup()
    _L0_ffn_in = {k: v for k, v in _L0_ffn_all.items() if k in ('gate_w', 'shared_gate_w', 'shared_gate_up_w', 'shared_down_w', 'w13', 'w2')}
    del _L0_ffn_all

    def _L1_attn_setup():
        import jax, jax.numpy as jnp
        import numpy as np
        H = 256
        Q_RANK = 32
        SCALE = float(np.sqrt(Q_RANK))
        key = jax.random.key(seed)
        k_x, k_s, k_a, k_o, k_b = jax.random.split(key, 5)
        B, L = (4, 512)
        x = jax.random.normal(k_x, (B, L, H), dtype=jnp.float32)
        Ws = jax.random.normal(k_s, (H, Q_RANK), dtype=jnp.float32) / np.sqrt(H)
        Wa = jax.random.normal(k_a, (H, Q_RANK), dtype=jnp.float32) / np.sqrt(H)
        Wo = jax.random.normal(k_o, (H, H), dtype=jnp.float32) / np.sqrt(H)
        bo = jax.random.normal(k_b, (H,), dtype=jnp.float32) * 0.01
        return {'x': x, 'Ws': Ws, 'Wa': Wa, 'Wo': Wo, 'bo': bo}
    _L1_attn_all = _L1_attn_setup()
    _L1_attn_in = {k: v for k, v in _L1_attn_all.items() if k in ('Ws', 'Wa', 'Wo', 'bo')}
    del _L1_attn_all

    def _L1_xattn_setup():
        import jax, jax.numpy as jnp
        import numpy as np
        B_DIM, T_DIM, C_DIM = (16, 128, 256)

        def _wkv(w, u, k, v):
            Bn, Tn, Cn = k.shape
            NEG_INF = jnp.float32(-1e+38)

            def step(carry, kv_t):
                p, q, o = carry
                kt, vt = kv_t
                no = jnp.maximum(o, u + kt)
                A = jnp.exp(o - no)
                E = jnp.exp(u + kt - no)
                y = (A * p + E * vt) / (A * q + E)
                no2 = jnp.maximum(w + o, kt)
                A2 = jnp.exp(w + o - no2)
                E2 = jnp.exp(kt - no2)
                return ((A2 * p + E2 * vt, A2 * q + E2, no2), y)
            init = (jnp.zeros((Bn, Cn), k.dtype), jnp.zeros((Bn, Cn), k.dtype), jnp.full((Bn, Cn), NEG_INF, k.dtype))
            kT = jnp.moveaxis(k, 1, 0)
            vT = jnp.moveaxis(v, 1, 0)
            _, yT = jax.lax.scan(step, init, (kT, vT))
            return jnp.moveaxis(yT, 0, 1)
        key = jax.random.key(seed)
        k1, k2, k3, k4 = jax.random.split(key, 4)
        w = -jnp.exp(jax.random.normal(k1, (C_DIM,), jnp.float32))
        u = jax.random.normal(k2, (C_DIM,), jnp.float32)
        k = jax.random.normal(k3, (B_DIM, T_DIM, C_DIM), jnp.float32)
        v = jax.random.normal(k4, (B_DIM, T_DIM, C_DIM), jnp.float32)
        return {'B': B_DIM, 'T': T_DIM, 'C': C_DIM, 'w': w, 'u': u, 'k': k, 'v': v}
    _L1_xattn_all = _L1_xattn_setup()
    _L1_xattn_in = {k: v for k, v in _L1_xattn_all.items() if k in ('w', 'u')}
    del _L1_xattn_all

    def _L1_ffn_setup():
        import jax, jax.numpy as jnp
        import numpy as np
        ALPHA = 1.702
        LIMIT = 7.0
        EPS = 1e-05
        TOP_K = 4
        key = jax.random.key(seed)
        ks = jax.random.split(key, 8)
        B, S, H, I, E = (2, 64, 256, 256, 16)
        return {'x': jax.random.normal(ks[0], (B, S, H), jnp.float32), 'norm_w': jnp.ones((H,), jnp.float32), 'gate_w': jax.random.normal(ks[1], (E, H), jnp.float32) * 0.02, 'gate_b': jax.random.normal(ks[2], (E,), jnp.float32) * 0.02, 'w1': jax.random.normal(ks[3], (E, 2 * I, H), jnp.float32) * 0.02, 'b1': jax.random.normal(ks[4], (E, 2 * I), jnp.float32) * 0.02, 'w2': jax.random.normal(ks[5], (E, H, I), jnp.float32) * 0.02, 'b2': jax.random.normal(ks[6], (E, H), jnp.float32) * 0.02}
    _L1_ffn_all = _L1_ffn_setup()
    _L1_ffn_in = {k: v for k, v in _L1_ffn_all.items() if k in ('norm_w', 'gate_w', 'gate_b', 'w1', 'b1', 'w2', 'b2')}
    del _L1_ffn_all
    return {'x': x, 'ctx_2048': ctx_2048, 'L0_attn_w_qkv': _L0_attn_in['w_qkv'], 'L0_attn_w_o': _L0_attn_in['w_o'], 'L0_xattn_Wq': _L0_xattn_in['Wq'], 'L0_xattn_bq': _L0_xattn_in['bq'], 'L0_xattn_Wk': _L0_xattn_in['Wk'], 'L0_xattn_bk': _L0_xattn_in['bk'], 'L0_xattn_Wv': _L0_xattn_in['Wv'], 'L0_xattn_bv': _L0_xattn_in['bv'], 'L0_xattn_Wo': _L0_xattn_in['Wo'], 'L0_xattn_bo': _L0_xattn_in['bo'], 'L0_ffn_gate_w': _L0_ffn_in['gate_w'], 'L0_ffn_shared_gate_w': _L0_ffn_in['shared_gate_w'], 'L0_ffn_shared_gate_up_w': _L0_ffn_in['shared_gate_up_w'], 'L0_ffn_shared_down_w': _L0_ffn_in['shared_down_w'], 'L0_ffn_w13': _L0_ffn_in['w13'], 'L0_ffn_w2': _L0_ffn_in['w2'], 'L1_attn_Ws': _L1_attn_in['Ws'], 'L1_attn_Wa': _L1_attn_in['Wa'], 'L1_attn_Wo': _L1_attn_in['Wo'], 'L1_attn_bo': _L1_attn_in['bo'], 'L1_xattn_w': _L1_xattn_in['w'], 'L1_xattn_u': _L1_xattn_in['u'], 'L1_ffn_norm_w': _L1_ffn_in['norm_w'], 'L1_ffn_gate_w': _L1_ffn_in['gate_w'], 'L1_ffn_gate_b': _L1_ffn_in['gate_b'], 'L1_ffn_w1': _L1_ffn_in['w1'], 'L1_ffn_b1': _L1_ffn_in['b1'], 'L1_ffn_w2': _L1_ffn_in['w2'], 'L1_ffn_b2': _L1_ffn_in['b2']}

def reference(x, ctx_2048, L0_attn_w_qkv, L0_attn_w_o, L0_xattn_Wq, L0_xattn_bq, L0_xattn_Wk, L0_xattn_bk, L0_xattn_Wv, L0_xattn_bv, L0_xattn_Wo, L0_xattn_bo, L0_ffn_gate_w, L0_ffn_shared_gate_w, L0_ffn_shared_gate_up_w, L0_ffn_shared_down_w, L0_ffn_w13, L0_ffn_w2, L1_attn_Ws, L1_attn_Wa, L1_attn_Wo, L1_attn_bo, L1_xattn_w, L1_xattn_u, L1_ffn_norm_w, L1_ffn_gate_w, L1_ffn_gate_b, L1_ffn_w1, L1_ffn_b1, L1_ffn_w2, L1_ffn_b2):
    import jax
    import jax.numpy as jnp

    def _L0_attn_ref(x, w_qkv, w_o):
        import jax, jax.numpy as jnp
        import numpy as np
        D_MODEL = 256
        N_HEADS = 16
        HEAD_DIM = 128
        WINDOW = 64
        ROPE_BASE = 10000.0
        B, N = (2, 256)
        INNER = N_HEADS * HEAD_DIM

        def _rotate_half(t):
            t1, t2 = jnp.split(t, 2, axis=-1)
            return jnp.concatenate([-t2, t1], axis=-1)

        def _rope(q, k, offset=0):
            D = q.shape[-1]
            inv_freq = 1.0 / ROPE_BASE ** (jnp.arange(0, D, 2, dtype=jnp.float32) / D)
            pos = jnp.arange(q.shape[2], dtype=jnp.float32) + offset
            ang = pos[:, None] * inv_freq[None, :]
            cos = jnp.concatenate([jnp.cos(ang), jnp.cos(ang)], axis=-1)
            sin = jnp.concatenate([jnp.sin(ang), jnp.sin(ang)], axis=-1)
            q_r = q * cos + _rotate_half(q) * sin
            k_r = k * cos + _rotate_half(k) * sin
            return (q_r, k_r)
        Bq, Nq, _ = x.shape
        qkv = jnp.einsum('bnd,ed->bne', x, w_qkv)
        q, k, v = jnp.split(qkv, 3, axis=-1)

        def to_heads(t):
            return t.reshape(Bq, Nq, N_HEADS, HEAD_DIM).transpose(0, 2, 1, 3)
        q, k, v = (to_heads(q), to_heads(k), to_heads(v))
        q, k = _rope(q, k, offset=0)
        i = jnp.arange(Nq)[:, None]
        j = jnp.arange(Nq)[None, :]
        valid = (j > i - WINDOW) & (j <= i)
        scale = 1.0 / np.sqrt(HEAD_DIM)
        scores = jnp.einsum('bhnd,bhkd->bhnk', q, k) * scale
        scores = jnp.where(valid[None, None], scores, -jnp.inf)
        att = jax.nn.softmax(scores, axis=-1)
        out = jnp.einsum('bhnk,bhkd->bhnd', att, v)
        out = out.transpose(0, 2, 1, 3).reshape(Bq, Nq, INNER)
        y = jnp.einsum('bni,di->bnd', out, w_o)
        return y

    def _L0_xattn_ref(query, key, value, Wq, bq, Wk, bk, Wv, bv, Wo, bo):
        import jax, jax.numpy as jnp
        import numpy as np
        NUM_FEATURES = 128
        NUM_HEADS = 16
        HEAD_DIM = NUM_FEATURES // NUM_HEADS
        B, SQ, SKV = (4, 256, 256)

        def _split_heads(x):
            b, s, _ = x.shape
            return x.reshape(b, s, NUM_HEADS, HEAD_DIM).transpose(0, 2, 1, 3)
        q_in = query.transpose(0, 2, 1)
        k_in = key.transpose(0, 2, 1)
        v_in = value.transpose(0, 2, 1)
        q = _split_heads(jnp.einsum('bsf,of->bso', q_in, Wq) + bq)
        k = _split_heads(jnp.einsum('bsf,of->bso', k_in, Wk) + bk)
        v = _split_heads(jnp.einsum('bsf,of->bso', v_in, Wv) + bv)
        scale = 1.0 / jnp.sqrt(jnp.float32(NUM_FEATURES))
        scores = jnp.einsum('bhqd,bhkd->bhqk', q, k) * scale
        attn = jax.nn.softmax(scores, axis=-1)
        out = jnp.einsum('bhqk,bhkd->bhqd', attn, v)
        b = out.shape[0]
        out = out.transpose(0, 2, 1, 3).reshape(b, -1, NUM_FEATURES)
        out = jnp.einsum('bsf,of->bso', out, Wo) + bo
        return out.transpose(0, 2, 1)

    def _L0_ffn_ref(hidden_states, gate_w, shared_gate_w, shared_gate_up_w, shared_down_w, w13, w2):
        import jax, jax.numpy as jnp
        import numpy as np
        HIDDEN = 256
        NUM_EXPERTS = 8
        TOP_K = 2
        MOE_INTER = 176
        SHARED_INTER = 704

        def _silu_and_mul(gu):
            i = gu.shape[-1] // 2
            return jax.nn.silu(gu[:, :i]) * gu[:, i:]
        orig_shape = hidden_states.shape
        x = hidden_states.reshape(-1, orig_shape[-1])
        shared = _silu_and_mul(x @ shared_gate_up_w.T) @ shared_down_w.T
        shared = shared * jax.nn.sigmoid(x @ shared_gate_w.T)
        router_logits = x @ gate_w.T
        probs = jax.nn.softmax(router_logits.astype(jnp.float32), axis=-1)
        routing_weights, selected_experts = jax.lax.top_k(probs, TOP_K)
        combined = jnp.zeros(x.shape, dtype=jnp.float32)
        E = w13.shape[0]
        for e in range(E):
            w_e = jnp.where(selected_experts == e, routing_weights, 0.0).sum(-1)
            h = _silu_and_mul(x @ w13[e].T) @ w2[e].T
            combined = combined + w_e[:, None] * h.astype(jnp.float32)
        out = shared + combined.astype(x.dtype)
        return out.reshape(orig_shape)

    def _L1_attn_ref(x, Ws, Wa, Wo, bo):
        import jax, jax.numpy as jnp
        import numpy as np
        H = 256
        Q_RANK = 32
        SCALE = float(np.sqrt(Q_RANK))
        B, L, _ = x.shape
        state = jnp.einsum('blh,hr->blr', x, Ws)
        action = jnp.einsum('blh,hr->blr', x, Wa)
        q_values = jnp.einsum('bir,bjr->bij', state, action) / SCALE
        causal = jnp.tril(jnp.ones((L, L), dtype=bool))
        q_values = jnp.where(causal, q_values, -jnp.inf)
        weights = jax.nn.softmax(q_values, axis=-1)
        out = jnp.einsum('bij,bjh->bih', weights, x)
        return jnp.einsum('bih,ho->bio', out, Wo.T) + bo

    def _L1_xattn_ref(B, T, C, w, u, k, v):
        import jax, jax.numpy as jnp
        import numpy as np
        B_DIM, T_DIM, C_DIM = (16, 128, 256)

        def _wkv(w, u, k, v):
            Bn, Tn, Cn = k.shape
            NEG_INF = jnp.float32(-1e+38)

            def step(carry, kv_t):
                p, q, o = carry
                kt, vt = kv_t
                no = jnp.maximum(o, u + kt)
                A = jnp.exp(o - no)
                E = jnp.exp(u + kt - no)
                y = (A * p + E * vt) / (A * q + E)
                no2 = jnp.maximum(w + o, kt)
                A2 = jnp.exp(w + o - no2)
                E2 = jnp.exp(kt - no2)
                return ((A2 * p + E2 * vt, A2 * q + E2, no2), y)
            init = (jnp.zeros((Bn, Cn), k.dtype), jnp.zeros((Bn, Cn), k.dtype), jnp.full((Bn, Cn), NEG_INF, k.dtype))
            kT = jnp.moveaxis(k, 1, 0)
            vT = jnp.moveaxis(v, 1, 0)
            _, yT = jax.lax.scan(step, init, (kT, vT))
            return jnp.moveaxis(yT, 0, 1)
        return _wkv(w, u, k, v)

    def _L1_ffn_ref(x, norm_w, gate_w, gate_b, w1, b1, w2, b2):
        import jax, jax.numpy as jnp
        import numpy as np
        ALPHA = 1.702
        LIMIT = 7.0
        EPS = 1e-05
        TOP_K = 4
        B, S, H = x.shape
        M = B * S
        E = gate_w.shape[0]
        xf = x.reshape(M, H)
        t = xf * jax.lax.rsqrt(jnp.mean(xf * xf, axis=-1, keepdims=True) + EPS) * norm_w
        logits = t @ gate_w.T + gate_b
        vals, idx = jax.lax.top_k(logits, TOP_K)
        gates_k = jax.nn.softmax(vals, axis=-1)
        G = jnp.zeros((M, E), x.dtype).at[jnp.arange(M)[:, None], idx].set(gates_k)
        h = jnp.einsum('mh,eoh->emo', t, w1) + b1[:, None, :]
        a = jnp.minimum(h[..., ::2], LIMIT)
        b = jnp.clip(h[..., 1::2], -LIMIT, LIMIT)
        act = a * jax.nn.sigmoid(ALPHA * a) * (b + 1.0)
        y = jnp.einsum('emi,edi->emd', act, w2) + b2[:, None, :]
        delta = jnp.einsum('me,emd->md', G, y)
        return x + delta.reshape(B, S, H)
    x = _layernorm(x + _L0_attn_ref(x, L0_attn_w_qkv, L0_attn_w_o), axis=-1)
    x = _layernorm(x + _L0_xattn_ref(x, ctx_2048, ctx_2048, L0_xattn_Wq, L0_xattn_bq, L0_xattn_Wk, L0_xattn_bk, L0_xattn_Wv, L0_xattn_bv, L0_xattn_Wo, L0_xattn_bo), axis=-1)
    x = _layernorm(x + _L0_ffn_ref(x, L0_ffn_gate_w, L0_ffn_shared_gate_w, L0_ffn_shared_gate_up_w, L0_ffn_shared_down_w, L0_ffn_w13, L0_ffn_w2), axis=-1)
    x = _layernorm(x + _L1_attn_ref(x, L1_attn_Ws, L1_attn_Wa, L1_attn_Wo, L1_attn_bo), axis=-1)
    x = _layernorm(x + _L1_xattn_ref(16, 128, 256, L1_xattn_w, L1_xattn_u, x, ctx_2048), axis=-1)
    x = _layernorm(x + _L1_ffn_ref(x, L1_ffn_norm_w, L1_ffn_gate_w, L1_ffn_gate_b, L1_ffn_w1, L1_ffn_b1, L1_ffn_w2, L1_ffn_b2), axis=-1)
    return x

_drawn_inputs = setup_inputs


def setup_inputs(seed=0):
    import zlib

    import numpy as np

    out = dict(_drawn_inputs(seed))
    spreads = {'L0_xattn_bq': (0.0, 0.8),
     'L0_xattn_bk': (0.0, 0.8),
     'L0_xattn_bv': (0.0, 0.8),
     'L0_xattn_bo': (0.0, 0.8),
     'L1_ffn_norm_w': (1.0, 0.6)}
    factors = {'L0_ffn_gate_w': 8.0,
     'L0_ffn_shared_gate_w': 8.0,
     'L0_ffn_shared_gate_up_w': 4.575,
     'L0_ffn_shared_down_w': 4.587,
     'L0_ffn_w13': 8.0,
     'L0_ffn_w2': 8.0,
     'L1_attn_bo': 7.556,
     'L1_ffn_gate_w': 3.979,
     'L1_ffn_gate_b': 8.0,
     'L1_ffn_w1': 3.672,
     'L1_ffn_b1': 8.0,
     'L1_ffn_w2': 3.577,
     'L1_ffn_b2': 8.0}
    for name, (base, spread) in spreads.items():
        noise = np.random.default_rng([zlib.crc32(name.encode()), seed]).standard_normal(out[name].shape)
        drawn = base * np.exp(spread * noise) if base else spread * noise
        out[name] = jnp.asarray(drawn.astype(out[name].dtype))
    for name, factor in factors.items():
        out[name] = (out[name] * factor).astype(out[name].dtype)
    return out
```

```python
from contextlib import ExitStack

import concourse.bass as bass
import numpy as np
from concourse import mybir

F32 = mybir.dt.float32
BF16 = mybir.dt.bfloat16
ALU = mybir.AluOpType
ACT = mybir.ActivationFunctionType
AX = mybir.AxisListType

P = 128
B = 16
D = 256
KC = D // P
H = 16
HD = 128
G = 4
HG = H // G
GW = HG * HD
WINDOW = 64
NEG = -3.0e38
EPS = 1e-5


def reached(eng, sem, count):
    if not isinstance(count, int) or count > 0:
        eng.wait_ge(sem, count)


class Room:

    def __init__(self, nc, stack, prefix, banks):
        self.nc, self.stack, self.prefix, self.banks = nc, stack, prefix, list(banks)
        self.taken = []

    def sb(self, name, shape, dt=F32):
        return self.stack.enter_context(self.nc.sbuf_tensor(f"{self.prefix}_{name}", shape, dt))

    def ps(self, shape):
        bank = self.banks.pop(0)[:]
        return bank if len(shape) == 2 else bank.rearrange("p (a b) -> p a b", a=shape[1])

    def sem(self, name):
        self.taken.append(self.nc.alloc_semaphore(name=f"{self.prefix}_{name}"))
        return self.taken[-1]

    def sems(self, names):
        return [self.sem(n) for n in names.split()]

    def close(self):
        with self.nc.Block() as block:

            @block.gpsimd
            def _(pool):
                self.nc.clear_and_free_semaphores(self.taken)


class RowNorm:

    def __init__(self, nc, room, X, eps):
        self.nc, self.X, self.eps, self.in_loop = nc, X, eps, True
        self.row = room.sb("row", [P, D])
        self.moments = room.sb("moments", [P, 6])
        self.all_moments = room.sb("all_moments", [P, B, 6])
        self.stats = room.sb("stats", [P, B, 2])
        self.root = room.sb("root", [P, B])
        self.rstd = room.sb("rstd", [P, B])
        self.row_ready, self.kept, self.bn_ready, self.moments_ready = room.sems(
            "row_ready row_kept bn_ready moments_ready")
        self.stats_ready, self.root_ready, self.rstd_ready, self.normed = room.sems(
            "stats_ready root_ready rstd_ready normed")

    def put(self, dve, b):
        nc = self.nc
        dve.wait_ge(self.row_ready, b + 1)
        nc.vector.tensor_scalar(self.X[:, bass.ds(b * D, D)], self.row[:], 0.0, None,
                                ALU.add).then_inc(self.kept, 1)
        nc.vector.bn_stats(self.moments[:], self.row[:]).then_inc(self.bn_ready, 1)
        dve.wait_ge(self.bn_ready, b + 1)
        nc.vector.tensor_scalar(self.all_moments[:, bass.ds(b, 1), :].rearrange("p b s -> p (b s)"),
                                self.moments[:], 0.0, None, ALU.add).then_inc(self.moments_ready, 1)

    def all_rows(self, dve, added, count):
        dve.wait_ge(added, count)
        for b in range(B):
            m = self.nc.vector.bn_stats(self.all_moments[:, b], self.X[:, b * D:(b + 1) * D])
            m.then_inc(self.moments_ready, 1)
        self.in_loop = False

    def scalar_part(self, act):
        act.wait_ge(self.stats_ready, B)
        self.nc.scalar.activation(self.root[:], self.stats[:, :, 1], ACT.Sqrt,
                                  bias=self.eps[:]).then_inc(self.root_ready, 1)

    def vector_part(self, dve):
        nc = self.nc
        dve.wait_ge(self.moments_ready, B)
        for b in range(B):
            nc.vector.bn_aggr(self.stats[:, b], self.all_moments[:, b]).then_inc(self.stats_ready, 1)
        dve.wait_ge(self.root_ready, 1)
        nc.vector.reciprocal(self.rstd[:], self.root[:]).then_inc(self.rstd_ready, 1)
        dve.wait_ge(self.rstd_ready, 1)
        if self.in_loop:
            dve.wait_ge(self.kept, B)
        for b in range(B):
            row = self.X[:, b * D:(b + 1) * D]
            nc.vector.tensor_scalar(row, row, self.stats[:, b, 0:1], self.rstd[:, b:b + 1],
                                    ALU.subtract, ALU.mult).then_inc(self.normed, 1)


def self_attention(nc, room, A, X, ident, eps):
    wqkv = room.sb("wqkv", [P, KC, G, 3, GW])
    wo = room.sb("wo", [P, H, D])
    cos = room.sb("cos", [P, HD])
    sin = room.sb("sin", [P, HD])
    mask = room.sb("mask", [P, P])
    xin = room.sb("xin", [P, D])
    xT = room.sb("xT", [P, KC, P])
    t1 = room.sb("t1", [P, 2, GW])
    t2 = room.sb("t2", [P, 2, GW])
    qk = room.sb("qk", [P, 2, GW])
    qkT = room.sb("qkT", [P, 2, GW])
    v = room.sb("v", [P, G, GW])
    s = room.sb("s", [P, HG, P])
    p = room.sb("p", [P, HG, P])
    negmax = room.sb("negmax", [P, HG])
    total = room.sb("total", [P, HG])
    inverse = room.sb("inverse", [P, HG])
    pT = room.sb("pT", [P, HG, P])
    oT = room.sb("oT", [P, HG, P])
    norm = RowNorm(nc, room, X, eps)
    qkv_ps = [room.ps([P, GW]) for n in ("q_ps", "k_ps", "v_ps")]
    turn_ps = room.ps([P, GW])
    y_ps = room.ps([P, GW])
    s_ps = room.ps([P, HG, P])
    pT_ps = room.ps([P, HG, P])
    o_ps = room.ps([P, HG, P])

    x_loaded, table_loaded, wo_loaded = room.sems("x_loaded table_loaded wo_loaded")
    w_loaded = [room.sem(f"w_loaded{g}") for g in range(G)]
    xin_ready, xT_done, xT_copied = room.sems("xin_ready xT_done xT_copied")
    made = room.sems("q_made k_made v_made")
    taken = room.sems("q_taken k_taken v_taken")
    rotated = room.sems("q_rotated k_rotated")
    turned = room.sems("q_turned k_turned")
    copied = room.sems("qT_copied kT_copied")
    s_made, s_taken, s_max, max_ready, e_ready = room.sems("s_made s_taken s_max max_ready e_ready")
    inv_ready, p_ready, pT_made, pT_copied = room.sems("inv_ready p_ready pT_made pT_copied")
    o_made, oT_copied, wo_done = room.sems("o_made oT_copied wo_done")
    SCALE = float(1.0 / np.sqrt(HD))
    U = B * G

    def sequences(eng, unit, tail):
        for g in range(G):
            unit(0, g)
        with eng.Fori(1, B - 1) as b:
            for g in range(G):
                unit(b, g)
        for n in range(G + tail):
            unit(B - 1 + n // G, n % G)

    def live(b, g, back=0):
        return not isinstance(b, int) or 0 <= b * G + g - back < B * G

    def has_next(b):
        return not isinstance(b, int) or b + 1 < B

    with nc.Block() as block:

        @block.sync
        def _(sp):
            sp.dma_start(X[:, 0:D], A["x"][:, 0, :]).then_inc(x_loaded, 16)
            for g in range(G):
                for c in range(KC):
                    sp.dma_start(wqkv[:, c, g], A["wqkv"][:, c, g]).then_inc(w_loaded[g], 16)
            sp.dma_start(wo[:], A["wo"]).then_inc(wo_loaded, 16)

        @block.gpsimd
        def _(pool):
            def unit(b, g):
                u = b * G + g
                for i in range(2):
                    pool.wait_ge(taken[i], u + 1)
                    reached(pool, turned[i], u)
                    nc.gpsimd.tensor_tensor(qk[:, i], t1[:, i], t2[:, i],
                                            ALU.add).then_inc(rotated[i], 1)
                if g == 0 and has_next(b):
                    pool.wait_ge(xT_done, b + 1)
                    nc.gpsimd.tensor_copy(xin[:], X[:, bass.ds((b + 1) * D, D)]).then_inc(xin_ready, 1)

            pool.wait_ge(x_loaded, 16)
            nc.gpsimd.tensor_copy(xin[:], X[:, 0:D]).then_inc(xin_ready, 1)
            pool.wait_ge(table_loaded, 64)
            sequences(pool, unit, 0)

        @block.scalar
        def _(act):
            act.dma_start(cos[:], A["cos"]).then_inc(table_loaded, 16)
            act.dma_start(sin[:], A["sin"]).then_inc(table_loaded, 16)
            act.dma_start(mask[:], A["mask"]).then_inc(table_loaded, 16)
            act.dma_start(X[:, D:B * D].rearrange("p (b d) -> p b d", b=B - 1),
                          A["x"][:, 1:B, :]).then_inc(table_loaded, 16)

            def copy_xT(b):
                act.wait_ge(xT_done, b + 1)
                nc.scalar.copy(xT[:].rearrange("p c t -> p (c t)"), turn_ps[:, 0:D]).then_inc(xT_copied, 1)

            def unit(b, g):
                u = b * G + g
                if live(b, g, 1):
                    for i in range(2):
                        act.wait_ge(turned[i], u)
                        reached(act, s_made, u - 1)
                        nc.scalar.copy(qkT[:, i], turn_ps[:]).then_inc(copied[i], 1)
                if live(b, g, 2):
                    act.wait_ge(pT_made, u - 1)
                    reached(act, o_made, u - 2)
                    nc.scalar.copy(pT[:], pT_ps[:]).then_inc(pT_copied, 1)
                if live(b, g):
                    act.wait_ge(made[2], u + 1)
                    reached(act, o_made, u - 3)
                    nc.scalar.copy(v[:, g], qkv_ps[2][:]).then_inc(taken[2], 1)
                    if g == G - 1 and has_next(b):
                        copy_xT(b + 1)
                if live(b, g, 1):
                    act.wait_ge(max_ready, u)
                    reached(act, pT_made, u - 1)
                    for h in range(HG):
                        e = nc.scalar.activation(p[:, h], s[:, h], ACT.Exp, bias=negmax[:, h:h + 1],
                                                 accum_out=total[:, h:h + 1])
                    e.then_inc(e_ready, 1)
                if live(b, g, 2):
                    act.wait_ge(o_made, u - 1)
                    reached(act, wo_done, u - 2)
                    nc.scalar.copy(oT[:], o_ps[:]).then_inc(oT_copied, 1)

            copy_xT(0)
            sequences(act, unit, 2)
            norm.scalar_part(act)

        @block.tensor
        def _(pe):
            def turn(i, b, g):
                u = b * G + g
                pe.wait_ge(rotated[i], u)
                if i == 0:
                    reached(pe, copied[1], u - 1)
                    if g == 0 and has_next(b - 1 if isinstance(b, int) else b):
                        pe.wait_ge(xT_copied, b + 1)
                else:
                    pe.wait_ge(copied[0], u)
                for h in range(HG):
                    m = nc.tensor.transpose(turn_ps[:, h * HD:(h + 1) * HD],
                                            qk[:, i, h * HD:(h + 1) * HD], ident[:])
                m.then_inc(turned[i], 1)

            def project(i, b, g):
                u = b * G + g
                reached(pe, taken[i], u)
                if i == 0:
                    if g == 0:
                        pe.wait_ge(xT_copied, b + 1)
                    if isinstance(b, int) and b == 0:
                        pe.wait_ge(w_loaded[g], 16 * KC)
                for c in range(KC):
                    m = nc.tensor.matmul(qkv_ps[i][:], xT[:, c], wqkv[:, c, g, i],
                                         start=(c == 0), stop=(c == KC - 1))
                m.then_inc(made[i], 1)

            def turn_x(b):
                pe.wait_ge(xin_ready, b + 1)
                for c in range(KC):
                    m = nc.tensor.transpose(turn_ps[:, c * P:(c + 1) * P], xin[:, c * P:(c + 1) * P], ident[:])
                m.then_inc(xT_done, 1)

            def project_heads(b, g):
                u, gh = b * G + g, (g - 3) % G
                pe.wait_ge(oT_copied, u - 2)
                if isinstance(b, int) and u == 3:
                    pe.wait_ge(wo_loaded, 16)
                if gh == 0:
                    reached(pe, norm.row_ready, (b if g == 3 else b - 1))
                for h in range(HG):
                    m = nc.tensor.matmul(y_ps[:, 0:D], oT[:, h], wo[:, gh * HG + h],
                                         start=(gh == 0 and h == 0), stop=(gh == G - 1 and h == HG - 1))
                m.then_inc(wo_done, 1)

            def unit(b, g):
                u = b * G + g
                if live(b, g, 1):
                    turn(0, b, g)
                if live(b, g):
                    project(0, b, g)
                if live(b, g, 3):
                    project_heads(b, g)
                if live(b, g, 1):
                    turn(1, b, g)
                if live(b, g):
                    project(1, b, g)
                if live(b, g, 2):
                    pe.wait_ge(p_ready, u - 1)
                    reached(pe, pT_copied, u - 2)
                    for h in range(HG):
                        m = nc.tensor.transpose(pT_ps[:, h], p[:, h], ident[:])
                    m.then_inc(pT_made, 1)
                if live(b, g):
                    project(2, b, g)
                    if g == G - 1 and has_next(b):
                        pe.wait_ge(copied[1], u)
                        turn_x(b + 1)
                if live(b, g, 1):
                    pe.wait_ge(copied[1], u)
                    reached(pe, s_taken, u - 1)
                    for h in range(HG):
                        m = nc.tensor.matmul(s_ps[:, h], qkT[:, 0, h * HD:(h + 1) * HD],
                                             qkT[:, 1, h * HD:(h + 1) * HD], start=True, stop=True)
                    m.then_inc(s_made, 1)
                if live(b, g, 2):
                    pe.wait_ge(pT_copied, u - 1)
                    reached(pe, oT_copied, u - 2)
                    for h in range(HG):
                        m = nc.tensor.matmul(o_ps[:, h], v[:, (g - 2) % G, h * HD:(h + 1) * HD],
                                             pT[:, h], start=True, stop=True)
                    m.then_inc(o_made, 1)

            turn_x(0)
            sequences(pe, unit, 3)

        @block.vector
        def _(dve):
            half = HD // 2

            def rotate(i, b, g):
                u = b * G + g
                src = qkv_ps[i][:].rearrange("p (h e) -> p h e", h=HG)
                a = t1[:, i].rearrange("p (h e) -> p h e", h=HG)
                c = t2[:, i].rearrange("p (h e) -> p h e", h=HG)
                dve.wait_ge(made[i], u + 1)
                reached(dve, rotated[i], u)
                nc.vector.tensor_tensor(a, src, cos[:, None, :].to_broadcast([P, HG, HD]), ALU.mult)
                nc.vector.tensor_tensor(c[:, :, 0:half], src[:, :, half:HD],
                                        sin[:, None, 0:half].to_broadcast([P, HG, half]), ALU.mult)
                nc.vector.tensor_tensor(c[:, :, half:HD], src[:, :, 0:half],
                                        sin[:, None, half:HD].to_broadcast([P, HG, half]),
                                        ALU.mult).then_inc(taken[i], 1)

            def unit(b, g):
                u = b * G + g
                if live(b, g, 2):
                    dve.wait_ge(e_ready, u - 1)
                    nc.vector.reciprocal(inverse[:], total[:]).then_inc(inv_ready, 1)
                    dve.wait_ge(inv_ready, u - 1)
                    nc.vector.tensor_tensor(p[:], p[:], inverse[:, :, None].to_broadcast([P, HG, P]),
                                            ALU.mult).then_inc(p_ready, 1)
                if live(b, g):
                    rotate(0, b, g)
                    rotate(1, b, g)
                if g == 2 and live(b, g, 6):
                    dve.wait_ge(wo_done, b * G)
                    nc.vector.tensor_tensor(norm.row[:], X[:, bass.ds((b - 1) * D, D)], y_ps[:, 0:D],
                                            ALU.add).then_inc(norm.row_ready, 1)
                    norm.put(dve, b - 1)
                if live(b, g, 1):
                    dve.wait_ge(s_made, u)
                    reached(dve, e_ready, u - 1)
                    nc.vector.scalar_tensor_tensor(s[:], s_ps[:], SCALE,
                                                   mask[:, None, :].to_broadcast([P, HG, P]),
                                                   ALU.mult, ALU.add).then_inc(s_taken, 1)
                    dve.wait_ge(s_taken, u)
                    nc.vector.tensor_reduce(negmax[:], s[:], AX.X, ALU.max, negate=True).then_inc(max_ready, 1)

            dve.wait_ge(table_loaded, 64)
            sequences(dve, unit, 3)
            norm.vector_part(dve)


def cross_attention(nc, room, A, X, ident, eps):
    FD = 8
    RUNS = ((0, 3, 0), (3, 2, 1), (5, 1, 2))
    SHIFT = FD * 6
    NPAR = 2
    VW = 32
    SCALE = float(1.0 / np.sqrt(P))
    N_STACK = 2 * len(RUNS)
    NR = 1 + 3 * 3
    R = 3
    spread = nc.dram_tensor("spread", [R, 6, P, D], BF16, kind="Internal").ap()

    w = room.sb("w", [P, 4, P])
    bias = room.sb("bias", [P, 4])
    bq = room.sb("bq", [P, 1])
    ctx = [room.sb(f"ctx{j}", [P, D]) for j in range(R)]
    full = room.sb("full", [P, 2, D])
    rest = room.sb("rest", [P, 2, D])
    part = room.sb("part", [P, 3, 2, D], BF16)
    QS = [room.sb(f"QS{j}", [P, H, D], BF16) for j in range(R)]
    KS = [room.sb(f"KS{j}", [P, H, D], BF16) for j in range(R)]
    zero = room.sb("zero", [NPAR, H * D], BF16)
    V = [room.sb(f"V{j}", [P, KC, H, VW]) for j in range(R)]
    negmax = room.sb("negmax", [P, KC, H])
    high = room.sb("high", [P, KC, H], BF16)
    pair = room.sb("pair", [P, KC, NPAR, H])
    shift = room.sb("shift", [NPAR * H, D], BF16)
    pr = [room.sb(f"pr{j}", [P, KC, D]) for j in range(2)]
    oT = room.sb("oT", [P, 4, D])
    inverse = room.sb("inverse", [P, KC, H])
    o = room.sb("o", [P, KC, H, FD])
    onT = room.sb("onT", [P, D])
    norm = RowNorm(nc, room, X, eps)
    a_ps = room.ps([P, KC, D])
    b_ps = room.ps([P, KC, D])
    m_ps = [room.ps([P, KC, D]) for j in range(2)]
    s_ps = [room.ps([P, KC, D]) for j in range(2)]
    o_ps = [room.ps([P, KC, D]) for j in range(2)]

    w_loaded, ready, ctx_loaded, parts_out, zeroed, stacked, shifted = room.sems(
        "w_loaded ready ctx_loaded parts_out zeroed stacked shifted")
    qk_made, qk_taken, v_made, v_ready = room.sems("qk_made qk_taken v_made v_ready")
    bq_ready, part0, part1, part2, rest0 = room.sems("bq_ready part0 part1 part2 rest0")
    m_made, max_ready = room.sems("m_made max_ready")
    high_ready, pair_ready, pair_turned, shift_ready = room.sems("high_ready pair_ready pair_turned shift_ready")
    s_made, p_ready, pv_done = room.sems("s_made p_ready pv_done")
    oT_copied, nat_made, inv_ready, o_ready = room.sems("oT_copied nat_made inv_ready o_ready")
    onT_made, onT_copied, y_made = room.sems("onT_made onT_copied y_made")

    def rounds(eng, work):
        for r in range(R):
            work(r, r)
        with eng.Fori(R, B - R, R) as r:
            for j in range(R):
                work(r + j, j)
        for r in range(B - 1, B + 2):
            work(r, r % R)

    def exists(b):
        return not isinstance(b, int) or 0 <= b < B

    with nc.Block() as block:

        @block.sync
        def _(sp):
            def load(b, j):
                sp.dma_start(ctx[j][:], A["ctx"][:, bass.ds(b * D, D)]).then_inc(ctx_loaded, 16)

            def stack(b, j):
                sp.wait_ge(part2, b + 1)
                sp.dma_start(spread[j].rearrange("n p s -> p n s"),
                             part[:].rearrange("p k i s -> p (k i) s")).then_inc(parts_out, 16)
                reached(sp, s_made, (b - 2) * H)
                sp.dma_start(QS[j][SHIFT:SHIFT + NPAR].rearrange("n h s -> n (h s)"), zero[:]).then_inc(zeroed, 16)
                sp.wait_ge(parts_out, 16 * (b + 1))
                src = spread[j].rearrange("(k i) (d h) s -> k i d (h s)", i=2, d=FD)
                for n, m, k in RUNS:
                    rows = slice(n * FD, (n + m) * FD)
                    sp.dma_start(KS[j][rows].rearrange("r h s -> r (h s)"), src[0:m, 1]).then_inc(stacked, 16)
                    sp.dma_start(QS[j][rows].rearrange("r h s -> r (h s)"),
                                 src[k:k + 1, 0].to_broadcast([m, FD, H * D])).then_inc(stacked, 16)

            def work(r, j):
                if exists(r + 1):
                    reached(sp, v_made, r - 1)
                    sp.wait_ge(w_loaded, 32)
                    load(r + 1, (j + 1) % R)
                    stack(r + 1, (j + 1) % R)
                if exists(r):
                    sp.wait_ge(shift_ready, r + 1)
                    for n in range(NPAR):
                        sp.dma_start(QS[j][SHIFT + n:SHIFT + n + 1],
                                     shift[n * H:(n + 1) * H]).then_inc(shifted, 16)

            sp.dma_start(w[:], A["xw"]).then_inc(w_loaded, 16)
            sp.dma_start(bias[:], A["xbias"]).then_inc(w_loaded, 16)
            load(0, 0)
            sp.wait_ge(ready, NR + 1)
            stack(0, 0)
            rounds(sp, work)

        @block.gpsimd
        def _(pool):
            nc.gpsimd.memset(zero[:], 0.0).then_inc(ready, 1)
            for j in range(R):
                nc.gpsimd.memset(V[j][:, :, :, FD:VW], 0.0).then_inc(ready, 1)
                nc.gpsimd.memset(QS[j][:], 0.0).then_inc(ready, 1)
                nc.gpsimd.memset(KS[j][:], 0.0).then_inc(ready, 1)

            def split(b):
                pool.wait_ge(part0, b + 1)
                nc.gpsimd.tensor_tensor(rest[:], full[:], part[:, 0], ALU.subtract).then_inc(rest0, 1)
                pool.wait_ge(part1, b + 1)
                nc.gpsimd.tensor_tensor(part[:, 2], rest[:], part[:, 1], ALU.subtract).then_inc(part2, 1)

            def work(r, j):
                if exists(r + 1):
                    split(r + 1)

            split(0)
            rounds(pool, work)

        @block.scalar
        def _(act):
            def take_qk(b):
                act.wait_ge(qk_made, b + 1)
                reached(act, part2, b)
                nc.scalar.activation(full[:, 0], a_ps[:, 0], ACT.Identity, bias=bq[:], scale=SCALE)
                nc.scalar.activation(full[:, 1], a_ps[:, 1], ACT.Identity,
                                     bias=bias[:, 1:2]).then_inc(qk_taken, 1)
                act.wait_ge(qk_taken, b + 1)
                reached(act, parts_out, b * 16)
                nc.scalar.copy(part[:, 0], full[:]).then_inc(part0, 1)

            def second_part(b):
                act.wait_ge(rest0, b + 1)
                nc.scalar.copy(part[:, 1], rest[:]).then_inc(part1, 1)

            def work(r, j):
                if exists(r - 2):
                    act.wait_ge(pv_done, H * (r - 1))
                    nc.scalar.copy(oT[:, 2:4], o_ps[1][:]).then_inc(oT_copied, 1)
                for h in range(H):
                    if exists(r - 1):
                        act.wait_ge(s_made, (r - 1) * H + h + 1)
                        reached(act, pv_done, (r - 1) * H + h - 1)
                        nc.scalar.activation(pr[h % 2][:], s_ps[h % 2][:], ACT.Exp).then_inc(p_ready, 1)
                    if h == 4 and exists(r - 2):
                        act.wait_ge(onT_made, r - 1)
                        nc.scalar.activation(onT[:], a_ps[:, 0], ACT.Identity,
                                             bias=bias[:, 2:3]).then_inc(onT_copied, 1)
                    if h == 9 and exists(r - 1):
                        act.wait_ge(pv_done, H * (r - 1) + H // 2)
                        nc.scalar.copy(oT[:, 0:2], o_ps[0][:]).then_inc(oT_copied, 1)
                    if h == 7 and exists(r + 1):
                        take_qk(r + 1)
                    if h == 9 and exists(r + 1):
                        second_part(r + 1)
                    if h == 11 and exists(r):
                        act.wait_ge(v_made, r + 1)
                        nc.scalar.copy(V[j][:, :, :, 0:FD],
                                       b_ps[:].rearrange("p c (o e) -> p c o e", o=2)[:, :, 0].rearrange(
                                           "p c (h e) -> p c h e", h=H)).then_inc(v_ready, 1)
                    if h == 13 and exists(r):
                        act.wait_ge(pair_turned, r + 1)
                        reached(act, shifted, 32 * r)
                        nc.scalar.copy(shift[:], a_ps[0:NPAR * H, 1]).then_inc(shift_ready, 1)

            act.wait_ge(w_loaded, 32)
            nc.scalar.mul(bq[:], bias[:, 0:1], SCALE).then_inc(bq_ready, 1)
            act.wait_ge(bq_ready, 1)
            take_qk(0)
            second_part(0)
            rounds(act, work)
            norm.scalar_part(act)

        @block.tensor
        def _(pe):
            def project_qk(b, j):
                pe.wait_ge(ctx_loaded, 16 * (b + 1))
                if isinstance(b, int) and b == 0:
                    pe.wait_ge(w_loaded, 32)
                nc.tensor.matmul(a_ps[:, 0], w[:, 0], X[:, bass.ds(b * D, D)], start=True, stop=True)
                nc.tensor.matmul(a_ps[:, 1], w[:, 1], ctx[j][:], start=True, stop=True).then_inc(qk_made, 1)

            def work(r, j):
                i = (j - 1) % R
                for h in range(H):
                    if exists(r - 1):
                        if h == 0:
                            pe.wait_ge(shifted, 32 * r)
                        reached(pe, p_ready, (r - 1) * H + h - 1)
                        for c in range(KC):
                            m = nc.tensor.matmul(s_ps[h % 2][:, c], KS[i][:, h, c * P:(c + 1) * P],
                                                 QS[i][:, h], start=True, stop=True)
                        m.then_inc(s_made, 1)
                    if h < H // 2 and exists(r):
                        if h == 0:
                            pe.wait_ge(zeroed, 16 * (r + 1))
                            pe.wait_ge(stacked, 16 * N_STACK * (r + 1))
                        for g in (2 * h, 2 * h + 1):
                            reached(pe, max_ready, r * H + g - 1)
                            for c in range(KC):
                                m = nc.tensor.matmul(m_ps[g % 2][:, c], QS[j][:, g, c * P:(c + 1) * P],
                                                     KS[j][:, g], start=True, stop=True)
                            m.then_inc(m_made, 1)
                    if exists(r - 2):
                        if h == 0:
                            pe.wait_ge(oT_copied, 2 * (r - 1))
                            if exists(r - 1):
                                pe.wait_ge(shift_ready, r)
                                pe.wait_ge(v_ready, r)
                            else:
                                pe.wait_ge(norm.row_ready, r - 2)
                            for c, to in enumerate((a_ps, b_ps)):
                                for k in range(4):
                                    m = nc.tensor.transpose(to[:].rearrange("p c s -> p (c s)")[:, k * P:(k + 1) * P],
                                                            oT[:, k, c * P:(c + 1) * P], ident[:])
                            m.then_inc(nat_made, 1)
                        if h == 3:
                            pe.wait_ge(o_ready, r - 1)
                            for c in range(KC):
                                m = nc.tensor.transpose(a_ps[:, 0, c * P:(c + 1) * P],
                                                        o[:, c].rearrange("p h d -> p (h d)"), ident[:])
                            m.then_inc(onT_made, 1)
                        if h == 5:
                            pe.wait_ge(onT_copied, r - 1)
                            nc.tensor.matmul(b_ps[:, 0], w[:, 3], onT[:], start=True, stop=True).then_inc(y_made, 1)
                    if h == 6 and exists(r + 1):
                        project_qk(r + 1, (j + 1) % R)
                    if h == 9:
                        if exists(r):
                            reached(pe, norm.row_ready, r - 1)
                            pe.wait_ge(ctx_loaded, 16 * (r + 1))
                            for c in range(KC):
                                m = nc.tensor.matmul(b_ps[:, c, 0:P], ctx[j][:, c * P:(c + 1) * P], w[:, 2],
                                                     start=True, stop=True)
                            m.then_inc(v_made, 1)
                    if h == 12 and exists(r):
                        pe.wait_ge(pair_ready, r + 1)
                        if exists(r + 1):
                            pe.wait_ge(qk_taken, r + 2)
                        for c in range(KC):
                            m = nc.tensor.transpose(a_ps[0:NPAR * H, 1, c * P:(c + 1) * P],
                                                    pair[:, c].rearrange("p n h -> p (n h)"), ident[:])
                        m.then_inc(pair_turned, 1)
                    if exists(r - 1):
                        if h >= 1:
                            attend(r, i, h - 1)
                        if h == H - 1:
                            attend(r, i, h)

            def attend(r, i, h):
                if h == 0:
                    pe.wait_ge(v_ready, r)
                if h in (0, H // 2):
                    reached(pe, oT_copied, 2 * (r - 2) + (1 if h else 0))
                pe.wait_ge(p_ready, (r - 1) * H + h + 1)
                q = h % 4 * VW
                for c in range(KC):
                    m = nc.tensor.matmul(o_ps[h // 8][q:q + VW, h // 4 % 2], V[i][:, c, h], pr[h % 2][:, c],
                                         start=(c == 0), stop=(c == KC - 1))
                m.then_inc(pv_done, 1)

            pe.wait_ge(ready, NR + 1)
            project_qk(0, 0)
            rounds(pe, work)

        @block.vector
        def _(dve):
            def work(r, j):
                for g in range(H):
                    if exists(r):
                        dve.wait_ge(m_made, r * H + g + 1)
                        nc.vector.tensor_reduce(negmax[:, :, g], m_ps[g % 2][:], AX.X, ALU.max,
                                                negate=True).then_inc(max_ready, 1)
                    if g == 2 and exists(r - 2):
                        dve.wait_ge(nat_made, r - 1)
                        for c, src in enumerate((a_ps, b_ps)):
                            s4 = src[:].rearrange("p c s -> p (c s)").rearrange("p (h e) -> p h e", h=H)
                            nc.vector.reciprocal(inverse[:, c], s4[:, :, FD]).then_inc(inv_ready, 1)
                        for c, src in enumerate((a_ps, b_ps)):
                            s4 = src[:].rearrange("p c s -> p (c s)").rearrange("p (h e) -> p h e", h=H)
                            dve.wait_ge(inv_ready, 2 * (r - 1) - 1 + c)
                            m = nc.vector.tensor_tensor(o[:, c], s4[:, :, 0:FD],
                                                        inverse[:, c, :, None].to_broadcast([P, H, FD]), ALU.mult)
                        m.then_inc(o_ready, 1)
                    if g == 13 and exists(r - 2):
                        dve.wait_ge(y_made, r - 1)
                        nc.vector.scalar_tensor_tensor(norm.row[:], b_ps[:, 0], bias[:, 3:4],
                                                       X[:, bass.ds((r - 2) * D, D)], ALU.add,
                                                       ALU.add).then_inc(norm.row_ready, 1)
                        norm.put(dve, r - 2)
                if exists(r):
                    dve.wait_ge(max_ready, (r + 1) * H)
                    reached(dve, pair_turned, r)
                    nc.vector.tensor_copy(high[:], negmax[:]).then_inc(high_ready, 1)
                    dve.wait_ge(high_ready, r + 1)
                    nc.vector.tensor_copy(pair[:, :, 0], high[:])
                    nc.vector.tensor_tensor(pair[:, :, 1], negmax[:], high[:],
                                            ALU.subtract).then_inc(pair_ready, 1)

            dve.wait_ge(ready, NR)
            for j in range(R):
                nc.vector.memset(V[j][:, :, :, FD:FD + 1], 1.0)
                m = nc.vector.memset(KS[j][32:64], 1.0)
            m.then_inc(ready, 1)
            dve.wait_ge(w_loaded, 32)
            rounds(dve, work)
            norm.vector_part(dve)


def ffn(nc, room, A, X, ident, eps):
    E, W, SW = 8, 176, 704
    GROUPS = [(e * W, W, e) for e in range(E)] + [(E * W + at, min(256, SW - at), E) for at in range(0, SW, 256)]
    NG = len(GROUPS)
    LAST = [max(p for p in range(-NG, k) if p % NG % 3 == k % 3) + 1 for k in range(NG)]
    INNER = E * W + SW
    CHUNKS = list(range(0, INNER, P))
    BUNDLES = [list(range(n, min(n + 4, len(CHUNKS)))) for n in range(0, len(CHUNKS), 4)]
    NB = len(BUNDLES)
    TOP = 2
    PAD = E + 8 - TOP
    R = 2

    w_up = room.sb("w_up", [P, KC, 2 * INNER])
    w_down = room.sb("w_down", [P, len(CHUNKS), D])
    w_router = room.sb("w_router", [P, KC, E + 1])
    xin = room.sb("xin", [P, D])
    xT = [room.sb(f"xT{j}", [P, KC, P]) for j in range(R)]
    th = [room.sb(f"th{j}", [P, 256]) for j in range(3)]
    gate = [room.sb(f"gate{j}", [P, 256]) for j in range(2)]
    hid = room.sb("hid", [P, len(CHUNKS) * P])
    hT = [room.sb(f"hT{j}", [P, 4, P]) for j in range(2)]
    logits = room.sb("logits", [P, E + 1])
    negmax = room.sb("negmax", [P, 1])
    total = room.sb("total", [P, 1])
    inverse = room.sb("inverse", [P, 1])
    expd = room.sb("expd", [P, E + 1])
    probs = room.sb("probs", [P, PAD])
    best = room.sb("best", [P, 8])
    places = room.sb("places", [P, 8])
    left = room.sb("left", [P, PAD])
    weight = room.sb("weight", [P, E + 1])
    norm = RowNorm(nc, room, X, eps)
    up_ps = [room.ps([P, 512]) for j in range(3)]
    hT_ps = [room.ps([P, 4, P]) for j in range(2)]
    y_ps = room.ps([P, 512])
    x_ps = room.ps([P, KC, D])
    r_ps = room.ps([P, 512])

    w_loaded, down_loaded, ready = room.sems("w_loaded down_loaded ready")
    up_loaded = [room.sem(f"up_loaded{k}") for k in range(NG)]
    xin_ready, x_turned, xT_copied = room.sems("xin_ready x_turned xT_copied")
    up_made, th_ready, gate_ready, h_ready = room.sems("up_made th_ready gate_ready h_ready")
    hT_made, hT_copied, down_done = room.sems("hT_made hT_copied down_done")
    r_made, r_taken, r_max, e_ready, r_inv, p_ready = room.sems("r_made r_taken r_max e_ready r_inv p_ready")
    best_ready, list_ready, left_ready, weight_ready = room.sems("best_ready list_ready left_ready weight_ready")

    def rounds(eng, work):
        for r in range(R):
            work(r, r)
        with eng.Fori(R, B - R - 1, R) as r:
            for j in range(R):
                work(r + j, j)
        for r in range(B - R, B + 1):
            work(r, r % R)

    def exists(b):
        return not isinstance(b, int) or 0 <= b < B

    with nc.Block() as block:

        @block.sync
        def _(sp):
            sp.dma_start(w_router[:], A["f_router"]).then_inc(w_loaded, 16)
            for k, (at, n, e) in enumerate(GROUPS):
                cols = slice(2 * at, 2 * (at + n))
                sp.dma_start(w_up[:, :, cols], A["f_up"][:, :, cols]).then_inc(up_loaded[k], 16)
            sp.dma_start(w_down[:], A["f_down"]).then_inc(down_loaded, 16)
            sp.wait_ge(down_loaded, 16)

        @block.gpsimd
        def _(pool):
            def copy(b):
                reached(pool, x_turned, b)
                nc.gpsimd.tensor_copy(xin[:], X[:, bass.ds(b * D, D)]).then_inc(xin_ready, 1)

            def work(r, j):
                if exists(r + 1):
                    copy(r + 1)

            copy(0)
            rounds(pool, work)

        @block.scalar
        def _(act):
            def copy_xT(b, j):
                act.wait_ge(x_turned, b + 1)
                nc.scalar.copy(xT[j][:], x_ps[:, 0].rearrange("p (c t) -> p c t", c=KC)).then_inc(xT_copied, 1)

            def router_exp(b):
                act.wait_ge(r_max, b + 1)
                nc.scalar.activation(expd[:, 0:E], logits[:, 0:E], ACT.Exp, bias=negmax[:], accum_out=total[:])
                nc.scalar.activation(expd[:, E:E + 1], logits[:, E:E + 1], ACT.Tanh, scale=0.5).then_inc(e_ready, 1)

            def work(r, j):
                for k in range(NG):
                    n = GROUPS[k][1]
                    if exists(r):
                        act.wait_ge(up_made, r * NG + k + 1)
                        reached(act, gate_ready, r * NG + LAST[k])
                        nc.scalar.activation(th[k % 3][:, 0:n], up_ps[k % 3][:, 0:n],
                                             ACT.Tanh, scale=0.5).then_inc(th_ready, 1)
                    if k < NB and exists(r - 1):
                        act.wait_ge(hT_made, (r - 1) * NB + k + 1)
                        reached(act, down_done, (r - 1) * NB + k - 1)
                        m = 4 if k < NB - 1 else 1
                        nc.scalar.copy(hT[k % 2][:, 0:m], hT_ps[k % 2][:, 0:m]).then_inc(hT_copied, 1)
                    if k == 7 and exists(r + 1):
                        copy_xT(r + 1, 1 - j)
                if exists(r + 1):
                    router_exp(r + 1)

            copy_xT(0, 0)
            router_exp(0)
            rounds(act, work)
            norm.scalar_part(act)

        @block.tensor
        def _(pe):
            def turn_x(b):
                pe.wait_ge(xin_ready, b + 1)
                for c in range(KC):
                    m = nc.tensor.transpose(x_ps[:, 0, c * P:(c + 1) * P], xin[:, c * P:(c + 1) * P], ident[:])
                m.then_inc(x_turned, 1)

            def router(b, j):
                pe.wait_ge(xT_copied, b + 1)
                for c in range(KC):
                    m = nc.tensor.matmul(r_ps[:, 0:E + 1], xT[j][:, c], w_router[:, c],
                                         start=(c == 0), stop=(c == KC - 1))
                m.then_inc(r_made, 1)

            def down(b, k):
                pe.wait_ge(hT_copied, b * NB + k + 1)
                if k == 0:
                    reached(pe, norm.row_ready, b)
                for n, c in enumerate(BUNDLES[k]):
                    m = nc.tensor.matmul(y_ps[:, 0:D], hT[k % 2][:, n], w_down[:, c],
                                         start=(c == 0), stop=(c == len(CHUNKS) - 1))
                m.then_inc(down_done, 1)

            def work(r, j):
                for k in range(NG):
                    if k < NB and exists(r - 1):
                        if k == 0:
                            pe.wait_ge(h_ready, r * NG)
                        reached(pe, hT_copied, (r - 1) * NB + k - 1)
                        for n, c in enumerate(BUNDLES[k]):
                            at = CHUNKS[c]
                            m = nc.tensor.transpose(hT_ps[k % 2][:, n], hid[:, at:at + P], ident[:])
                        m.then_inc(hT_made, 1)
                    if exists(r):
                        at, n, e = GROUPS[k]
                        reached(pe, h_ready, r * NG + LAST[k])
                        if isinstance(r, int) and r == 0:
                            pe.wait_ge(up_loaded[k], 16)
                        for c in range(KC):
                            m = nc.tensor.matmul(up_ps[k % 3][:, 0:2 * n], xT[j][:, c],
                                                 w_up[:, c, 2 * at:2 * (at + n)],
                                                 start=(c == 0), stop=(c == KC - 1))
                        m.then_inc(up_made, 1)
                    if 1 <= k <= NB and exists(r - 1):
                        down(r - 1, k - 1)
                    if k == 6 and exists(r + 1):
                        turn_x(r + 1)
                    if k == NG - 1 and isinstance(r, int) and r == 0:
                        pe.wait_ge(down_loaded, 16)
                    if k == 8 and exists(r + 1):
                        pe.wait_ge(r_taken, r + 1)
                        router(r + 1, 1 - j)

            turn_x(0)
            pe.wait_ge(w_loaded, 16)
            router(0, 0)
            rounds(pe, work)

        @block.vector
        def _(dve):
            def route(b):
                dve.wait_ge(r_made, b + 1)
                nc.vector.tensor_copy(logits[:], r_ps[:, 0:E + 1]).then_inc(r_taken, 1)
                dve.wait_ge(r_taken, b + 1)
                nc.vector.tensor_reduce(negmax[:], logits[:, 0:E], AX.X, ALU.max, negate=True).then_inc(r_max, 1)
                dve.wait_ge(e_ready, b + 1)
                nc.vector.reciprocal(inverse[:], total[:]).then_inc(r_inv, 1)
                dve.wait_ge(r_inv, b + 1)
                nc.vector.tensor_scalar(probs[:, 0:E], expd[:, 0:E], inverse[:], None, ALU.mult).then_inc(p_ready, 1)
                dve.wait_ge(p_ready, b + 1)
                nc.vector.memset(places[:], -1.0)
                nc.vector.max(best[:], probs[:]).then_inc(best_ready, 1)
                dve.wait_ge(best_ready, b + 1)
                nc.vector.tensor_copy(places[:, 0:TOP], best[:, 0:TOP]).then_inc(list_ready, 1)
                dve.wait_ge(list_ready, b + 1)
                nc.vector.tensor_scalar(expd[:, E:E + 1], expd[:, E:E + 1], 1.0, 0.25, ALU.add, ALU.mult)
                nc.vector.match_replace(left[:], places[:], probs[:], -2.0).then_inc(left_ready, 1)
                dve.wait_ge(left_ready, b + 1)
                nc.vector.tensor_scalar(left[:, 0:E], left[:, 0:E], -2.0, 0.5, ALU.is_equal,
                                        ALU.mult).then_inc(weight_ready, 1)
                dve.wait_ge(weight_ready, 3 * b + 1)
                nc.vector.tensor_tensor(weight[:, 0:E], left[:, 0:E], probs[:, 0:E], ALU.mult).then_inc(weight_ready, 1)
                nc.vector.tensor_copy(weight[:, E:E + 1], expd[:, E:E + 1]).then_inc(weight_ready, 1)
                dve.wait_ge(weight_ready, 3 * b + 3)

            def work(r, j):
                for k in range(NG):
                    if exists(r):
                        at, n, e = GROUPS[k]
                        dve.wait_ge(th_ready, r * NG + k + 1)
                        nc.vector.scalar_tensor_tensor(gate[k % 2][:, 0:n], th[k % 3][:, 0:n], 1.0,
                                                       up_ps[k % 3][:, 0:n], ALU.add, ALU.mult).then_inc(gate_ready, 1)
                        dve.wait_ge(gate_ready, r * NG + k + 1)
                        if exists(r - 1):
                            dve.wait_ge(hT_made, (r - 1) * NB + 1 + (at + n - 1) // (4 * P))
                        nc.vector.scalar_tensor_tensor(hid[:, at:at + n], gate[k % 2][:, 0:n], weight[:, e:e + 1],
                                                       up_ps[k % 3][:, n:2 * n], ALU.mult, ALU.mult).then_inc(h_ready, 1)
                    if k == 8 and exists(r - 1):
                        dve.wait_ge(down_done, r * NB)
                        nc.vector.tensor_tensor(norm.row[:], X[:, bass.ds((r - 1) * D, D)], y_ps[:, 0:D],
                                                ALU.add).then_inc(norm.row_ready, 1)
                        norm.put(dve, r - 1)
                if exists(r + 1):
                    route(r + 1)

            nc.vector.memset(hid[:, INNER:], 0.0)
            nc.vector.memset(probs[:], -1.0).then_inc(ready, 1)
            dve.wait_ge(ready, 1)
            route(0)
            rounds(dve, work)
            norm.vector_part(dve)


def low_rank_attention(nc, room, A, X, ident, eps):
    RANK = 32
    SCALE = float(1.0 / np.sqrt(np.float32(RANK)))
    R = 4

    w_rank = room.sb("w_rank", [P, KC, 2, RANK])
    wo = room.sb("wo", [P, KC, D])
    bo = room.sb("bo", [P, D])
    mask = room.sb("mask", [P, P])
    xin = [room.sb(f"xin{j}", [P, D]) for j in range(R)]
    xT = [room.sb(f"xT{j}", [P, KC, P]) for j in range(2)]
    sa = [room.sb(f"sa{j}", [RANK, 2, P]) for j in range(2)]
    sc = [room.sb(f"sc{j}", [P, P]) for j in range(2)]
    p = [room.sb(f"p{j}", [P, P]) for j in range(2)]
    negmax = [room.sb(f"negmax{j}", [P, 1]) for j in range(2)]
    total = [room.sb(f"total{j}", [P, 1]) for j in range(2)]
    inverse = room.sb("inverse", [P, 1])
    pT = [room.sb(f"pT{j}", [P, P]) for j in range(2)]
    oT = [room.sb(f"oT{j}", [P, KC, P]) for j in range(2)]
    xb = [room.sb(f"xb{j}", [P, D]) for j in range(2)]
    norm = RowNorm(nc, room, X, eps)
    x_ps = room.ps([P, 512])
    sa_ps = room.ps([P, 512])
    s_ps = room.ps([P, 512])
    pT_ps = room.ps([P, 512])
    o_ps = room.ps([P, 512])
    y_ps = room.ps([P, 512])

    w_loaded, = room.sems("w_loaded")
    xin_ready, x_turned, xT_copied, sa_made, sa_copied = room.sems(
        "xin_ready x_turned xT_copied sa_made sa_copied")
    s_made, s_taken, max_ready, e_ready, inv_ready, p_ready = room.sems(
        "s_made s_taken max_ready e_ready inv_ready p_ready")
    pT_made, pT_copied, o_made, oT_copied, y_made, xb_ready = room.sems(
        "pT_made pT_copied o_made oT_copied y_made xb_ready")

    def rounds(eng, work, last):
        n = 2 * R
        for r in range(n):
            work(r, r % R)
        with eng.Fori(n, B - R + 1, R) as r:
            for j in range(R):
                work(r + j, j)
        for r in range(B, B + last):
            work(r, r % R)

    def exists(b):
        return not isinstance(b, int) or 0 <= b < B

    with nc.Block() as block:

        @block.sync
        def _(sp):
            sp.dma_start(w_rank[:], A["r_rank"]).then_inc(w_loaded, 16)
            sp.dma_start(wo[:], A["r_wo"]).then_inc(w_loaded, 16)
            sp.dma_start(bo[:], A["r_bo"].partition_broadcast(P)).then_inc(w_loaded, 16)
            sp.dma_start(mask[:], A["causal"]).then_inc(w_loaded, 16)
            sp.wait_ge(w_loaded, 64)

        @block.gpsimd
        def _(pool):
            def work(r, j):
                if exists(r):
                    reached(pool, o_made, r - R + 1)
                    nc.gpsimd.tensor_copy(xin[j][:], X[:, bass.ds(r * D, D)]).then_inc(xin_ready, 1)
                if exists(r - 5):
                    reached(pool, norm.row_ready, r - 6)
                    nc.gpsimd.tensor_tensor(xb[(j - 5) % 2][:], X[:, bass.ds((r - 5) * D, D)], bo[:],
                                            ALU.add).then_inc(xb_ready, 1)

            pool.wait_ge(w_loaded, 64)
            rounds(pool, work, 5)

        @block.scalar
        def _(act):
            def work(r, j):
                if exists(r - 1):
                    act.wait_ge(x_turned, r)
                    reached(act, sa_made, r - 2)
                    nc.scalar.copy(xT[(j - 1) % 2][:], x_ps[:, 0:D].rearrange("p (c t) -> p c t", c=KC)).then_inc(xT_copied, 1)
                if exists(r - 2):
                    act.wait_ge(sa_made, r - 1)
                    reached(act, s_made, r - 3)
                    nc.scalar.copy(sa[(j - 2) % 2][:], sa_ps[0:RANK, 0:2 * P].rearrange("p (c t) -> p c t", c=2)).then_inc(sa_copied, 1)
                if exists(r - 3):
                    act.wait_ge(max_ready, r - 2)
                    reached(act, pT_made, r - 4)
                    nc.scalar.activation(p[(j - 3) % 2][:], sc[(j - 3) % 2][:], ACT.Exp, bias=negmax[(j - 3) % 2][:],
                                         accum_out=total[(j - 3) % 2][:]).then_inc(e_ready, 1)
                if exists(r - 4):
                    act.wait_ge(pT_made, r - 3)
                    reached(act, o_made, r - 5)
                    nc.scalar.copy(pT[(j - 4) % 2][:], pT_ps[:, 0:P]).then_inc(pT_copied, 1)
                if exists(r - 5):
                    act.wait_ge(o_made, r - 4)
                    reached(act, y_made, r - 6)
                    nc.scalar.copy(oT[(j - 5) % 2][:], o_ps[:, 0:D].rearrange("p (c t) -> p c t", c=KC)).then_inc(oT_copied, 1)

            rounds(act, work, 6)
            norm.scalar_part(act)

        @block.tensor
        def _(pe):
            def work(r, j):
                if exists(r - 5):
                    pe.wait_ge(oT_copied, r - 4)
                    reached(pe, norm.row_ready, r - 5)
                    for c in range(KC):
                        m = nc.tensor.matmul(y_ps[:, 0:D], oT[(j - 5) % 2][:, c], wo[:, c],
                                             start=(c == 0), stop=(c == KC - 1))
                    m.then_inc(y_made, 1)
                if exists(r - 4):
                    pe.wait_ge(pT_copied, r - 3)
                    reached(pe, oT_copied, r - 4)
                    for c in range(KC):
                        m = nc.tensor.matmul(o_ps[:, c * P:(c + 1) * P], xin[(j - 4) % R][:, c * P:(c + 1) * P],
                                             pT[(j - 4) % 2][:], start=True, stop=True)
                    m.then_inc(o_made, 1)
                if exists(r - 3):
                    pe.wait_ge(p_ready, r - 2)
                    reached(pe, pT_copied, r - 3)
                    nc.tensor.transpose(pT_ps[:, 0:P], p[(j - 3) % 2][:], ident[:]).then_inc(pT_made, 1)
                if exists(r - 2):
                    pe.wait_ge(sa_copied, r - 1)
                    reached(pe, s_taken, r - 2)
                    nc.tensor.matmul(s_ps[:, 0:P], sa[(j - 2) % 2][:, 0], sa[(j - 2) % 2][:, 1],
                                     start=True, stop=True).then_inc(s_made, 1)
                if exists(r - 1):
                    pe.wait_ge(xT_copied, r)
                    reached(pe, sa_copied, r - 1)
                    for i in range(2):
                        for c in range(KC):
                            m = nc.tensor.matmul(sa_ps[0:RANK, i * P:(i + 1) * P], w_rank[:, c, i], xT[(j - 1) % 2][:, c],
                                                 start=(c == 0), stop=(c == KC - 1))
                    m.then_inc(sa_made, 1)
                if exists(r):
                    pe.wait_ge(xin_ready, r + 1)
                    reached(pe, xT_copied, r)
                    for c in range(KC):
                        m = nc.tensor.transpose(x_ps[:, c * P:(c + 1) * P], xin[j][:, c * P:(c + 1) * P], ident[:])
                    m.then_inc(x_turned, 1)

            pe.wait_ge(w_loaded, 64)
            rounds(pe, work, 6)

        @block.vector
        def _(dve):
            def work(r, j):
                if exists(r - 5):
                    dve.wait_ge(y_made, r - 4)
                    dve.wait_ge(xb_ready, r - 4)
                    nc.vector.tensor_tensor(norm.row[:], xb[(j - 5) % 2][:], y_ps[:, 0:D],
                                            ALU.add).then_inc(norm.row_ready, 1)
                    norm.put(dve, r - 5)
                if exists(r - 3):
                    i = (j - 3) % 2
                    dve.wait_ge(e_ready, r - 2)
                    nc.vector.reciprocal(inverse[:], total[i][:]).then_inc(inv_ready, 1)
                    dve.wait_ge(inv_ready, r - 2)
                    nc.vector.tensor_scalar(p[i][:], p[i][:], inverse[:], None, ALU.mult).then_inc(p_ready, 1)
                if exists(r - 2):
                    i = (j - 2) % 2
                    dve.wait_ge(s_made, r - 1)
                    reached(dve, e_ready, r - 3)
                    nc.vector.scalar_tensor_tensor(sc[i][:], s_ps[:, 0:P], SCALE, mask[:], ALU.mult,
                                                   ALU.add).then_inc(s_taken, 1)
                    dve.wait_ge(s_taken, r - 1)
                    nc.vector.tensor_reduce(negmax[i][:], sc[i][:], AX.X, ALU.max, negate=True).then_inc(max_ready, 1)

            dve.wait_ge(w_loaded, 64)
            rounds(dve, work, 6)
            norm.vector_part(dve)


def wkv(nc, room, A, X, ident, eps):
    BG = 4
    NG = B // BG
    T1 = P + 1
    LOW = -1.0e38
    U = NG * KC
    OLD, NEW, CARRY, ENTER = range(4)

    wu = room.sb("wu", [P, 2, KC])
    zeros = room.sb("zeros", [P, BG, T1])
    decay = [room.sb(f"decay{c}", [P, BG, T1]) for c in range(KC)]
    xin = [room.sb(f"xin{j}", [P, BG, P]) for j in range(2)]
    vin = [room.sb(f"vin{j}", [P, BG, P]) for j in range(2)]
    k = [room.sb(f"k{j}", [P, BG, T1]) for j in range(2)]
    v = [room.sb(f"v{j}", [P, BG, P]) for j in range(2)]
    o = [room.sb(f"o{j}", [P, BG, T1]) for j in range(2)]
    no = room.sb("no", [P, BG, P])
    arg = [room.sb(f"arg{j}", [P, 4, BG, P]) for j in range(2)]
    ex = [room.sb(f"ex{j}", [P, 4, BG, T1]) for j in range(2)]
    ev = room.sb("ev", [P, BG, T1])
    ps = room.sb("ps", [P, BG, T1])
    qs = room.sb("qs", [P, BG, T1])
    enter = room.sb("enter", [P, BG, P])
    old = room.sb("old", [P, BG, P])
    num = room.sb("num", [P, BG, P])
    den1 = room.sb("den1", [P, BG, P])
    den = room.sb("den", [P, BG, P])
    inv = room.sb("inv", [P, BG, P])
    y = [room.sb(f"y{j}", [P, BG, P]) for j in range(2)]
    norm = RowNorm(nc, room, X, eps)
    k_ps = [room.ps([P, BG, P]) for j in range(2)]
    v_ps = [room.ps([P, BG, P]) for j in range(2)]
    y_ps = [room.ps([P, BG, P]) for j in range(2)]

    w_loaded, cleared, ready = room.sems("w_loaded cleared ready")
    v_loaded = room.sems("v_loaded0 v_loaded1")
    xin_ready, turned, kv_copied = room.sems("xin_ready turned kv_copied")
    o_ready, no_ready, arg_dve, arg_pool, ex_ready = room.sems("o_ready no_ready arg_dve arg_pool ex_ready")
    ev_ready, p_ready, q_ready, enter_ready, old_ready = room.sems("ev_ready p_ready q_ready enter_ready old_ready")
    num_ready, den1_ready, den_ready, inv_ready, y_ready = room.sems("num_ready den1_ready den_ready inv_ready y_ready")
    y_turned, added = room.sems("y_turned added")

    def rounds(eng, work):
        for r in range(4):
            work(r, r % 2, r // 2)
        with eng.Fori(2, NG) as g:
            for c in range(2):
                work(g * 2 + c, c, g)
        for r in range(U, U + 3):
            work(r, r % 2, r // 2)

    def exists(u):
        return not isinstance(u, int) or 0 <= u < U

    def part(t, g, c):
        return t[:, bass.ds(g * (BG * D), BG * D)].rearrange("p (b d) -> p b d", b=BG)[:, :, c * P:(c + 1) * P]

    def flat(t):
        return t[:].rearrange("p b t -> p (b t)")

    with nc.Block() as block:

        @block.sync
        def _(sp):
            def work(r, c, g):
                if exists(r):
                    reached(sp, turned, r - 1)
                    sp.dma_start(vin[c][:], part(A["ctx"], g, c)).then_inc(v_loaded[c], 16)

            sp.dma_start(wu[:], A["w_wu"]).then_inc(w_loaded, 16)
            rounds(sp, work)
            for c in range(KC):
                sp.wait_ge(v_loaded[c], 16 * NG)

        @block.gpsimd
        def _(pool):
            def work(r, c, g):
                if exists(r):
                    reached(pool, turned, r - 1)
                    nc.gpsimd.tensor_copy(xin[c][:], part(X, g, c)).then_inc(xin_ready, 1)
                i = 1 - c
                if exists(r - 1):
                    pool.wait_ge(ex_ready, r)
                    reached(pool, p_ready, r - 1)
                    nc.gpsimd.tensor_tensor(ev[:, :, 1:], ex[i][:, ENTER, :, 1:], v[i][:], ALU.mult).then_inc(ev_ready, 1)
                    reached(pool, num_ready, r - 1)
                    nc.gpsimd.tensor_tensor(enter[:], ex[i][:, NEW, :, 1:], v[i][:], ALU.mult).then_inc(enter_ready, 1)
                    pool.wait_ge(q_ready, r)
                    nc.gpsimd.tensor_tensor(den1[:], ex[i][:, OLD, :, 1:], qs[:, :, 0:P], ALU.mult).then_inc(den1_ready, 1)
                    pool.wait_ge(den1_ready, r)
                    reached(pool, inv_ready, r - 1)
                    nc.gpsimd.tensor_tensor(den[:], den1[:], ex[i][:, NEW, :, 1:], ALU.add).then_inc(den_ready, 1)
                if exists(r):
                    pool.wait_ge(o_ready, r + 1)
                    reached(pool, ex_ready, r - 1)
                    nc.gpsimd.tensor_tensor(arg[c][:, ENTER], k[c][:, :, 1:], o[c][:, :, 1:], ALU.subtract)
                    pool.wait_ge(no_ready, r + 1)
                    nc.gpsimd.tensor_tensor(arg[c][:, OLD], o[c][:, :, 0:P], no[:], ALU.subtract).then_inc(arg_pool, 1)

            nc.gpsimd.memset(zeros[:], 0.0)
            nc.gpsimd.memset(ev[:], 0.0)
            for j in range(2):
                nc.gpsimd.memset(k[j][:], LOW)
                m = nc.gpsimd.memset(ex[j][:], 0.0)
            m.then_inc(cleared, 1)
            pool.wait_ge(cleared, 1)
            rounds(pool, work)

        @block.scalar
        def _(act):
            def work(r, c, g):
                if exists(r):
                    act.wait_ge(turned, r + 1)
                    reached(act, den_ready, r - 1)
                    nc.scalar.copy(k[c][:, :, 1:], k_ps[c][:])
                    nc.scalar.copy(v[c][:], v_ps[c][:]).then_inc(kv_copied, 1)
                    act.wait_ge(arg_dve, r + 1)
                    act.wait_ge(arg_pool, r + 1)
                    reached(act, num_ready, r - 1)
                    nc.scalar.activation(ex[c][:, :, :, 1:].rearrange("p k b t -> p (k b) t"),
                                         arg[c][:].rearrange("p k b t -> p (k b) t"), ACT.Exp).then_inc(ex_ready, 1)

            act.wait_ge(cleared, 1)
            rounds(act, work)
            norm.scalar_part(act)

        @block.tensor
        def _(pe):
            def work(r, c, g):
                if exists(r):
                    pe.wait_ge(xin_ready, r + 1)
                    pe.wait_ge(v_loaded[c], 16 * (g + 1))
                    reached(pe, kv_copied, r - 1)
                    for n in range(BG):
                        nc.tensor.transpose(k_ps[c][:, n], xin[c][:, n], ident[:])
                        m = nc.tensor.transpose(v_ps[c][:, n], vin[c][:, n], ident[:])
                    m.then_inc(turned, 1)
                if exists(r - 2):
                    pe.wait_ge(y_ready, r - 1)
                    reached(pe, added, r - 3)
                    for n in range(BG):
                        m = nc.tensor.transpose(y_ps[c][:, n], y[c][:, n], ident[:])
                    m.then_inc(y_turned, 1)

            rounds(pe, work)

        @block.vector
        def _(dve):
            def work(r, c, g):
                if exists(r):
                    w, u = wu[:, 0, c:c + 1], wu[:, 1, c:c + 1]
                    dve.wait_ge(kv_copied, r + 1)
                    reached(dve, arg_pool, r - 1)
                    nc.vector.tensor_tensor_scan(flat(o[c]), flat(decay[c]), flat(k[c]), LOW, ALU.add,
                                                 ALU.max).then_inc(o_ready, 1)
                    dve.wait_ge(o_ready, r + 1)
                    reached(dve, arg_pool, r)
                    nc.vector.scalar_tensor_tensor(no[:], k[c][:, :, 1:], u, o[c][:, :, 0:P], ALU.add,
                                                   ALU.max).then_inc(no_ready, 1)
                    reached(dve, ex_ready, r - 1)
                    nc.vector.scalar_tensor_tensor(arg[c][:, CARRY], o[c][:, :, 0:P], w, o[c][:, :, 1:], ALU.add,
                                                   ALU.subtract)
                    dve.wait_ge(no_ready, r + 1)
                    nc.vector.scalar_tensor_tensor(arg[c][:, NEW], k[c][:, :, 1:], u, no[:], ALU.add,
                                                   ALU.subtract).then_inc(arg_dve, 1)
                i = 1 - c
                if exists(r - 1):
                    dve.wait_ge(ex_ready, r)
                    reached(dve, den1_ready, r - 1)
                    nc.vector.tensor_tensor_scan(flat(qs), ex[i][:, CARRY].rearrange("p b t -> p (b t)"),
                                                 ex[i][:, ENTER].rearrange("p b t -> p (b t)"), 0.0, ALU.mult,
                                                 ALU.add).then_inc(q_ready, 1)
                    dve.wait_ge(ev_ready, r)
                    nc.vector.tensor_tensor_scan(flat(ps), ex[i][:, CARRY].rearrange("p b t -> p (b t)"), flat(ev),
                                                 0.0, ALU.mult, ALU.add).then_inc(p_ready, 1)
                    dve.wait_ge(p_ready, r)
                    nc.vector.tensor_tensor(old[:], ex[i][:, OLD, :, 1:], ps[:, :, 0:P], ALU.mult).then_inc(old_ready, 1)
                    dve.wait_ge(old_ready, r)
                    dve.wait_ge(enter_ready, r)
                    nc.vector.tensor_tensor(num[:], old[:], enter[:], ALU.add).then_inc(num_ready, 1)
                    dve.wait_ge(den_ready, r)
                    nc.vector.reciprocal(inv[:], den[:]).then_inc(inv_ready, 1)
                    dve.wait_ge(inv_ready, r)
                    reached(dve, y_turned, r - 2)
                    nc.vector.tensor_tensor(y[i][:], num[:], inv[:], ALU.mult).then_inc(y_ready, 1)
                if exists(r - 2):
                    dve.wait_ge(y_turned, r - 1)
                    nc.vector.tensor_tensor(part(X, g - 1, c), part(X, g - 1, c), y_ps[c][:], ALU.add).then_inc(added, 1)

            dve.wait_ge(w_loaded, 16)
            dve.wait_ge(cleared, 1)
            for c in range(KC):
                nc.vector.memset(decay[c][:], LOW).then_inc(ready, 1)
                dve.wait_ge(ready, 2 * c + 1)
                nc.vector.tensor_scalar(decay[c][:, :, 1:], zeros[:, :, 1:], wu[:, 0, c:c + 1], None,
                                        ALU.add).then_inc(ready, 1)
            dve.wait_ge(ready, 2 * KC)
            rounds(dve, work)
            norm.all_rows(dve, added, U)
            norm.vector_part(dve)


def mixture(nc, room, A, X, ident, eps):
    E, I, TOP = 16, 256, 4
    IC = I // P
    LIMIT, ALPHA = 7.0, 1.702
    PAD = E + 8 - TOP
    NT = 512
    TT = B * P // NT
    TB = NT // P
    R = 2

    norm_w = room.sb("norm_w", [P, KC])
    w_gate = room.sb("w_gate", [P, KC, E])
    b_gate = room.sb("b_gate", [P, E])
    b2 = room.sb("b2", [E, D])
    b1 = room.sb("b1", [P, E, 2, IC])
    w1 = [room.sb(f"w1_{j}", [P, KC, IC, 2, P]) for j in range(R)]
    w2 = [room.sb(f"w2_{j}", [P, IC, D]) for j in range(R)]
    ss = room.sb("ss", [P, B])
    rms = room.sb("rms", [P, B])
    scale = room.sb("scale", [P, B])
    tin = [room.sb(f"tin{j}", [P, D]) for j in range(R)]
    tT1 = [room.sb(f"tT1_{j}", [P, KC, P]) for j in range(R)]
    tT = room.sb("tT", [P, KC * B * P])
    logits = [room.sb(f"logits{j}", [P, PAD]) for j in range(R)]
    best = room.sb("best", [P, 8])
    places = room.sb("places", [P, 8])
    left = room.sb("left", [P, PAD])
    negmax = [room.sb(f"negmax{j}", [P, 1]) for j in range(R)]
    chosen = [room.sb(f"chosen{j}", [P, E]) for j in range(R)]
    expd = [room.sb(f"expd{j}", [P, E]) for j in range(R)]
    kept = room.sb("kept", [P, E])
    total = room.sb("total", [P, 1])
    inverse = room.sb("inverse", [P, 1])
    gates1 = [room.sb(f"gates1_{j}", [P, E]) for j in range(R)]
    gates = room.sb("gates", [P, B * E])
    gT = [room.sb(f"gT{j}", [E, P]) for j in range(R)]
    a = [room.sb(f"a{j}", [P, NT]) for j in range(2)]
    sg = [room.sb(f"sg{j}", [P, NT]) for j in range(2)]
    ag = [room.sb(f"ag{j}", [P, NT]) for j in range(2)]
    bb = [room.sb(f"bb{j}", [P, NT]) for j in range(2)]
    act_ = [room.sb(f"act{j}", [P, IC, NT]) for j in range(2)]
    norm = RowNorm(nc, room, X, eps)
    up_ps = [[room.ps([P, NT]) for h in range(2)] for ic in range(IC)]
    y_ps = [[room.ps([P, 2, D]) for h in range(2)] for j in range(2)]
    x_ps, l_ps, g_ps, b_ps = up_ps[0][0], up_ps[0][1], up_ps[1][0], up_ps[1][1]

    w_loaded, filled, squared, rms_ready, scale_ready = room.sems("w_loaded filled squared rms_ready scale_ready")
    w1_loaded = room.sems("w1_loaded0 w1_loaded1")
    w2_loaded = room.sems("w2_loaded0 w2_loaded1")
    tin_ready, t_turned, t_copied, t_kept = room.sems("tin_ready t_turned t_copied t_kept")
    l_made, l_ready, best_ready, list_ready, left_ready = room.sems("l_made l_ready best_ready list_ready left_ready")
    nm_ready, chosen_ready, e_ready, kept_ready, total_ready, inv_ready, g_ready, g_kept = room.sems(
        "nm_ready chosen_ready e_ready kept_ready total_ready inv_ready g_ready g_kept")
    g_turned, g_copied, b2_made, b2_added = room.sems("g_turned g_copied b2_made b2_added")
    up_made, a_ready, b_ready, sg_ready, ag_ready, act_ready = room.sems(
        "up_made a_ready b_ready sg_ready ag_ready act_ready")
    down_done, y_added = room.sems("down_done y_added")

    def prologue(eng, work):
        for r in range(4):
            work(r, r % R)
        with eng.Fori(4, B - 1, R) as r:
            for j in range(R):
                work(r + j, j)
        for r in range(B, B + 4):
            work(r, r % R)

    def exists(b):
        return not isinstance(b, int) or 0 <= b < B

    U = E * TT

    def experts(eng, work):
        for e in range(R):
            for tt in range(TT):
                work(e, tt, e)
        with eng.Fori(R, E - 1, R) as e:
            for j in range(R):
                for tt in range(TT):
                    work(e + j, tt, j)
        work(E, 0, 0)

    def live(e, tt, back=0):
        return not isinstance(e, int) or 0 <= e * TT + tt - back < U

    with nc.Block() as block:

        @block.sync
        def _(sp):
            def load(e, j):
                sp.dma_start(w1[j][:].rearrange("p c i h n -> p (c i h n)"),
                             A["m_w1"][bass.ds(e, 1)].rearrange("o p n -> (o p) n")).then_inc(w1_loaded[j], 16)
                sp.dma_start(w2[j][:].rearrange("p c n -> p (c n)"),
                             A["m_w2"][bass.ds(e, 1)].rearrange("o p n -> (o p) n")).then_inc(w2_loaded[j], 16)

            for dst, name in ((norm_w, "m_norm"), (w_gate, "m_gate"), (b2, "m_b2"), (b1, "m_b1")):
                sp.dma_start(dst[:], A[name]).then_inc(w_loaded, 16)
            sp.dma_start(b_gate[:], A["m_bgate"].partition_broadcast(P)).then_inc(w_loaded, 16)
            for e in range(R):
                load(e, e)
            with sp.Fori(R, E - 1, R) as e:
                for j in range(R):
                    sp.wait_ge(down_done, (e + j - 1) * TT)
                    load(e + j, j)
            for j in range(R):
                sp.wait_ge(w1_loaded[j], 16 * E // R)
                sp.wait_ge(w2_loaded[j], 16 * E // R)

        @block.gpsimd
        def _(pool):
            def work(r, j):
                if exists(r - 1):
                    pool.wait_ge(t_copied, r)
                    for c in range(KC):
                        m = nc.gpsimd.tensor_copy(tT[:, bass.ds((r - 1) * P + c * B * P, P)], tT1[1 - j][:, c])
                    m.then_inc(t_kept, 1)
                if exists(r - 3):
                    pool.wait_ge(g_ready, r - 2)
                    nc.gpsimd.tensor_copy(gates[:, bass.ds((r - 3) * E, E)], gates1[1 - j][:]).then_inc(g_kept, 1)

            def unit(e, tt, j):
                if live(e, tt):
                    u = (e * TT + tt) * IC
                    for ic in range(IC):
                        pool.wait_ge(sg_ready, u + ic + 1)
                        reached(pool, act_ready, u + ic - 1)
                        nc.gpsimd.tensor_tensor(ag[ic][:], a[ic][:], sg[ic][:], ALU.mult).then_inc(ag_ready, 1)

            prologue(pool, work)
            experts(pool, unit)

        @block.scalar
        def _(act):
            def work(r, j):
                if exists(r - 1):
                    act.wait_ge(t_turned, r)
                    reached(act, t_kept, r - 2)
                    reached(act, l_made, r - 2)
                    for c in range(KC):
                        m = nc.scalar.mul(tT1[1 - j][:, c], x_ps[:, c * P:(c + 1) * P], norm_w[:, c:c + 1])
                    m.then_inc(t_copied, 1)
                if exists(r - 2):
                    act.wait_ge(chosen_ready, r - 1)
                    reached(act, kept_ready, r - 3)
                    nc.scalar.activation(expd[j][:], logits[j][:, 0:E], ACT.Exp, bias=negmax[j][:]).then_inc(e_ready, 1)
                if exists(r - 3):
                    act.wait_ge(g_turned, r - 2)
                    reached(act, b2_made, r - 4)
                    nc.scalar.copy(gT[1 - j][:], g_ps[0:E, 0:P]).then_inc(g_copied, 1)

            def unit(e, tt, j):
                if live(e, tt):
                    u = (e * TT + tt) * IC
                    for ic in range(IC):
                        act.wait_ge(a_ready, u + ic + 1)
                        reached(act, ag_ready, u + ic - 1)
                        nc.scalar.activation(sg[ic][:], a[ic][:], ACT.Sigmoid, scale=ALPHA).then_inc(sg_ready, 1)

            for b in range(B):
                m = nc.scalar.activation(tT[:, b * D:(b + 1) * D], X[:, b * D:(b + 1) * D], ACT.Square,
                                         accum_out=ss[:, b:b + 1])
            m.then_inc(squared, 1)
            act.wait_ge(squared, 1)
            nc.scalar.activation(rms[:], ss[:], ACT.Sqrt, scale=1.0 / D, bias=eps[:]).then_inc(rms_ready, 1)
            act.wait_ge(w_loaded, 80)
            prologue(act, work)
            experts(act, unit)
            norm.scalar_part(act)

        @block.tensor
        def _(pe):
            def work(r, j):
                if exists(r - 3):
                    pe.wait_ge(g_ready, r - 2)
                    reached(pe, g_copied, r - 3)
                    nc.tensor.transpose(g_ps[0:E, 0:P], gates1[1 - j][:], ident[:]).then_inc(g_turned, 1)
                if exists(r - 1):
                    pe.wait_ge(t_copied, r)
                    reached(pe, l_ready, r - 1)
                    for c in range(KC):
                        m = nc.tensor.matmul(l_ps[:, 0:E], tT1[1 - j][:, c], w_gate[:, c],
                                             start=(c == 0), stop=(c == KC - 1))
                    m.then_inc(l_made, 1)
                if exists(r):
                    pe.wait_ge(tin_ready, r + 1)
                    reached(pe, t_copied, r)
                    for c in range(KC):
                        m = nc.tensor.transpose(x_ps[:, c * P:(c + 1) * P], tin[j][:, c * P:(c + 1) * P], ident[:])
                    m.then_inc(t_turned, 1)
                if exists(r - 3):
                    pe.wait_ge(g_copied, r - 2)
                    reached(pe, b2_added, r - 3)
                    nc.tensor.matmul(b_ps[:, 0:D], gT[1 - j][:], b2[:], start=True, stop=True).then_inc(b2_made, 1)

            def unit(e, tt, j):
                u = e * TT + tt
                if live(e, tt):
                    if tt == 0:
                        half = e // R + 1 if isinstance(e, int) else None
                        if half is not None:
                            pe.wait_ge(w1_loaded[j], 16 * half)
                            pe.wait_ge(w2_loaded[j], 16 * half)
                        else:
                            pe.wait_ge(w1_loaded[j], (e - j) * 8 + 16)
                            pe.wait_ge(w2_loaded[j], (e - j) * 8 + 16)
                    for ic in range(IC):
                        reached(pe, b_ready, u * IC + ic - IC + 1)
                        reached(pe, a_ready, u * IC + ic - IC + 1)
                        for h in range(2):
                            for c in range(KC):
                                m = nc.tensor.matmul(up_ps[ic][h][:], w1[j][:, c, ic, h],
                                                     tT[:, c * B * P + tt * NT:c * B * P + (tt + 1) * NT],
                                                     start=(c == 0), stop=(c == KC - 1))
                            m.then_inc(up_made, 1)
                if live(e, tt, 1):
                    i = j if tt else 1 - j
                    v = (tt - 1) % 2
                    pe.wait_ge(act_ready, u * IC)
                    reached(pe, y_added, u - 2)
                    for n in range(TB):
                        for c in range(IC):
                            m = nc.tensor.matmul(y_ps[v][n // 2][:, n % 2], act_[v][:, c, n * P:(n + 1) * P], w2[i][:, c],
                                                 start=(c == 0), stop=(c == IC - 1))
                    m.then_inc(down_done, 1)

            pe.wait_ge(w_loaded, 80)
            prologue(pe, work)
            pe.wait_ge(t_kept, B)
            pe.wait_ge(b2_added, B)
            experts(pe, unit)

        @block.vector
        def _(dve):
            def work(r, j):
                if exists(r):
                    reached(dve, t_turned, r - 1)
                    nc.vector.tensor_scalar(tin[j][:], X[:, bass.ds(r * D, D)], scale[:, bass.ds(r, 1)], None,
                                            ALU.mult).then_inc(tin_ready, 1)
                if exists(r - 3):
                    dve.wait_ge(b2_made, r - 2)
                    row = X[:, bass.ds((r - 3) * D, D)]
                    nc.vector.scalar_tensor_tensor(row, row, 2.0, b_ps[:, 0:D], ALU.mult,
                                                   ALU.add).then_inc(b2_added, 1)
                if exists(r - 2):
                    dve.wait_ge(e_ready, r - 1)
                    nc.vector.tensor_tensor(kept[:], expd[j][:], chosen[j][:], ALU.mult).then_inc(kept_ready, 1)
                    dve.wait_ge(kept_ready, r - 1)
                    nc.vector.tensor_reduce(total[:], kept[:], AX.X, ALU.add).then_inc(total_ready, 1)
                    dve.wait_ge(total_ready, r - 1)
                    nc.vector.reciprocal(inverse[:], total[:]).then_inc(inv_ready, 1)
                    dve.wait_ge(inv_ready, r - 1)
                    reached(dve, g_turned, r - 3)
                    reached(dve, g_kept, r - 3)
                    nc.vector.tensor_scalar(gates1[j][:], kept[:], inverse[:], None, ALU.mult).then_inc(g_ready, 1)
                if exists(r - 1):
                    i = 1 - j
                    dve.wait_ge(l_made, r)
                    reached(dve, e_ready, r - 2)
                    nc.vector.tensor_tensor(logits[i][:, 0:E], l_ps[:, 0:E], b_gate[:], ALU.add).then_inc(l_ready, 1)
                    dve.wait_ge(l_ready, r)
                    nc.vector.memset(places[:], NEG)
                    nc.vector.max(best[:], logits[i][:]).then_inc(best_ready, 1)
                    dve.wait_ge(best_ready, r)
                    nc.vector.tensor_copy(places[:, 0:TOP], best[:, 0:TOP]).then_inc(list_ready, 1)
                    dve.wait_ge(list_ready, r)
                    nc.vector.tensor_scalar(negmax[i][:], best[:, 0:1], -1.0, None, ALU.mult)
                    nc.vector.match_replace(left[:], places[:], logits[i][:], NEG).then_inc(left_ready, 1)
                    dve.wait_ge(left_ready, r)
                    nc.vector.tensor_tensor(chosen[i][:], left[:, 0:E], logits[i][:, 0:E],
                                            ALU.not_equal).then_inc(chosen_ready, 1)

            def unit(e, tt, j):
                u = e * TT + tt
                if live(e, tt):
                    for ic in range(IC):
                        n = u * IC + ic
                        dve.wait_ge(up_made, 2 * n + 1)
                        reached(dve, ag_ready, n - 1)
                        nc.vector.tensor_scalar(a[ic][:], up_ps[ic][0][:], b1[:, bass.ds(e, 1), 0, ic],
                                                LIMIT, ALU.add, ALU.min).then_inc(a_ready, 1)
                        dve.wait_ge(up_made, 2 * n + 2)
                        reached(dve, act_ready, n - 1)
                        nc.vector.tensor_scalar(bb[ic][:], up_ps[ic][1][:], b1[:, bass.ds(e, 1), 1, ic],
                                                LIMIT + 1.0, ALU.add, ALU.min).then_inc(b_ready, 1)
                    dve.wait_ge(b_ready, (u + 1) * IC)
                    for ic in range(IC):
                        n = u * IC + ic
                        dve.wait_ge(ag_ready, n + 1)
                        reached(dve, down_done, u - 1)
                        nc.vector.scalar_tensor_tensor(act_[tt % 2][:, ic], bb[ic][:], 1.0 - LIMIT, ag[ic][:],
                                                       ALU.max, ALU.mult).then_inc(act_ready, 1)
                if live(e, tt, 1):
                    v = (tt - 1) % 2
                    dve.wait_ge(down_done, u)
                    for n in range(TB):
                        at = (tt - 1) % TT * TB + n
                        eb = e if tt else e - 1
                        row = X[:, at * D:(at + 1) * D]
                        m = nc.vector.scalar_tensor_tensor(row, y_ps[v][n // 2][:, n % 2],
                                                           gates[:, bass.ds(at * E + eb, 1)], row, ALU.mult, ALU.add)
                    m.then_inc(y_added, 1)

            for j in range(R):
                nc.vector.memset(logits[j][:], NEG)
            dve.wait_ge(rms_ready, 1)
            nc.vector.reciprocal(scale[:], rms[:]).then_inc(scale_ready, 1)
            dve.wait_ge(scale_ready, 1)
            dve.wait_ge(w_loaded, 80)
            nc.vector.tensor_scalar(b1[:, :, 1], b1[:, :, 1], 1.0, None, ALU.add).then_inc(filled, 1)
            dve.wait_ge(filled, 1)
            prologue(dve, work)
            dve.wait_ge(b2_added, B)
            dve.wait_ge(g_kept, B)
            experts(dve, unit)
            norm.all_rows(dve, y_added, U)
            norm.vector_part(dve)


def rotary_tables():
    f = np.float32
    inv = (f(1.0) / np.power(f(10000.0), np.arange(0, HD, 2, dtype=f) / f(HD))).astype(f)
    ang = np.arange(P, dtype=f)[:, None] * inv[None, :]
    c, s = np.cos(ang).astype(f), np.sin(ang).astype(f)
    return np.concatenate([c, c], -1), np.concatenate([-s, s], -1)


def band_mask(window):
    i, j = np.arange(P)[:, None], np.arange(P)[None, :]
    return np.where((j <= i) & (j > i - window), 0.0, NEG).astype(np.float32)


def by_feature(w, name):
    if name in "vo":
        return w
    return w.reshape(H, P // H, -1).transpose(1, 0, 2).reshape(w.shape)


def lay_out(t):
    c = np.ascontiguousarray
    t = {k: np.asarray(v) for k, v in t.items()}
    cos, sin = rotary_tables()
    up = [w for w in t["L0_ffn_w13"]]
    g, u = np.split(t["L0_ffn_shared_gate_up_w"], 2)
    for at in range(0, len(g), 256):
        up += [g[at:at + 256], u[at:at + 256]]
    down = np.concatenate([t["L0_ffn_w2"].transpose(0, 2, 1).reshape(-1, D), t["L0_ffn_shared_down_w"].T])
    return {
        "x": c(t["x"].transpose(1, 0, 2)),
        "ident": np.eye(P, dtype=np.float32),
        "cos": cos, "sin": sin, "mask": band_mask(WINDOW),
        "wqkv": c(t["L0_attn_w_qkv"].reshape(3, G, GW, KC, P).transpose(4, 3, 1, 0, 2)),
        "ctx": c(t["ctx_2048"].transpose(1, 0, 2)).reshape(P, B * D),
        "xw": c(np.stack([by_feature(t[f"L0_xattn_W{n}"], n).T for n in "qkvo"], 1)),
        "xbias": c(np.stack([by_feature(t[f"L0_xattn_b{n}"], n) for n in "qkvo"], 1)),
        "causal": band_mask(P),
        "m_norm": c(t["L1_ffn_norm_w"].reshape(KC, P).T),
        "m_gate": c(t["L1_ffn_gate_w"].T.reshape(KC, P, 16).transpose(1, 0, 2)),
        "m_bgate": t["L1_ffn_gate_b"],
        "m_b2": t["L1_ffn_b2"],
        "m_b1": c(t["L1_ffn_b1"].reshape(16, KC, P, 2).transpose(2, 0, 3, 1)),
        "m_w1": c(t["L1_ffn_w1"].reshape(16, KC, P, 2, KC, P).transpose(0, 5, 4, 1, 3, 2)).reshape(16, P, -1),
        "m_w2": c(t["L1_ffn_w2"].reshape(16, D, KC, P).transpose(0, 3, 2, 1)).reshape(16, P, -1),
        "w_wu": c(np.stack([t["L1_xattn_w"], t["L1_xattn_u"]]).reshape(2, KC, P).transpose(2, 0, 1)),
        "r_rank": c(np.stack([t["L1_attn_Ws"], t["L1_attn_Wa"]], 1).reshape(KC, P, 2, 32).transpose(1, 0, 2, 3)),
        "r_wo": c(t["L1_attn_Wo"].T.reshape(KC, P, D).transpose(1, 0, 2)),
        "r_bo": t["L1_attn_bo"],
        "f_router": c(np.concatenate([t["L0_ffn_gate_w"], t["L0_ffn_shared_gate_w"]]).reshape(9, KC, P).transpose(2, 1, 0)),
        "f_up": c(np.concatenate(up, 0).reshape(-1, KC, P).transpose(2, 1, 0)),
        "f_down": c(np.concatenate([down, np.zeros((-len(down) % P, D), np.float32)]).reshape(-1, P, D).transpose(1, 0, 2)),
        "wo": c(t["L0_attn_w_o"].reshape(D, H, P).transpose(2, 1, 0)),
    }


def program(nc, A, out, stages="ABCDEF"):
    with ExitStack() as outer:
        banks = [outer.enter_context(nc.psum_tensor(f"bank{n}", [P, 512], F32)) for n in range(8)]
        room = Room(nc, outer, "all", banks)
        X = room.sb("X", [P, B * D])
        ident = room.sb("ident", [P, P])
        eps = room.sb("eps", [P, 1])
        start, made, stored = room.sems("start made stored")
        with nc.Block() as block:

            @block.sync
            def _(sp):
                sp.dma_start(ident[:], A["ident"]).then_inc(start, 16)
                sp.wait_ge(start, 16)

            @block.vector
            def _(dve):
                nc.vector.memset(eps[:], EPS).then_inc(made, 1)
                dve.wait_ge(made, 1)

        if stages[0] != "A":
            with nc.Block() as block:

                @block.sync
                def _(sp):
                    sp.dma_start(X[:].rearrange("p (b d) -> p b d", b=B), A["x"]).then_inc(start, 16)
                    sp.wait_ge(start, 32)
        for letter, stage in (("A", self_attention), ("B", cross_attention), ("C", ffn),
                              ("D", low_rank_attention), ("E", wkv), ("F", mixture)):
            if letter in stages:
                with ExitStack() as stack:
                    own = Room(nc, stack, letter, banks)
                    stage(nc, own, A, X, ident, eps)
                    own.close()
        with nc.Block() as block:

            @block.sync
            def _(sp):
                sp.dma_start(out.rearrange("b t d -> t b d"), X[:].rearrange("p (b d) -> p b d", b=B)).then_inc(stored, 16)
                sp.wait_ge(stored, 16)


def kernel(**inputs):
    import concourse.bacc as bacc
    from concourse.bass_utils import run_bass_kernel_spmd

    arrays = lay_out(inputs)
    nc = bacc.Bacc("TRN2", target_bir_lowering=False, num_devices=1)
    A = {n: nc.dram_tensor(f"in_{n}", a.shape, mybir.dt.from_np(a.dtype), kind="ExternalInput").ap()
         for n, a in arrays.items()}
    out = nc.dram_tensor("out", (B, P, D), F32, kind="ExternalOutput").ap()
    program(nc, A, out)
    r = run_bass_kernel_spmd(nc, [{f"in_{n}": a for n, a in arrays.items()}], core_ids=[0])
    return r.results[0]["out"]
```

```python
from contextlib import ExitStack

import concourse.bass as bass
import numpy as np
from concourse import mybir

F32 = mybir.dt.float32
BF16 = mybir.dt.bfloat16
ALU = mybir.AluOpType
ACT = mybir.ActivationFunctionType
AX = mybir.AxisListType

P = 128
B = 16
D = 256
KC = D // P
H = 16
HD = 128
G = 4
HG = H // G
GW = HG * HD
WINDOW = 64
NEG = -3.0e38
EPS = 1e-5


def reached(eng, sem, count):
    if not isinstance(count, int) or count > 0:
        eng.wait_ge(sem, count)


class Room:

    def __init__(self, nc, stack, prefix, banks):
        self.nc, self.stack, self.prefix, self.banks = nc, stack, prefix, list(banks)
        self.taken = []

    def sb(self, name, shape, dt=F32):
        return self.stack.enter_context(self.nc.sbuf_tensor(f"{self.prefix}_{name}", shape, dt))

    def ps(self, shape):
        bank = self.banks.pop(0)[:]
        return bank if len(shape) == 2 else bank.rearrange("p (a b) -> p a b", a=shape[1])

    def sem(self, name):
        self.taken.append(self.nc.alloc_semaphore(name=f"{self.prefix}_{name}"))
        return self.taken[-1]

    def sems(self, names):
        return [self.sem(n) for n in names.split()]

    def close(self):
        with self.nc.Block() as block:

            @block.gpsimd
            def _(pool):
                self.nc.clear_and_free_semaphores(self.taken)


class RowNorm:

    def __init__(self, nc, room, X, eps):
        self.nc, self.X, self.eps, self.in_loop = nc, X, eps, True
        self.row = room.sb("row", [P, D])
        self.moments = room.sb("moments", [P, 6])
        self.all_moments = room.sb("all_moments", [P, B, 6])
        self.stats = room.sb("stats", [P, B, 2])
        self.root = room.sb("root", [P, B])
        self.rstd = room.sb("rstd", [P, B])
        self.row_ready, self.kept, self.bn_ready, self.moments_ready = room.sems(
            "row_ready row_kept bn_ready moments_ready")
        self.stats_ready, self.root_ready, self.rstd_ready, self.normed = room.sems(
            "stats_ready root_ready rstd_ready normed")

    def put(self, dve, b):
        nc = self.nc
        dve.wait_ge(self.row_ready, b + 1)
        nc.vector.tensor_scalar(self.X[:, bass.ds(b * D, D)], self.row[:], 0.0, None,
                                ALU.add).then_inc(self.kept, 1)
        nc.vector.bn_stats(self.moments[:], self.row[:]).then_inc(self.bn_ready, 1)
        dve.wait_ge(self.bn_ready, b + 1)
        nc.vector.tensor_scalar(self.all_moments[:, bass.ds(b, 1), :].rearrange("p b s -> p (b s)"),
                                self.moments[:], 0.0, None, ALU.add).then_inc(self.moments_ready, 1)

    def all_rows(self, dve, added, count):
        dve.wait_ge(added, count)
        for b in range(B):
            m = self.nc.vector.bn_stats(self.all_moments[:, b], self.X[:, b * D:(b + 1) * D])
            m.then_inc(self.moments_ready, 1)
        self.in_loop = False

    def scalar_part(self, act):
        act.wait_ge(self.stats_ready, B)
        self.nc.scalar.activation(self.root[:], self.stats[:, :, 1], ACT.Sqrt,
                                  bias=self.eps[:]).then_inc(self.root_ready, 1)

    def vector_part(self, dve):
        nc = self.nc
        dve.wait_ge(self.moments_ready, B)
        for b in range(B):
            nc.vector.bn_aggr(self.stats[:, b], self.all_moments[:, b]).then_inc(self.stats_ready, 1)
        dve.wait_ge(self.root_ready, 1)
        nc.vector.reciprocal(self.rstd[:], self.root[:]).then_inc(self.rstd_ready, 1)
        dve.wait_ge(self.rstd_ready, 1)
        if self.in_loop:
            dve.wait_ge(self.kept, B)
        for b in range(B):
            row = self.X[:, b * D:(b + 1) * D]
            nc.vector.tensor_scalar(row, row, self.stats[:, b, 0:1], self.rstd[:, b:b + 1],
                                    ALU.subtract, ALU.mult).then_inc(self.normed, 1)


def self_attention(nc, room, A, X, ident, eps, ctx, ctx_loaded):
    wqkv = room.sb("wqkv", [P, KC, G, 3, GW])
    wo = room.sb("wo", [P, H, D])
    cos = room.sb("cos", [P, HD])
    sin = room.sb("sin", [P, HD])
    mask = room.sb("mask", [P, P])
    xin = room.sb("xin", [P, D])
    xT = room.sb("xT", [P, KC, P])
    t1 = room.sb("t1", [P, 2, GW])
    t2 = room.sb("t2", [P, 2, GW])
    qk = room.sb("qk", [P, 2, GW])
    qkT = room.sb("qkT", [P, 2, GW])
    v = room.sb("v", [P, G, GW])
    s = room.sb("s", [P, HG, P])
    p = room.sb("p", [P, HG, P])
    negmax = room.sb("negmax", [P, HG])
    total = room.sb("total", [P, HG])
    inverse = room.sb("inverse", [P, HG])
    pT = room.sb("pT", [P, HG, P])
    oT = room.sb("oT", [P, HG, P])
    norm = RowNorm(nc, room, X, eps)
    qkv_ps = [room.ps([P, GW]) for n in ("q_ps", "k_ps", "v_ps")]
    turn_ps = room.ps([P, GW])
    y_ps = room.ps([P, GW])
    s_ps = room.ps([P, HG, P])
    pT_ps = room.ps([P, HG, P])
    o_ps = room.ps([P, HG, P])

    x_loaded, table_loaded, wo_loaded = room.sems("x_loaded table_loaded wo_loaded")
    w_loaded = [room.sem(f"w_loaded{g}") for g in range(G)]
    xin_ready, xT_done, xT_copied = room.sems("xin_ready xT_done xT_copied")
    made = room.sems("q_made k_made v_made")
    taken = room.sems("q_taken k_taken v_taken")
    rotated = room.sems("q_rotated k_rotated")
    turned = room.sems("q_turned k_turned")
    copied = room.sems("qT_copied kT_copied")
    s_made, s_taken, s_max, max_ready, e_ready = room.sems("s_made s_taken s_max max_ready e_ready")
    inv_ready, p_ready, pT_made, pT_copied = room.sems("inv_ready p_ready pT_made pT_copied")
    o_made, oT_copied, wo_done = room.sems("o_made oT_copied wo_done")
    SCALE = float(1.0 / np.sqrt(HD))
    U = B * G

    def sequences(eng, unit, tail):
        for g in range(G):
            unit(0, g)
        with eng.Fori(1, B - 1) as b:
            for g in range(G):
                unit(b, g)
        for n in range(G + tail):
            unit(B - 1 + n // G, n % G)

    def live(b, g, back=0):
        return not isinstance(b, int) or 0 <= b * G + g - back < B * G

    def has_next(b):
        return not isinstance(b, int) or b + 1 < B

    with nc.Block() as block:

        @block.sync
        def _(sp):
            sp.dma_start(X[:, 0:D], A["x"][:, 0, :]).then_inc(x_loaded, 16)
            for g in range(G):
                for c in range(KC):
                    sp.dma_start(wqkv[:, c, g], A["wqkv"][:, c, g]).then_inc(w_loaded[g], 16)
            sp.dma_start(wo[:], A["wo"]).then_inc(wo_loaded, 16)

        @block.gpsimd
        def _(pool):
            def unit(b, g):
                u = b * G + g
                for i in range(2):
                    pool.wait_ge(taken[i], u + 1)
                    reached(pool, turned[i], u)
                    nc.gpsimd.tensor_tensor(qk[:, i], t1[:, i], t2[:, i],
                                            ALU.add).then_inc(rotated[i], 1)
                if g == 0 and has_next(b):
                    pool.wait_ge(xT_done, b + 1)
                    nc.gpsimd.tensor_copy(xin[:], X[:, bass.ds((b + 1) * D, D)]).then_inc(xin_ready, 1)

            pool.wait_ge(x_loaded, 16)
            nc.gpsimd.tensor_copy(xin[:], X[:, 0:D]).then_inc(xin_ready, 1)
            pool.wait_ge(table_loaded, 64)
            sequences(pool, unit, 0)

        @block.scalar
        def _(act):
            act.dma_start(cos[:], A["cos"]).then_inc(table_loaded, 16)
            act.dma_start(sin[:], A["sin"]).then_inc(table_loaded, 16)
            act.dma_start(mask[:], A["mask"]).then_inc(table_loaded, 16)
            act.dma_start(X[:, D:B * D].rearrange("p (b d) -> p b d", b=B - 1),
                          A["x"][:, 1:B, :]).then_inc(table_loaded, 16)
            act.dma_start(ctx[:], A["ctx"]).then_inc(ctx_loaded, 16)

            def copy_xT(b):
                act.wait_ge(xT_done, b + 1)
                nc.scalar.copy(xT[:].rearrange("p c t -> p (c t)"), turn_ps[:, 0:D]).then_inc(xT_copied, 1)

            def unit(b, g):
                u = b * G + g
                if live(b, g, 1):
                    for i in range(2):
                        act.wait_ge(turned[i], u)
                        reached(act, s_made, u - 1)
                        nc.scalar.copy(qkT[:, i], turn_ps[:]).then_inc(copied[i], 1)
                if live(b, g, 2):
                    act.wait_ge(pT_made, u - 1)
                    reached(act, o_made, u - 2)
                    nc.scalar.copy(pT[:], pT_ps[:]).then_inc(pT_copied, 1)
                if live(b, g):
                    act.wait_ge(made[2], u + 1)
                    reached(act, o_made, u - 3)
                    nc.scalar.copy(v[:, g], qkv_ps[2][:]).then_inc(taken[2], 1)
                    if g == G - 1 and has_next(b):
                        copy_xT(b + 1)
                if live(b, g, 1):
                    act.wait_ge(max_ready, u)
                    reached(act, pT_made, u - 1)
                    for h in range(HG):
                        e = nc.scalar.activation(p[:, h], s[:, h], ACT.Exp, bias=negmax[:, h:h + 1],
                                                 accum_out=total[:, h:h + 1])
                    e.then_inc(e_ready, 1)
                if live(b, g, 2):
                    act.wait_ge(o_made, u - 1)
                    reached(act, wo_done, u - 2)
                    nc.scalar.copy(oT[:], o_ps[:]).then_inc(oT_copied, 1)

            copy_xT(0)
            sequences(act, unit, 2)
            norm.scalar_part(act)

        @block.tensor
        def _(pe):
            def turn(i, b, g):
                u = b * G + g
                pe.wait_ge(rotated[i], u)
                if i == 0:
                    reached(pe, copied[1], u - 1)
                    if g == 0 and has_next(b - 1 if isinstance(b, int) else b):
                        pe.wait_ge(xT_copied, b + 1)
                else:
                    pe.wait_ge(copied[0], u)
                for h in range(HG):
                    m = nc.tensor.transpose(turn_ps[:, h * HD:(h + 1) * HD],
                                            qk[:, i, h * HD:(h + 1) * HD], ident[:])
                m.then_inc(turned[i], 1)

            def project(i, b, g):
                u = b * G + g
                reached(pe, taken[i], u)
                if i == 0:
                    if g == 0:
                        pe.wait_ge(xT_copied, b + 1)
                    if isinstance(b, int) and b == 0:
                        pe.wait_ge(w_loaded[g], 16 * KC)
                for c in range(KC):
                    m = nc.tensor.matmul(qkv_ps[i][:], xT[:, c], wqkv[:, c, g, i],
                                         start=(c == 0), stop=(c == KC - 1))
                m.then_inc(made[i], 1)

            def turn_x(b):
                pe.wait_ge(xin_ready, b + 1)
                for c in range(KC):
                    m = nc.tensor.transpose(turn_ps[:, c * P:(c + 1) * P], xin[:, c * P:(c + 1) * P], ident[:])
                m.then_inc(xT_done, 1)

            def project_heads(b, g):
                u, gh = b * G + g, (g - 3) % G
                pe.wait_ge(oT_copied, u - 2)
                if isinstance(b, int) and u == 3:
                    pe.wait_ge(wo_loaded, 16)
                if gh == 0:
                    reached(pe, norm.row_ready, (b if g == 3 else b - 1))
                for h in range(HG):
                    m = nc.tensor.matmul(y_ps[:, 0:D], oT[:, h], wo[:, gh * HG + h],
                                         start=(gh == 0 and h == 0), stop=(gh == G - 1 and h == HG - 1))
                m.then_inc(wo_done, 1)

            def unit(b, g):
                u = b * G + g
                if live(b, g, 1):
                    turn(0, b, g)
                if live(b, g):
                    project(0, b, g)
                if live(b, g, 3):
                    project_heads(b, g)
                if live(b, g, 1):
                    turn(1, b, g)
                if live(b, g):
                    project(1, b, g)
                if live(b, g, 2):
                    pe.wait_ge(p_ready, u - 1)
                    reached(pe, pT_copied, u - 2)
                    for h in range(HG):
                        m = nc.tensor.transpose(pT_ps[:, h], p[:, h], ident[:])
                    m.then_inc(pT_made, 1)
                if live(b, g):
                    project(2, b, g)
                    if g == G - 1 and has_next(b):
                        pe.wait_ge(copied[1], u)
                        turn_x(b + 1)
                if live(b, g, 1):
                    pe.wait_ge(copied[1], u)
                    reached(pe, s_taken, u - 1)
                    for h in range(HG):
                        m = nc.tensor.matmul(s_ps[:, h], qkT[:, 0, h * HD:(h + 1) * HD],
                                             qkT[:, 1, h * HD:(h + 1) * HD], start=True, stop=True)
                    m.then_inc(s_made, 1)
                if live(b, g, 2):
                    pe.wait_ge(pT_copied, u - 1)
                    reached(pe, oT_copied, u - 2)
                    for h in range(HG):
                        m = nc.tensor.matmul(o_ps[:, h], v[:, (g - 2) % G, h * HD:(h + 1) * HD],
                                             pT[:, h], start=True, stop=True)
                    m.then_inc(o_made, 1)

            turn_x(0)
            sequences(pe, unit, 3)

        @block.vector
        def _(dve):
            half = HD // 2

            def rotate(i, b, g):
                u = b * G + g
                src = qkv_ps[i][:].rearrange("p (h e) -> p h e", h=HG)
                a = t1[:, i].rearrange("p (h e) -> p h e", h=HG)
                c = t2[:, i].rearrange("p (h e) -> p h e", h=HG)
                dve.wait_ge(made[i], u + 1)
                reached(dve, rotated[i], u)
                nc.vector.tensor_tensor(a, src, cos[:, None, :].to_broadcast([P, HG, HD]), ALU.mult)
                nc.vector.tensor_tensor(c[:, :, 0:half], src[:, :, half:HD],
                                        sin[:, None, 0:half].to_broadcast([P, HG, half]), ALU.mult)
                nc.vector.tensor_tensor(c[:, :, half:HD], src[:, :, 0:half],
                                        sin[:, None, half:HD].to_broadcast([P, HG, half]),
                                        ALU.mult).then_inc(taken[i], 1)

            def unit(b, g):
                u = b * G + g
                if live(b, g, 2):
                    dve.wait_ge(e_ready, u - 1)
                    nc.vector.reciprocal(inverse[:], total[:]).then_inc(inv_ready, 1)
                    dve.wait_ge(inv_ready, u - 1)
                    nc.vector.tensor_tensor(p[:], p[:], inverse[:, :, None].to_broadcast([P, HG, P]),
                                            ALU.mult).then_inc(p_ready, 1)
                if live(b, g):
                    rotate(0, b, g)
                    rotate(1, b, g)
                if g == 2 and live(b, g, 6):
                    dve.wait_ge(wo_done, b * G)
                    nc.vector.tensor_tensor(norm.row[:], X[:, bass.ds((b - 1) * D, D)], y_ps[:, 0:D],
                                            ALU.add).then_inc(norm.row_ready, 1)
                    norm.put(dve, b - 1)
                if live(b, g, 1):
                    dve.wait_ge(s_made, u)
                    reached(dve, e_ready, u - 1)
                    nc.vector.scalar_tensor_tensor(s[:], s_ps[:], SCALE,
                                                   mask[:, None, :].to_broadcast([P, HG, P]),
                                                   ALU.mult, ALU.add).then_inc(s_taken, 1)
                    dve.wait_ge(s_taken, u)
                    nc.vector.tensor_reduce(negmax[:], s[:], AX.X, ALU.max, negate=True).then_inc(max_ready, 1)

            dve.wait_ge(table_loaded, 64)
            sequences(dve, unit, 3)
            norm.vector_part(dve)


def cross_attention(nc, room, A, X, ident, eps, ctx, ctx_loaded):
    FD = 8
    RUNS = ((0, 3, 0), (3, 2, 1), (5, 1, 2))
    SHIFT = FD * 6
    NPAR = 2
    VW = 32
    SCALE = float(1.0 / np.sqrt(P))
    N_STACK = 2 * len(RUNS)
    R = 4
    spread = nc.dram_tensor("spread", [R, 6, P, D], BF16, kind="Internal").ap()

    w = room.sb("w", [P, 4, P])
    bias = room.sb("bias", [P, 4])
    bq = room.sb("bq", [P, 1])
    full = room.sb("full", [P, 2, D])
    rest = room.sb("rest", [P, 2, D])
    part = room.sb("part", [P, 3, 2, D], BF16)
    cin = [room.sb(f"cin{j}", [P, D]) for j in range(2)]
    QS = [room.sb(f"QS{j}", [P, H, D], BF16) for j in range(R)]
    KS = [room.sb(f"KS{j}", [P, H, D], BF16) for j in range(R)]
    zero = room.sb("zero", [NPAR, H * D], BF16)
    V = [room.sb(f"V{j}", [P, KC, H, VW]) for j in range(R)]
    negmax = room.sb("negmax", [P, KC, H])
    high = room.sb("high", [P, KC, H], BF16)
    pair = room.sb("pair", [P, KC, NPAR, H])
    shift = room.sb("shift", [NPAR * H, D], BF16)
    pr = [room.sb(f"pr{j}", [P, KC, D]) for j in range(2)]
    oT = room.sb("oT", [P, 4, D])
    inverse = room.sb("inverse", [P, KC, H])
    o = room.sb("o", [P, KC, H, FD])
    onT = room.sb("onT", [P, D])
    norm = RowNorm(nc, room, X, eps)
    a_ps = room.ps([P, KC, D])
    b_ps = room.ps([P, KC, D])
    m_ps = [room.ps([P, KC, D]) for j in range(2)]
    s_ps = [room.ps([P, KC, D]) for j in range(2)]
    o_ps = [room.ps([P, KC, D]) for j in range(2)]

    cin_ready = room.sem("cin_ready")
    w_loaded, zero_ready, v_cleared, parts_out, zeroed, stacked, shifted = room.sems(
        "w_loaded zero_ready v_cleared parts_out zeroed stacked shifted")
    cleared = [room.sem(f"cleared{j}") for j in range(R)]
    qk_made, qk_taken, v_made, v_ready = room.sems("qk_made qk_taken v_made v_ready")
    bq_ready, part0, part1, part2, rest0 = room.sems("bq_ready part0 part1 part2 rest0")
    m_made, max_ready = room.sems("m_made max_ready")
    high_ready, pair_ready, pair_turned, shift_ready = room.sems("high_ready pair_ready pair_turned shift_ready")
    s_made, p_ready, pv_done = room.sems("s_made p_ready pv_done")
    oT_copied, nat_made, inv_ready, o_ready = room.sems("oT_copied nat_made inv_ready o_ready")
    onT_made, onT_copied, y_made = room.sems("onT_made onT_copied y_made")

    def rounds(eng, work):
        for r in range(R - 1):
            work(r, r)
        with eng.Fori(R - 1, B - R, R) as r:
            for n in range(R):
                work(r + n, (R - 1 + n) % R)
        for r in range(B - 1, B + 3):
            work(r, r % R)

    def exists(b):
        return not isinstance(b, int) or 0 <= b < B

    with nc.Block() as block:

        @block.sync
        def _(sp):
            def stack(b, j):
                sp.wait_ge(part2, b + 1)
                sp.dma_start(spread[j].rearrange("n p s -> p n s"),
                             part[:].rearrange("p k i s -> p (k i) s")).then_inc(parts_out, 16)
                reached(sp, s_made, (b - 3) * H)
                if isinstance(b, int) and b < R:
                    sp.wait_ge(cleared[b], 1)
                sp.dma_start(QS[j][SHIFT:SHIFT + NPAR].rearrange("n h s -> n (h s)"), zero[:]).then_inc(zeroed, 16)
                sp.wait_ge(parts_out, 16 * (b + 1))
                src = spread[j].rearrange("(k i) (d h) s -> k i d (h s)", i=2, d=FD)
                for n, m, k in RUNS:
                    rows = slice(n * FD, (n + m) * FD)
                    sp.dma_start(KS[j][rows].rearrange("r h s -> r (h s)"), src[0:m, 1]).then_inc(stacked, 16)
                    sp.dma_start(QS[j][rows].rearrange("r h s -> r (h s)"),
                                 src[k:k + 1, 0].to_broadcast([m, FD, H * D])).then_inc(stacked, 16)

            def work(r, j):
                if exists(r - 1):
                    sp.wait_ge(shift_ready, r)
                    for n in range(NPAR):
                        sp.dma_start(QS[(j - 1) % R][SHIFT + n:SHIFT + n + 1],
                                     shift[n * H:(n + 1) * H]).then_inc(shifted, 16)
                if exists(r + 1):
                    stack(r + 1, (j + 1) % R)

            sp.dma_start(w[:], A["xw"]).then_inc(w_loaded, 16)
            sp.dma_start(bias[:], A["xbias"]).then_inc(w_loaded, 16)
            sp.wait_ge(zero_ready, 1)
            stack(0, 0)
            rounds(sp, work)

        @block.gpsimd
        def _(pool):
            nc.gpsimd.memset(zero[:], 0.0).then_inc(zero_ready, 1)

            def split(b):
                pool.wait_ge(part0, b + 1)
                nc.gpsimd.tensor_tensor(rest[:], full[:], part[:, 0], ALU.subtract).then_inc(rest0, 1)
                pool.wait_ge(part1, b + 1)
                nc.gpsimd.tensor_tensor(part[:, 2], rest[:], part[:, 1], ALU.subtract).then_inc(part2, 1)

            def work(r, j):
                if isinstance(r, int) and r < R - 1:
                    for n in (0, 1) if r == 0 else (r + 1,):
                        nc.gpsimd.memset(V[n][:, :, :, FD + 1:VW], 0.0)
                        nc.gpsimd.memset(V[n][:, :, :, FD:FD + 1], 1.0).then_inc(v_cleared, 1)
                if exists(r):
                    reached(pool, v_made, r - 1)
                    nc.gpsimd.tensor_copy(cin[j % 2][:], ctx[:, bass.ds(r * D, D)]).then_inc(cin_ready, 1)
                if exists(r + 1):
                    split(r + 1)

            split(0)
            pool.wait_ge(ctx_loaded, 16)
            rounds(pool, work)

        @block.scalar
        def _(act):
            def take_qk(b):
                act.wait_ge(qk_made, b + 1)
                reached(act, part2, b)
                nc.scalar.activation(full[:, 0], a_ps[:, 0], ACT.Identity, bias=bq[:], scale=SCALE)
                nc.scalar.activation(full[:, 1], a_ps[:, 1], ACT.Identity,
                                     bias=bias[:, 1:2]).then_inc(qk_taken, 1)
                act.wait_ge(qk_taken, b + 1)
                reached(act, parts_out, b * 16)
                nc.scalar.copy(part[:, 0], full[:]).then_inc(part0, 1)

            def second_part(b):
                act.wait_ge(rest0, b + 1)
                nc.scalar.copy(part[:, 1], rest[:]).then_inc(part1, 1)

            def work(r, j):
                for h in range(H):
                    if exists(r - 2):
                        act.wait_ge(s_made, (r - 2) * H + h + 1)
                        reached(act, pv_done, (r - 2) * H + h - 1)
                        nc.scalar.activation(pr[h % 2][:], s_ps[h % 2][:], ACT.Exp).then_inc(p_ready, 1)
                    if h == 1 and exists(r - 3):
                        act.wait_ge(pv_done, H * (r - 2))
                        nc.scalar.copy(oT[:, 2:4], o_ps[1][:]).then_inc(oT_copied, 1)
                    if h == 1 and exists(r + 1):
                        take_qk(r + 1)
                    if h == 3 and exists(r + 1):
                        second_part(r + 1)
                    if h == 5 and exists(r - 1):
                        act.wait_ge(pair_turned, r)
                        reached(act, shifted, 32 * (r - 1))
                        nc.scalar.copy(shift[:], a_ps[0:NPAR * H, 1]).then_inc(shift_ready, 1)
                    if h == 8 and exists(r - 3):
                        act.wait_ge(onT_made, r - 2)
                        nc.scalar.activation(onT[:], a_ps[:, 0], ACT.Identity,
                                             bias=bias[:, 2:3]).then_inc(onT_copied, 1)
                    if h == 9 and exists(r - 2):
                        act.wait_ge(pv_done, H * (r - 2) + H // 2)
                        nc.scalar.copy(oT[:, 0:2], o_ps[0][:]).then_inc(oT_copied, 1)
                    if h == 13 and exists(r):
                        act.wait_ge(v_made, r + 1)
                        if isinstance(r, int) and r < R - 1:
                            act.wait_ge(v_cleared, r + 2)
                        nc.scalar.copy(V[j][:, :, :, 0:FD],
                                       b_ps[:].rearrange("p c (o e) -> p c o e", o=2)[:, :, 0].rearrange(
                                           "p c (h e) -> p c h e", h=H)).then_inc(v_ready, 1)

            act.wait_ge(w_loaded, 32)
            nc.scalar.mul(bq[:], bias[:, 0:1], SCALE).then_inc(bq_ready, 1)
            act.wait_ge(bq_ready, 1)
            take_qk(0)
            second_part(0)
            rounds(act, work)
            norm.scalar_part(act)

        @block.tensor
        def _(pe):
            def project_qk(b):
                nc.tensor.matmul(a_ps[:, 0], w[:, 0], X[:, bass.ds(b * D, D)], start=True, stop=True)
                nc.tensor.matmul(a_ps[:, 1], w[:, 1], ctx[:, bass.ds(b * D, D)], start=True,
                                 stop=True).then_inc(qk_made, 1)

            def attend(r, i, h):
                if h == 0:
                    pe.wait_ge(v_ready, r - 1)
                if h % (H // 2) == 0:
                    half = 2 * h // H
                    reached(pe, oT_copied, 2 * (r - 3) + 1 + half)
                pe.wait_ge(p_ready, (r - 2) * H + h + 1)
                q = h % 4 * VW
                for c in range(KC):
                    m = nc.tensor.matmul(o_ps[h // 8][q:q + VW, h // 4 % 2], V[i][:, c, h], pr[h % 2][:, c],
                                         start=(c == 0), stop=(c == KC - 1))
                m.then_inc(pv_done, 1)

            def work(r, j):
                i = (j - 2) % R
                for h in range(H):
                    if exists(r - 2):
                        if h == 0:
                            pe.wait_ge(shifted, 32 * (r - 1))
                        reached(pe, p_ready, (r - 2) * H + h - 1)
                        for c in range(KC):
                            m = nc.tensor.matmul(s_ps[h % 2][:, c], KS[i][:, h, c * P:(c + 1) * P],
                                                 QS[i][:, h], start=True, stop=True)
                        m.then_inc(s_made, 1)
                    if exists(r):
                        if h == 0:
                            pe.wait_ge(zeroed, 16 * (r + 1))
                            pe.wait_ge(stacked, 16 * N_STACK * (r + 1))
                        reached(pe, max_ready, r * H + h - 1)
                        for c in range(KC):
                            m = nc.tensor.matmul(m_ps[h % 2][:, c], QS[j][:, h, c * P:(c + 1) * P],
                                                 KS[j][:, h], start=True, stop=True)
                        m.then_inc(m_made, 1)
                    if h == 0 and exists(r + 1):
                        reached(pe, onT_copied, r - 3)
                        reached(pe, shift_ready, r - 1)
                        project_qk(r + 1)
                    if h == 3 and exists(r - 3):
                        pe.wait_ge(oT_copied, 2 * (r - 2))
                        if exists(r + 1):
                            pe.wait_ge(qk_taken, r + 2)
                        elif r > B:
                            pe.wait_ge(onT_copied, r - 3)
                            pe.wait_ge(norm.row_ready, r - 3)
                        if exists(r - 1):
                            pe.wait_ge(v_ready, r)
                        for c, to in enumerate((a_ps, b_ps)):
                            for k in range(4):
                                m = nc.tensor.transpose(to[:].rearrange("p c s -> p (c s)")[:, k * P:(k + 1) * P],
                                                        oT[:, k, c * P:(c + 1) * P], ident[:])
                        m.then_inc(nat_made, 1)
                    if h == 5 and exists(r - 1):
                        pe.wait_ge(pair_ready, r)
                        if exists(r - 3):
                            pe.wait_ge(o_ready, r - 2)
                        else:
                            pe.wait_ge(qk_taken, r + 2)
                        for c in range(KC):
                            m = nc.tensor.transpose(a_ps[0:NPAR * H, 1, c * P:(c + 1) * P],
                                                    pair[:, c].rearrange("p n h -> p (n h)"), ident[:])
                        m.then_inc(pair_turned, 1)
                    if h == 7 and exists(r - 3):
                        pe.wait_ge(o_ready, r - 2)
                        if exists(r - 1):
                            pe.wait_ge(shift_ready, r)
                        for c in range(KC):
                            m = nc.tensor.transpose(a_ps[:, 0, c * P:(c + 1) * P],
                                                    o[:, c].rearrange("p h d -> p (h d)"), ident[:])
                        m.then_inc(onT_made, 1)
                    if h == 9 and exists(r - 3):
                        pe.wait_ge(onT_copied, r - 2)
                        nc.tensor.matmul(b_ps[:, 0], w[:, 3], onT[:], start=True, stop=True).then_inc(y_made, 1)
                    if h == 12 and exists(r):
                        reached(pe, norm.row_ready, r - 2)
                        pe.wait_ge(cin_ready, r + 1)
                        for c in range(KC):
                            m = nc.tensor.matmul(b_ps[:, c, 0:P], cin[j % 2][:, c * P:(c + 1) * P], w[:, 2],
                                                 start=True, stop=True)
                        m.then_inc(v_made, 1)
                    if exists(r - 2):
                        if h >= 1:
                            attend(r, i, h - 1)
                        if h == H - 1:
                            attend(r, i, h)

            pe.wait_ge(w_loaded, 32)
            pe.wait_ge(ctx_loaded, 16)
            project_qk(0)
            rounds(pe, work)

        @block.vector
        def _(dve):
            def natural(r, j):
                dve.wait_ge(nat_made, r - 2)
                s4 = [src[:].rearrange("p c s -> p (c s)").rearrange("p (h e) -> p h e", h=H) for src in (a_ps, b_ps)]
                for c in range(KC):
                    nc.vector.reciprocal(inverse[:, c], s4[c][:, :, FD]).then_inc(inv_ready, 1)
                for c in range(KC):
                    dve.wait_ge(inv_ready, 2 * (r - 2) - 1 + c)
                    m = nc.vector.tensor_tensor(o[:, c], s4[c][:, :, 0:FD],
                                                inverse[:, c, :, None].to_broadcast([P, H, FD]), ALU.mult)
                m.then_inc(o_ready, 1)

            def work(r, j):
                for g in range(H):
                    if exists(r):
                        dve.wait_ge(m_made, r * H + g + 1)
                        if g == 0:
                            reached(dve, pair_ready, r)
                        nc.vector.tensor_reduce(negmax[:, :, g], m_ps[g % 2][:], AX.X, ALU.max,
                                                negate=True).then_inc(max_ready, 1)
                    if g == 3 and exists(r - 3):
                        natural(r, j)
                    if g == 10 and exists(r - 3):
                        dve.wait_ge(y_made, r - 2)
                        nc.vector.scalar_tensor_tensor(norm.row[:], b_ps[:, 0], bias[:, 3:4],
                                                       X[:, bass.ds((r - 3) * D, D)], ALU.add,
                                                       ALU.add).then_inc(norm.row_ready, 1)
                        norm.put(dve, r - 3)
                    if isinstance(r, int) and r == 0 and g in (0, 5, 10):
                        clear(g // 5 + 1)
                if exists(r):
                    dve.wait_ge(max_ready, (r + 1) * H)
                    reached(dve, pair_turned, r)
                    nc.vector.tensor_copy(high[:], negmax[:]).then_inc(high_ready, 1)
                    dve.wait_ge(high_ready, r + 1)
                    nc.vector.tensor_copy(pair[:, :, 0], high[:])
                    nc.vector.tensor_tensor(pair[:, :, 1], negmax[:], high[:],
                                            ALU.subtract).then_inc(pair_ready, 1)

            def clear(n):
                nc.vector.memset(QS[n][:].rearrange("p h s -> p (h s)").bitcast(F32), 0.0)
                nc.vector.memset(KS[n][:], 1.0).then_inc(cleared[n], 1)

            clear(0)
            dve.wait_ge(w_loaded, 32)
            rounds(dve, work)
            norm.vector_part(dve)


def ffn(nc, room, A, X, ident, eps):
    E, W, SW = 8, 176, 704
    GROUPS = [(e * W, W, e) for e in range(E)] + [(E * W + at, min(256, SW - at), E) for at in range(0, SW, 256)]
    NG = len(GROUPS)
    LAST = [max(p for p in range(-NG, k) if p % NG % 3 == k % 3) + 1 for k in range(NG)]
    INNER = E * W + SW
    CHUNKS = list(range(0, INNER, P))
    BUNDLES = [list(range(n, min(n + 4, len(CHUNKS)))) for n in range(0, len(CHUNKS), 4)]
    NB = len(BUNDLES)
    TOP = 2
    PAD = E + 8 - TOP
    R = 2

    w_up = room.sb("w_up", [P, KC, 2 * INNER])
    w_down = room.sb("w_down", [P, len(CHUNKS), D])
    w_router = room.sb("w_router", [P, KC, E + 1])
    xin = room.sb("xin", [P, D])
    xT = [room.sb(f"xT{j}", [P, KC, P]) for j in range(R)]
    th = [room.sb(f"th{j}", [P, 256]) for j in range(3)]
    gate = [room.sb(f"gate{j}", [P, 256]) for j in range(2)]
    hid = room.sb("hid", [P, len(CHUNKS) * P])
    hT = [room.sb(f"hT{j}", [P, 4, P]) for j in range(2)]
    logits = room.sb("logits", [P, E + 1])
    negmax = room.sb("negmax", [P, 1])
    total = room.sb("total", [P, 1])
    inverse = room.sb("inverse", [P, 1])
    expd = room.sb("expd", [P, E + 1])
    probs = room.sb("probs", [P, PAD])
    best = room.sb("best", [P, 8])
    places = room.sb("places", [P, 8])
    left = room.sb("left", [P, PAD])
    weight = room.sb("weight", [P, E + 1])
    norm = RowNorm(nc, room, X, eps)
    up_ps = [room.ps([P, 512]) for j in range(3)]
    hT_ps = [room.ps([P, 4, P]) for j in range(2)]
    y_ps = room.ps([P, 512])
    x_ps = room.ps([P, KC, D])
    r_ps = room.ps([P, 512])

    w_loaded, down_loaded, ready = room.sems("w_loaded down_loaded ready")
    up_loaded = [room.sem(f"up_loaded{k}") for k in range(NG)]
    xin_ready, x_turned, xT_copied = room.sems("xin_ready x_turned xT_copied")
    up_made, th_ready, gate_ready, h_ready = room.sems("up_made th_ready gate_ready h_ready")
    hT_made, hT_copied, down_done = room.sems("hT_made hT_copied down_done")
    r_made, r_taken, r_max, e_ready, r_inv, p_ready = room.sems("r_made r_taken r_max e_ready r_inv p_ready")
    best_ready, list_ready, left_ready, weight_ready = room.sems("best_ready list_ready left_ready weight_ready")

    def rounds(eng, work):
        for r in range(R):
            work(r, r)
        with eng.Fori(R, B - R - 1, R) as r:
            for j in range(R):
                work(r + j, j)
        for r in range(B - R, B + 1):
            work(r, r % R)

    def exists(b):
        return not isinstance(b, int) or 0 <= b < B

    with nc.Block() as block:

        @block.sync
        def _(sp):
            sp.dma_start(w_router[:], A["f_router"]).then_inc(w_loaded, 16)
            for k, (at, n, e) in enumerate(GROUPS):
                cols = slice(2 * at, 2 * (at + n))
                sp.dma_start(w_up[:, :, cols], A["f_up"][:, :, cols]).then_inc(up_loaded[k], 16)
            sp.dma_start(w_down[:], A["f_down"]).then_inc(down_loaded, 16)
            sp.wait_ge(down_loaded, 16)

        @block.gpsimd
        def _(pool):
            def copy(b):
                reached(pool, x_turned, b)
                nc.gpsimd.tensor_copy(xin[:], X[:, bass.ds(b * D, D)]).then_inc(xin_ready, 1)

            def work(r, j):
                if exists(r + 1):
                    copy(r + 1)

            copy(0)
            rounds(pool, work)

        @block.scalar
        def _(act):
            def copy_xT(b, j):
                act.wait_ge(x_turned, b + 1)
                nc.scalar.copy(xT[j][:], x_ps[:, 0].rearrange("p (c t) -> p c t", c=KC)).then_inc(xT_copied, 1)

            def router_exp(b):
                act.wait_ge(r_max, b + 1)
                nc.scalar.activation(expd[:, 0:E], logits[:, 0:E], ACT.Exp, bias=negmax[:], accum_out=total[:])
                nc.scalar.activation(expd[:, E:E + 1], logits[:, E:E + 1], ACT.Tanh, scale=0.5).then_inc(e_ready, 1)

            def work(r, j):
                for k in range(NG):
                    n = GROUPS[k][1]
                    if exists(r):
                        act.wait_ge(up_made, r * NG + k + 1)
                        reached(act, gate_ready, r * NG + LAST[k])
                        nc.scalar.activation(th[k % 3][:, 0:n], up_ps[k % 3][:, 0:n],
                                             ACT.Tanh, scale=0.5).then_inc(th_ready, 1)
                    if k < NB and exists(r - 1):
                        act.wait_ge(hT_made, (r - 1) * NB + k + 1)
                        reached(act, down_done, (r - 1) * NB + k - 1)
                        m = 4 if k < NB - 1 else 1
                        nc.scalar.copy(hT[k % 2][:, 0:m], hT_ps[k % 2][:, 0:m]).then_inc(hT_copied, 1)
                    if k == 7 and exists(r + 1):
                        copy_xT(r + 1, 1 - j)
                if exists(r + 1):
                    router_exp(r + 1)

            copy_xT(0, 0)
            router_exp(0)
            rounds(act, work)
            norm.scalar_part(act)

        @block.tensor
        def _(pe):
            def turn_x(b):
                pe.wait_ge(xin_ready, b + 1)
                for c in range(KC):
                    m = nc.tensor.transpose(x_ps[:, 0, c * P:(c + 1) * P], xin[:, c * P:(c + 1) * P], ident[:])
                m.then_inc(x_turned, 1)

            def router(b, j):
                pe.wait_ge(xT_copied, b + 1)
                for c in range(KC):
                    m = nc.tensor.matmul(r_ps[:, 0:E + 1], xT[j][:, c], w_router[:, c],
                                         start=(c == 0), stop=(c == KC - 1))
                m.then_inc(r_made, 1)

            def down(b, k):
                pe.wait_ge(hT_copied, b * NB + k + 1)
                if k == 0:
                    reached(pe, norm.row_ready, b)
                for n, c in enumerate(BUNDLES[k]):
                    m = nc.tensor.matmul(y_ps[:, 0:D], hT[k % 2][:, n], w_down[:, c],
                                         start=(c == 0), stop=(c == len(CHUNKS) - 1))
                m.then_inc(down_done, 1)

            def work(r, j):
                for k in range(NG):
                    if k < NB and exists(r - 1):
                        if k == 0:
                            pe.wait_ge(h_ready, r * NG)
                        reached(pe, hT_copied, (r - 1) * NB + k - 1)
                        for n, c in enumerate(BUNDLES[k]):
                            at = CHUNKS[c]
                            m = nc.tensor.transpose(hT_ps[k % 2][:, n], hid[:, at:at + P], ident[:])
                        m.then_inc(hT_made, 1)
                    if exists(r):
                        at, n, e = GROUPS[k]
                        reached(pe, h_ready, r * NG + LAST[k])
                        if isinstance(r, int) and r == 0:
                            pe.wait_ge(up_loaded[k], 16)
                        for c in range(KC):
                            m = nc.tensor.matmul(up_ps[k % 3][:, 0:2 * n], xT[j][:, c],
                                                 w_up[:, c, 2 * at:2 * (at + n)],
                                                 start=(c == 0), stop=(c == KC - 1))
                        m.then_inc(up_made, 1)
                    if 1 <= k <= NB and exists(r - 1):
                        down(r - 1, k - 1)
                    if k == 6 and exists(r + 1):
                        turn_x(r + 1)
                    if k == NG - 1 and isinstance(r, int) and r == 0:
                        pe.wait_ge(down_loaded, 16)
                    if k == 8 and exists(r + 1):
                        pe.wait_ge(r_taken, r + 1)
                        router(r + 1, 1 - j)

            turn_x(0)
            pe.wait_ge(w_loaded, 16)
            router(0, 0)
            rounds(pe, work)

        @block.vector
        def _(dve):
            def route(b):
                dve.wait_ge(r_made, b + 1)
                nc.vector.tensor_copy(logits[:], r_ps[:, 0:E + 1]).then_inc(r_taken, 1)
                dve.wait_ge(r_taken, b + 1)
                nc.vector.tensor_reduce(negmax[:], logits[:, 0:E], AX.X, ALU.max, negate=True).then_inc(r_max, 1)
                dve.wait_ge(e_ready, b + 1)
                nc.vector.reciprocal(inverse[:], total[:]).then_inc(r_inv, 1)
                dve.wait_ge(r_inv, b + 1)
                nc.vector.tensor_scalar(probs[:, 0:E], expd[:, 0:E], inverse[:], None, ALU.mult).then_inc(p_ready, 1)
                dve.wait_ge(p_ready, b + 1)
                nc.vector.memset(places[:], -1.0)
                nc.vector.max(best[:], probs[:]).then_inc(best_ready, 1)
                dve.wait_ge(best_ready, b + 1)
                nc.vector.tensor_copy(places[:, 0:TOP], best[:, 0:TOP]).then_inc(list_ready, 1)
                dve.wait_ge(list_ready, b + 1)
                nc.vector.tensor_scalar(expd[:, E:E + 1], expd[:, E:E + 1], 1.0, 0.25, ALU.add, ALU.mult)
                nc.vector.match_replace(left[:], places[:], probs[:], -2.0).then_inc(left_ready, 1)
                dve.wait_ge(left_ready, b + 1)
                nc.vector.tensor_scalar(left[:, 0:E], left[:, 0:E], -2.0, 0.5, ALU.is_equal,
                                        ALU.mult).then_inc(weight_ready, 1)
                dve.wait_ge(weight_ready, 3 * b + 1)
                nc.vector.tensor_tensor(weight[:, 0:E], left[:, 0:E], probs[:, 0:E], ALU.mult).then_inc(weight_ready, 1)
                nc.vector.tensor_copy(weight[:, E:E + 1], expd[:, E:E + 1]).then_inc(weight_ready, 1)
                dve.wait_ge(weight_ready, 3 * b + 3)

            def work(r, j):
                for k in range(NG):
                    if exists(r):
                        at, n, e = GROUPS[k]
                        dve.wait_ge(th_ready, r * NG + k + 1)
                        nc.vector.scalar_tensor_tensor(gate[k % 2][:, 0:n], th[k % 3][:, 0:n], 1.0,
                                                       up_ps[k % 3][:, 0:n], ALU.add, ALU.mult).then_inc(gate_ready, 1)
                        dve.wait_ge(gate_ready, r * NG + k + 1)
                        if exists(r - 1):
                            dve.wait_ge(hT_made, (r - 1) * NB + 1 + (at + n - 1) // (4 * P))
                        nc.vector.scalar_tensor_tensor(hid[:, at:at + n], gate[k % 2][:, 0:n], weight[:, e:e + 1],
                                                       up_ps[k % 3][:, n:2 * n], ALU.mult, ALU.mult).then_inc(h_ready, 1)
                    if k == 8 and exists(r - 1):
                        dve.wait_ge(down_done, r * NB)
                        nc.vector.tensor_tensor(norm.row[:], X[:, bass.ds((r - 1) * D, D)], y_ps[:, 0:D],
                                                ALU.add).then_inc(norm.row_ready, 1)
                        norm.put(dve, r - 1)
                if exists(r + 1):
                    route(r + 1)

            nc.vector.memset(hid[:, INNER:], 0.0)
            nc.vector.memset(probs[:], -1.0).then_inc(ready, 1)
            dve.wait_ge(ready, 1)
            route(0)
            rounds(dve, work)
            norm.vector_part(dve)


def low_rank_attention(nc, room, A, X, ident, eps):
    RANK = 32
    SCALE = float(1.0 / np.sqrt(np.float32(RANK)))
    R = 4

    w_rank = room.sb("w_rank", [P, KC, 2, RANK])
    wo = room.sb("wo", [P, KC, D])
    bo = room.sb("bo", [P, D])
    mask = room.sb("mask", [P, P])
    xin = [room.sb(f"xin{j}", [P, D]) for j in range(R)]
    xT = [room.sb(f"xT{j}", [P, KC, P]) for j in range(2)]
    sa = [room.sb(f"sa{j}", [RANK, 2, P]) for j in range(2)]
    sc = [room.sb(f"sc{j}", [P, P]) for j in range(2)]
    p = [room.sb(f"p{j}", [P, P]) for j in range(2)]
    negmax = [room.sb(f"negmax{j}", [P, 1]) for j in range(2)]
    total = [room.sb(f"total{j}", [P, 1]) for j in range(2)]
    inverse = room.sb("inverse", [P, 1])
    pT = [room.sb(f"pT{j}", [P, P]) for j in range(2)]
    oT = [room.sb(f"oT{j}", [P, KC, P]) for j in range(2)]
    xb = [room.sb(f"xb{j}", [P, D]) for j in range(R)]
    norm = RowNorm(nc, room, X, eps)
    x_ps = room.ps([P, 512])
    sa_ps = room.ps([P, 512])
    s_ps = room.ps([P, 512])
    pT_ps = room.ps([P, 512])
    o_ps = room.ps([P, 512])
    y_ps = room.ps([P, 512])

    w_loaded, = room.sems("w_loaded")
    xin_ready, x_turned, xT_copied, sa_made, sa_copied = room.sems(
        "xin_ready x_turned xT_copied sa_made sa_copied")
    s_made, s_taken, max_ready, e_ready, inv_ready, p_ready = room.sems(
        "s_made s_taken max_ready e_ready inv_ready p_ready")
    pT_made, pT_copied, o_made, oT_copied, y_made, xb_ready = room.sems(
        "pT_made pT_copied o_made oT_copied y_made xb_ready")

    def rounds(eng, work, last):
        n = 2 * R
        for r in range(n):
            work(r, r % R)
        with eng.Fori(n, B - R + 1, R) as r:
            for j in range(R):
                work(r + j, j)
        for r in range(B, B + last):
            work(r, r % R)

    def exists(b):
        return not isinstance(b, int) or 0 <= b < B

    with nc.Block() as block:

        @block.sync
        def _(sp):
            sp.dma_start(w_rank[:], A["r_rank"]).then_inc(w_loaded, 16)
            sp.dma_start(wo[:], A["r_wo"]).then_inc(w_loaded, 16)
            sp.dma_start(bo[:], A["r_bo"].partition_broadcast(P)).then_inc(w_loaded, 16)
            sp.dma_start(mask[:], A["causal"]).then_inc(w_loaded, 16)
            sp.wait_ge(w_loaded, 64)

        @block.gpsimd
        def _(pool):
            def work(r, j):
                if exists(r):
                    reached(pool, norm.row_ready, r - 5)
                    reached(pool, o_made, r - R + 1)
                    nc.gpsimd.tensor_copy(xin[j][:], X[:, bass.ds(r * D, D)]).then_inc(xin_ready, 1)
                if exists(r - 2):
                    if not exists(r):
                        pool.wait_ge(norm.row_ready, r - 5)
                    nc.gpsimd.tensor_tensor(xb[(j - 2) % R][:], X[:, bass.ds((r - 2) * D, D)], bo[:],
                                            ALU.add).then_inc(xb_ready, 1)

            pool.wait_ge(w_loaded, 64)
            rounds(pool, work, 2)

        @block.scalar
        def _(act):
            def work(r, j):
                i, k = j % 2, (j - 1) % 2
                if exists(r - 1):
                    act.wait_ge(sa_made, r)
                    reached(act, s_made, r - 2)
                    nc.scalar.copy(sa[k][:], sa_ps[0:RANK, 0:2 * P].rearrange("p (c t) -> p c t", c=2)).then_inc(sa_copied, 1)
                if exists(r - 3):
                    act.wait_ge(o_made, r - 2)
                    reached(act, y_made, r - 4)
                    nc.scalar.copy(oT[k][:], o_ps[:, 0:D].rearrange("p (c t) -> p c t", c=KC)).then_inc(oT_copied, 1)
                if exists(r):
                    act.wait_ge(x_turned, r + 1)
                    reached(act, sa_made, r - 1)
                    nc.scalar.copy(xT[i][:], x_ps[:, 0:D].rearrange("p (c t) -> p c t", c=KC)).then_inc(xT_copied, 1)
                if exists(r - 2):
                    act.wait_ge(pT_made, r - 1)
                    reached(act, o_made, r - 3)
                    nc.scalar.copy(pT[i][:], pT_ps[:, 0:P]).then_inc(pT_copied, 1)
                if exists(r - 1):
                    act.wait_ge(max_ready, r)
                    reached(act, pT_made, r - 2)
                    nc.scalar.activation(p[k][:], sc[k][:], ACT.Exp, bias=negmax[k][:],
                                         accum_out=total[k][:]).then_inc(e_ready, 1)

            rounds(act, work, 3)
            norm.scalar_part(act)

        @block.tensor
        def _(pe):
            def work(r, j):
                i, k = j % 2, (j - 1) % 2
                if exists(r):
                    pe.wait_ge(xin_ready, r + 1)
                    reached(pe, xT_copied, r)
                    for c in range(KC):
                        m = nc.tensor.transpose(x_ps[:, c * P:(c + 1) * P], xin[j][:, c * P:(c + 1) * P], ident[:])
                    m.then_inc(x_turned, 1)
                if exists(r - 1):
                    pe.wait_ge(sa_copied, r)
                    reached(pe, s_taken, r - 1)
                    nc.tensor.matmul(s_ps[:, 0:P], sa[k][:, 0], sa[k][:, 1], start=True, stop=True).then_inc(s_made, 1)
                if exists(r - 2):
                    pe.wait_ge(p_ready, r - 1)
                    reached(pe, pT_copied, r - 2)
                    nc.tensor.transpose(pT_ps[:, 0:P], p[i][:], ident[:]).then_inc(pT_made, 1)
                if exists(r - 3):
                    pe.wait_ge(oT_copied, r - 2)
                    reached(pe, norm.row_ready, r - 3)
                    for c in range(KC):
                        m = nc.tensor.matmul(y_ps[:, 0:D], oT[k][:, c], wo[:, c],
                                             start=(c == 0), stop=(c == KC - 1))
                    m.then_inc(y_made, 1)
                if exists(r - 2):
                    pe.wait_ge(pT_copied, r - 1)
                    reached(pe, oT_copied, r - 2)
                    for c in range(KC):
                        m = nc.tensor.matmul(o_ps[:, c * P:(c + 1) * P], xin[(j - 2) % R][:, c * P:(c + 1) * P],
                                             pT[i][:], start=True, stop=True)
                    m.then_inc(o_made, 1)
                if exists(r):
                    pe.wait_ge(xT_copied, r + 1)
                    reached(pe, sa_copied, r)
                    for n in range(2):
                        for c in range(KC):
                            m = nc.tensor.matmul(sa_ps[0:RANK, n * P:(n + 1) * P], w_rank[:, c, n], xT[i][:, c],
                                                 start=(c == 0), stop=(c == KC - 1))
                    m.then_inc(sa_made, 1)

            pe.wait_ge(w_loaded, 64)
            rounds(pe, work, 3)

        @block.vector
        def _(dve):
            def work(r, j):
                k = (j - 1) % 2
                if exists(r - 1):
                    dve.wait_ge(s_made, r)
                    reached(dve, e_ready, r - 2)
                    nc.vector.scalar_tensor_tensor(sc[k][:], s_ps[:, 0:P], SCALE, mask[:], ALU.mult,
                                                   ALU.add).then_inc(s_taken, 1)
                    dve.wait_ge(s_taken, r)
                    nc.vector.tensor_reduce(negmax[k][:], sc[k][:], AX.X, ALU.max, negate=True).then_inc(max_ready, 1)
                if exists(r - 3):
                    dve.wait_ge(y_made, r - 2)
                    dve.wait_ge(xb_ready, r - 2)
                    nc.vector.tensor_tensor(norm.row[:], xb[(j - 3) % R][:], y_ps[:, 0:D], ALU.add).then_inc(norm.row_ready, 1)
                    norm.put(dve, r - 3)
                if exists(r - 1):
                    dve.wait_ge(e_ready, r)
                    nc.vector.reciprocal(inverse[:], total[k][:]).then_inc(inv_ready, 1)
                    dve.wait_ge(inv_ready, r)
                    nc.vector.tensor_scalar(p[k][:], p[k][:], inverse[:], None, ALU.mult).then_inc(p_ready, 1)

            dve.wait_ge(w_loaded, 64)
            rounds(dve, work, 3)
            norm.vector_part(dve)


def wkv(nc, room, A, X, ident, eps):
    BG = 4
    NG = B // BG
    T1 = P + 1
    LOW = -1.0e38
    U = NG * KC
    OLD, NEW, CARRY, ENTER = range(4)

    wu = room.sb("wu", [P, 2, KC])
    zeros = room.sb("zeros", [P, BG, T1])
    decay = [room.sb(f"decay{c}", [P, BG, T1]) for c in range(KC)]
    xin = [room.sb(f"xin{j}", [P, BG, P]) for j in range(2)]
    vin = [room.sb(f"vin{j}", [P, BG, P]) for j in range(2)]
    k = [room.sb(f"k{j}", [P, BG, T1]) for j in range(2)]
    v = [room.sb(f"v{j}", [P, BG, P]) for j in range(2)]
    o = [room.sb(f"o{j}", [P, BG, T1]) for j in range(2)]
    no = room.sb("no", [P, BG, P])
    arg = [room.sb(f"arg{j}", [P, 4, BG, P]) for j in range(2)]
    ex = [room.sb(f"ex{j}", [P, 4, BG, T1]) for j in range(2)]
    ev = room.sb("ev", [P, BG, T1])
    ps = room.sb("ps", [P, BG, T1])
    qs = room.sb("qs", [P, BG, T1])
    enter = room.sb("enter", [P, BG, P])
    old = room.sb("old", [P, BG, P])
    num = room.sb("num", [P, BG, P])
    den1 = room.sb("den1", [P, BG, P])
    den = room.sb("den", [P, BG, P])
    inv = room.sb("inv", [P, BG, P])
    y = [room.sb(f"y{j}", [P, BG, P]) for j in range(2)]
    norm = RowNorm(nc, room, X, eps)
    k_ps = [room.ps([P, BG, P]) for j in range(2)]
    v_ps = [room.ps([P, BG, P]) for j in range(2)]
    y_ps = [room.ps([P, BG, P]) for j in range(2)]

    w_loaded, cleared, ready = room.sems("w_loaded cleared ready")
    v_loaded = room.sems("v_loaded0 v_loaded1")
    xin_ready, turned, kv_copied = room.sems("xin_ready turned kv_copied")
    o_ready, no_ready, arg_dve, arg_pool, ex_ready = room.sems("o_ready no_ready arg_dve arg_pool ex_ready")
    ev_ready, p_ready, q_ready, enter_ready, old_ready = room.sems("ev_ready p_ready q_ready enter_ready old_ready")
    num_ready, den1_ready, den_ready, inv_ready, y_ready = room.sems("num_ready den1_ready den_ready inv_ready y_ready")
    y_turned, added = room.sems("y_turned added")

    def rounds(eng, work):
        for r in range(4):
            work(r, r % 2, r // 2)
        with eng.Fori(2, NG) as g:
            for c in range(2):
                work(g * 2 + c, c, g)
        for r in range(U, U + 3):
            work(r, r % 2, r // 2)

    def exists(u):
        return not isinstance(u, int) or 0 <= u < U

    def part(t, g, c):
        return t[:, bass.ds(g * (BG * D), BG * D)].rearrange("p (b d) -> p b d", b=BG)[:, :, c * P:(c + 1) * P]

    def flat(t):
        return t[:].rearrange("p b t -> p (b t)")

    with nc.Block() as block:

        @block.sync
        def _(sp):
            def work(r, c, g):
                if exists(r):
                    reached(sp, turned, r - 1)
                    sp.dma_start(vin[c][:], part(A["ctx"], g, c)).then_inc(v_loaded[c], 16)

            sp.dma_start(wu[:], A["w_wu"]).then_inc(w_loaded, 16)
            rounds(sp, work)
            for c in range(KC):
                sp.wait_ge(v_loaded[c], 16 * NG)

        @block.gpsimd
        def _(pool):
            def work(r, c, g):
                if exists(r):
                    reached(pool, turned, r - 1)
                    nc.gpsimd.tensor_copy(xin[c][:], part(X, g, c)).then_inc(xin_ready, 1)
                i = 1 - c
                if exists(r - 1):
                    pool.wait_ge(ex_ready, r)
                    reached(pool, p_ready, r - 1)
                    nc.gpsimd.tensor_tensor(ev[:, :, 1:], ex[i][:, ENTER, :, 1:], v[i][:], ALU.mult).then_inc(ev_ready, 1)
                    reached(pool, num_ready, r - 1)
                    nc.gpsimd.tensor_tensor(enter[:], ex[i][:, NEW, :, 1:], v[i][:], ALU.mult).then_inc(enter_ready, 1)
                    pool.wait_ge(q_ready, r)
                    nc.gpsimd.tensor_tensor(den1[:], ex[i][:, OLD, :, 1:], qs[:, :, 0:P], ALU.mult).then_inc(den1_ready, 1)
                    pool.wait_ge(den1_ready, r)
                    reached(pool, inv_ready, r - 1)
                    nc.gpsimd.tensor_tensor(den[:], den1[:], ex[i][:, NEW, :, 1:], ALU.add).then_inc(den_ready, 1)
                if exists(r):
                    pool.wait_ge(o_ready, r + 1)
                    reached(pool, ex_ready, r - 1)
                    nc.gpsimd.tensor_tensor(arg[c][:, ENTER], k[c][:, :, 1:], o[c][:, :, 1:], ALU.subtract)
                    pool.wait_ge(no_ready, r + 1)
                    nc.gpsimd.tensor_tensor(arg[c][:, OLD], o[c][:, :, 0:P], no[:], ALU.subtract).then_inc(arg_pool, 1)

            nc.gpsimd.memset(zeros[:], 0.0)
            nc.gpsimd.memset(ev[:], 0.0)
            for j in range(2):
                nc.gpsimd.memset(k[j][:], LOW)
                m = nc.gpsimd.memset(ex[j][:], 0.0)
            m.then_inc(cleared, 1)
            pool.wait_ge(cleared, 1)
            rounds(pool, work)

        @block.scalar
        def _(act):
            def work(r, c, g):
                if exists(r):
                    act.wait_ge(turned, r + 1)
                    reached(act, den_ready, r - 1)
                    nc.scalar.copy(k[c][:, :, 1:], k_ps[c][:])
                    nc.scalar.copy(v[c][:], v_ps[c][:]).then_inc(kv_copied, 1)
                    act.wait_ge(arg_dve, r + 1)
                    act.wait_ge(arg_pool, r + 1)
                    reached(act, num_ready, r - 1)
                    nc.scalar.activation(ex[c][:, :, :, 1:].rearrange("p k b t -> p (k b) t"),
                                         arg[c][:].rearrange("p k b t -> p (k b) t"), ACT.Exp).then_inc(ex_ready, 1)

            act.wait_ge(cleared, 1)
            rounds(act, work)
            norm.scalar_part(act)

        @block.tensor
        def _(pe):
            def work(r, c, g):
                if exists(r):
                    pe.wait_ge(xin_ready, r + 1)
                    pe.wait_ge(v_loaded[c], 16 * (g + 1))
                    reached(pe, kv_copied, r - 1)
                    for n in range(BG):
                        nc.tensor.transpose(k_ps[c][:, n], xin[c][:, n], ident[:])
                        m = nc.tensor.transpose(v_ps[c][:, n], vin[c][:, n], ident[:])
                    m.then_inc(turned, 1)
                if exists(r - 2):
                    pe.wait_ge(y_ready, r - 1)
                    reached(pe, added, r - 3)
                    for n in range(BG):
                        m = nc.tensor.transpose(y_ps[c][:, n], y[c][:, n], ident[:])
                    m.then_inc(y_turned, 1)

            rounds(pe, work)

        @block.vector
        def _(dve):
            def work(r, c, g):
                if exists(r):
                    w, u = wu[:, 0, c:c + 1], wu[:, 1, c:c + 1]
                    dve.wait_ge(kv_copied, r + 1)
                    reached(dve, arg_pool, r - 1)
                    nc.vector.tensor_tensor_scan(flat(o[c]), flat(decay[c]), flat(k[c]), LOW, ALU.add,
                                                 ALU.max).then_inc(o_ready, 1)
                    dve.wait_ge(o_ready, r + 1)
                    reached(dve, arg_pool, r)
                    nc.vector.scalar_tensor_tensor(no[:], k[c][:, :, 1:], u, o[c][:, :, 0:P], ALU.add,
                                                   ALU.max).then_inc(no_ready, 1)
                    reached(dve, ex_ready, r - 1)
                    nc.vector.scalar_tensor_tensor(arg[c][:, CARRY], o[c][:, :, 0:P], w, o[c][:, :, 1:], ALU.add,
                                                   ALU.subtract)
                    dve.wait_ge(no_ready, r + 1)
                    nc.vector.scalar_tensor_tensor(arg[c][:, NEW], k[c][:, :, 1:], u, no[:], ALU.add,
                                                   ALU.subtract).then_inc(arg_dve, 1)
                i = 1 - c
                if exists(r - 1):
                    dve.wait_ge(ex_ready, r)
                    reached(dve, den1_ready, r - 1)
                    nc.vector.tensor_tensor_scan(flat(qs), ex[i][:, CARRY].rearrange("p b t -> p (b t)"),
                                                 ex[i][:, ENTER].rearrange("p b t -> p (b t)"), 0.0, ALU.mult,
                                                 ALU.add).then_inc(q_ready, 1)
                    dve.wait_ge(ev_ready, r)
                    nc.vector.tensor_tensor_scan(flat(ps), ex[i][:, CARRY].rearrange("p b t -> p (b t)"), flat(ev),
                                                 0.0, ALU.mult, ALU.add).then_inc(p_ready, 1)
                    dve.wait_ge(p_ready, r)
                    nc.vector.tensor_tensor(old[:], ex[i][:, OLD, :, 1:], ps[:, :, 0:P], ALU.mult).then_inc(old_ready, 1)
                    dve.wait_ge(old_ready, r)
                    dve.wait_ge(enter_ready, r)
                    nc.vector.tensor_tensor(num[:], old[:], enter[:], ALU.add).then_inc(num_ready, 1)
                    dve.wait_ge(den_ready, r)
                    nc.vector.reciprocal(inv[:], den[:]).then_inc(inv_ready, 1)
                    dve.wait_ge(inv_ready, r)
                    reached(dve, y_turned, r - 2)
                    nc.vector.tensor_tensor(y[i][:], num[:], inv[:], ALU.mult).then_inc(y_ready, 1)
                if exists(r - 2):
                    dve.wait_ge(y_turned, r - 1)
                    nc.vector.tensor_tensor(part(X, g - 1, c), part(X, g - 1, c), y_ps[c][:], ALU.add).then_inc(added, 1)

            dve.wait_ge(w_loaded, 16)
            dve.wait_ge(cleared, 1)
            for c in range(KC):
                nc.vector.memset(decay[c][:], LOW).then_inc(ready, 1)
                dve.wait_ge(ready, 2 * c + 1)
                nc.vector.tensor_scalar(decay[c][:, :, 1:], zeros[:, :, 1:], wu[:, 0, c:c + 1], None,
                                        ALU.add).then_inc(ready, 1)
            dve.wait_ge(ready, 2 * KC)
            rounds(dve, work)
            norm.all_rows(dve, added, U)
            norm.vector_part(dve)


def mixture(nc, room, A, X, ident, eps):
    E, I, TOP = 16, 256, 4
    IC = I // P
    LIMIT, ALPHA = 7.0, 1.702
    PAD = E + 8 - TOP
    NT = 512
    TT = B * P // NT
    TB = NT // P
    R = 2

    norm_w = room.sb("norm_w", [P, KC])
    w_gate = room.sb("w_gate", [P, KC, E])
    b_gate = room.sb("b_gate", [P, E])
    b2 = room.sb("b2", [E, D])
    b1 = room.sb("b1", [P, E, 2, IC])
    w1 = [room.sb(f"w1_{j}", [P, KC, IC, 2, P]) for j in range(R)]
    w2 = [room.sb(f"w2_{j}", [P, IC, D]) for j in range(R)]
    ss = room.sb("ss", [P, B])
    rms = room.sb("rms", [P, B])
    scale = room.sb("scale", [P, B])
    tin = [room.sb(f"tin{j}", [P, D]) for j in range(R)]
    tT1 = [room.sb(f"tT1_{j}", [P, KC, P]) for j in range(R)]
    tT = room.sb("tT", [P, KC * B * P])
    logits = [room.sb(f"logits{j}", [P, PAD]) for j in range(R)]
    best = room.sb("best", [P, 8])
    places = room.sb("places", [P, 8])
    left = room.sb("left", [P, PAD])
    negmax = [room.sb(f"negmax{j}", [P, 1]) for j in range(R)]
    chosen = [room.sb(f"chosen{j}", [P, E]) for j in range(R)]
    expd = [room.sb(f"expd{j}", [P, E]) for j in range(R)]
    kept = room.sb("kept", [P, E])
    total = room.sb("total", [P, 1])
    inverse = room.sb("inverse", [P, 1])
    gates1 = [room.sb(f"gates1_{j}", [P, E]) for j in range(R)]
    gates = room.sb("gates", [P, B * E])
    gT = [room.sb(f"gT{j}", [E, P]) for j in range(R)]
    a = [room.sb(f"a{j}", [P, NT]) for j in range(2)]
    sg = [room.sb(f"sg{j}", [P, NT]) for j in range(2)]
    ag = [room.sb(f"ag{j}", [P, NT]) for j in range(2)]
    bb = [room.sb(f"bb{j}", [P, NT]) for j in range(2)]
    act_ = [room.sb(f"act{j}", [P, IC, NT]) for j in range(2)]
    norm = RowNorm(nc, room, X, eps)
    up_ps = [[room.ps([P, NT]) for h in range(2)] for ic in range(IC)]
    y_ps = [[room.ps([P, 2, D]) for h in range(2)] for j in range(2)]
    x_ps, l_ps, g_ps, b_ps = up_ps[0][0], up_ps[0][1], up_ps[1][0], up_ps[1][1]

    w_loaded, filled, squared, rms_ready, scale_ready = room.sems("w_loaded filled squared rms_ready scale_ready")
    w1_loaded = room.sems("w1_loaded0 w1_loaded1")
    w2_loaded = room.sems("w2_loaded0 w2_loaded1")
    tin_ready, t_turned, t_copied, t_kept = room.sems("tin_ready t_turned t_copied t_kept")
    l_made, l_ready, best_ready, list_ready, left_ready = room.sems("l_made l_ready best_ready list_ready left_ready")
    nm_ready, chosen_ready, e_ready, kept_ready, total_ready, inv_ready, g_ready, g_kept = room.sems(
        "nm_ready chosen_ready e_ready kept_ready total_ready inv_ready g_ready g_kept")
    g_turned, g_copied, b2_made, b2_added = room.sems("g_turned g_copied b2_made b2_added")
    up_made, a_ready, b_ready, sg_ready, ag_ready, act_ready = room.sems(
        "up_made a_ready b_ready sg_ready ag_ready act_ready")
    down_done, y_added = room.sems("down_done y_added")

    def prologue(eng, work):
        for r in range(4):
            work(r, r % R)
        with eng.Fori(4, B - 1, R) as r:
            for j in range(R):
                work(r + j, j)
        for r in range(B, B + 4):
            work(r, r % R)

    def exists(b):
        return not isinstance(b, int) or 0 <= b < B

    U = E * TT

    def experts(eng, work):
        for e in range(R):
            for tt in range(TT):
                work(e, tt, e)
        with eng.Fori(R, E - 1, R) as e:
            for j in range(R):
                for tt in range(TT):
                    work(e + j, tt, j)
        work(E, 0, 0)

    def live(e, tt, back=0):
        return not isinstance(e, int) or 0 <= e * TT + tt - back < U

    with nc.Block() as block:

        @block.sync
        def _(sp):
            def load(e, j):
                sp.dma_start(w1[j][:].rearrange("p c i h n -> p (c i h n)"),
                             A["m_w1"][bass.ds(e, 1)].rearrange("o p n -> (o p) n")).then_inc(w1_loaded[j], 16)
                sp.dma_start(w2[j][:].rearrange("p c n -> p (c n)"),
                             A["m_w2"][bass.ds(e, 1)].rearrange("o p n -> (o p) n")).then_inc(w2_loaded[j], 16)

            for dst, name in ((norm_w, "m_norm"), (w_gate, "m_gate"), (b2, "m_b2"), (b1, "m_b1")):
                sp.dma_start(dst[:], A[name]).then_inc(w_loaded, 16)
            sp.dma_start(b_gate[:], A["m_bgate"].partition_broadcast(P)).then_inc(w_loaded, 16)
            for e in range(R):
                load(e, e)
            with sp.Fori(R, E - 1, R) as e:
                for j in range(R):
                    sp.wait_ge(down_done, (e + j - 1) * TT)
                    load(e + j, j)
            for j in range(R):
                sp.wait_ge(w1_loaded[j], 16 * E // R)
                sp.wait_ge(w2_loaded[j], 16 * E // R)

        @block.gpsimd
        def _(pool):
            def work(r, j):
                if exists(r - 1):
                    pool.wait_ge(t_copied, r)
                    for c in range(KC):
                        m = nc.gpsimd.tensor_copy(tT[:, bass.ds((r - 1) * P + c * B * P, P)], tT1[1 - j][:, c])
                    m.then_inc(t_kept, 1)
                if exists(r - 3):
                    pool.wait_ge(g_ready, r - 2)
                    nc.gpsimd.tensor_copy(gates[:, bass.ds((r - 3) * E, E)], gates1[1 - j][:]).then_inc(g_kept, 1)

            def unit(e, tt, j):
                if live(e, tt):
                    u = (e * TT + tt) * IC
                    for ic in range(IC):
                        pool.wait_ge(sg_ready, u + ic + 1)
                        reached(pool, act_ready, u + ic - 1)
                        nc.gpsimd.tensor_tensor(ag[ic][:], a[ic][:], sg[ic][:], ALU.mult).then_inc(ag_ready, 1)

            prologue(pool, work)
            experts(pool, unit)

        @block.scalar
        def _(act):
            def work(r, j):
                if exists(r - 1):
                    act.wait_ge(t_turned, r)
                    reached(act, t_kept, r - 2)
                    reached(act, l_made, r - 2)
                    for c in range(KC):
                        m = nc.scalar.mul(tT1[1 - j][:, c], x_ps[:, c * P:(c + 1) * P], norm_w[:, c:c + 1])
                    m.then_inc(t_copied, 1)
                if exists(r - 2):
                    act.wait_ge(chosen_ready, r - 1)
                    reached(act, kept_ready, r - 3)
                    nc.scalar.activation(expd[j][:], logits[j][:, 0:E], ACT.Exp, bias=negmax[j][:]).then_inc(e_ready, 1)
                if exists(r - 3):
                    act.wait_ge(g_turned, r - 2)
                    reached(act, b2_made, r - 4)
                    nc.scalar.copy(gT[1 - j][:], g_ps[0:E, 0:P]).then_inc(g_copied, 1)

            def unit(e, tt, j):
                if live(e, tt):
                    u = (e * TT + tt) * IC
                    for ic in range(IC):
                        act.wait_ge(a_ready, u + ic + 1)
                        reached(act, ag_ready, u + ic - 1)
                        nc.scalar.activation(sg[ic][:], a[ic][:], ACT.Sigmoid, scale=ALPHA).then_inc(sg_ready, 1)

            for b in range(B):
                m = nc.scalar.activation(tT[:, b * D:(b + 1) * D], X[:, b * D:(b + 1) * D], ACT.Square,
                                         accum_out=ss[:, b:b + 1])
            m.then_inc(squared, 1)
            act.wait_ge(squared, 1)
            nc.scalar.activation(rms[:], ss[:], ACT.Sqrt, scale=1.0 / D, bias=eps[:]).then_inc(rms_ready, 1)
            act.wait_ge(w_loaded, 80)
            prologue(act, work)
            experts(act, unit)
            norm.scalar_part(act)

        @block.tensor
        def _(pe):
            def work(r, j):
                if exists(r - 3):
                    pe.wait_ge(g_ready, r - 2)
                    reached(pe, g_copied, r - 3)
                    nc.tensor.transpose(g_ps[0:E, 0:P], gates1[1 - j][:], ident[:]).then_inc(g_turned, 1)
                if exists(r - 1):
                    pe.wait_ge(t_copied, r)
                    reached(pe, l_ready, r - 1)
                    for c in range(KC):
                        m = nc.tensor.matmul(l_ps[:, 0:E], tT1[1 - j][:, c], w_gate[:, c],
                                             start=(c == 0), stop=(c == KC - 1))
                    m.then_inc(l_made, 1)
                if exists(r):
                    pe.wait_ge(tin_ready, r + 1)
                    reached(pe, t_copied, r)
                    for c in range(KC):
                        m = nc.tensor.transpose(x_ps[:, c * P:(c + 1) * P], tin[j][:, c * P:(c + 1) * P], ident[:])
                    m.then_inc(t_turned, 1)
                if exists(r - 3):
                    pe.wait_ge(g_copied, r - 2)
                    reached(pe, b2_added, r - 3)
                    nc.tensor.matmul(b_ps[:, 0:D], gT[1 - j][:], b2[:], start=True, stop=True).then_inc(b2_made, 1)

            def unit(e, tt, j):
                u = e * TT + tt
                if live(e, tt):
                    if tt == 0:
                        half = e // R + 1 if isinstance(e, int) else None
                        if half is not None:
                            pe.wait_ge(w1_loaded[j], 16 * half)
                            pe.wait_ge(w2_loaded[j], 16 * half)
                        else:
                            pe.wait_ge(w1_loaded[j], (e - j) * 8 + 16)
                            pe.wait_ge(w2_loaded[j], (e - j) * 8 + 16)
                    for ic in range(IC):
                        reached(pe, b_ready, u * IC + ic - IC + 1)
                        reached(pe, a_ready, u * IC + ic - IC + 1)
                        for h in range(2):
                            for c in range(KC):
                                m = nc.tensor.matmul(up_ps[ic][h][:], w1[j][:, c, ic, h],
                                                     tT[:, c * B * P + tt * NT:c * B * P + (tt + 1) * NT],
                                                     start=(c == 0), stop=(c == KC - 1))
                            m.then_inc(up_made, 1)
                if live(e, tt, 1):
                    i = j if tt else 1 - j
                    v = (tt - 1) % 2
                    pe.wait_ge(act_ready, u * IC)
                    reached(pe, y_added, u - 2)
                    for n in range(TB):
                        for c in range(IC):
                            m = nc.tensor.matmul(y_ps[v][n // 2][:, n % 2], act_[v][:, c, n * P:(n + 1) * P], w2[i][:, c],
                                                 start=(c == 0), stop=(c == IC - 1))
                    m.then_inc(down_done, 1)

            pe.wait_ge(w_loaded, 80)
            prologue(pe, work)
            pe.wait_ge(t_kept, B)
            pe.wait_ge(b2_added, B)
            experts(pe, unit)

        @block.vector
        def _(dve):
            def work(r, j):
                if exists(r):
                    reached(dve, t_turned, r - 1)
                    nc.vector.tensor_scalar(tin[j][:], X[:, bass.ds(r * D, D)], scale[:, bass.ds(r, 1)], None,
                                            ALU.mult).then_inc(tin_ready, 1)
                if exists(r - 3):
                    dve.wait_ge(b2_made, r - 2)
                    row = X[:, bass.ds((r - 3) * D, D)]
                    nc.vector.scalar_tensor_tensor(row, row, 2.0, b_ps[:, 0:D], ALU.mult,
                                                   ALU.add).then_inc(b2_added, 1)
                if exists(r - 2):
                    dve.wait_ge(e_ready, r - 1)
                    nc.vector.tensor_tensor(kept[:], expd[j][:], chosen[j][:], ALU.mult).then_inc(kept_ready, 1)
                    dve.wait_ge(kept_ready, r - 1)
                    nc.vector.tensor_reduce(total[:], kept[:], AX.X, ALU.add).then_inc(total_ready, 1)
                    dve.wait_ge(total_ready, r - 1)
                    nc.vector.reciprocal(inverse[:], total[:]).then_inc(inv_ready, 1)
                    dve.wait_ge(inv_ready, r - 1)
                    reached(dve, g_turned, r - 3)
                    reached(dve, g_kept, r - 3)
                    nc.vector.tensor_scalar(gates1[j][:], kept[:], inverse[:], None, ALU.mult).then_inc(g_ready, 1)
                if exists(r - 1):
                    i = 1 - j
                    dve.wait_ge(l_made, r)
                    reached(dve, e_ready, r - 2)
                    nc.vector.tensor_tensor(logits[i][:, 0:E], l_ps[:, 0:E], b_gate[:], ALU.add).then_inc(l_ready, 1)
                    dve.wait_ge(l_ready, r)
                    nc.vector.memset(places[:], NEG)
                    nc.vector.max(best[:], logits[i][:]).then_inc(best_ready, 1)
                    dve.wait_ge(best_ready, r)
                    nc.vector.tensor_copy(places[:, 0:TOP], best[:, 0:TOP]).then_inc(list_ready, 1)
                    dve.wait_ge(list_ready, r)
                    nc.vector.tensor_scalar(negmax[i][:], best[:, 0:1], -1.0, None, ALU.mult)
                    nc.vector.match_replace(left[:], places[:], logits[i][:], NEG).then_inc(left_ready, 1)
                    dve.wait_ge(left_ready, r)
                    nc.vector.tensor_tensor(chosen[i][:], left[:, 0:E], logits[i][:, 0:E],
                                            ALU.not_equal).then_inc(chosen_ready, 1)

            def unit(e, tt, j):
                u = e * TT + tt
                if live(e, tt):
                    for ic in range(IC):
                        n = u * IC + ic
                        dve.wait_ge(up_made, 2 * n + 1)
                        reached(dve, ag_ready, n - 1)
                        nc.vector.tensor_scalar(a[ic][:], up_ps[ic][0][:], b1[:, bass.ds(e, 1), 0, ic],
                                                LIMIT, ALU.add, ALU.min).then_inc(a_ready, 1)
                        dve.wait_ge(up_made, 2 * n + 2)
                        reached(dve, act_ready, n - 1)
                        nc.vector.tensor_scalar(bb[ic][:], up_ps[ic][1][:], b1[:, bass.ds(e, 1), 1, ic],
                                                LIMIT + 1.0, ALU.add, ALU.min).then_inc(b_ready, 1)
                    dve.wait_ge(b_ready, (u + 1) * IC)
                    for ic in range(IC):
                        n = u * IC + ic
                        dve.wait_ge(ag_ready, n + 1)
                        reached(dve, down_done, u - 1)
                        nc.vector.scalar_tensor_tensor(act_[tt % 2][:, ic], bb[ic][:], 1.0 - LIMIT, ag[ic][:],
                                                       ALU.max, ALU.mult).then_inc(act_ready, 1)
                if live(e, tt, 1):
                    v = (tt - 1) % 2
                    dve.wait_ge(down_done, u)
                    for n in range(TB):
                        at = (tt - 1) % TT * TB + n
                        eb = e if tt else e - 1
                        row = X[:, at * D:(at + 1) * D]
                        m = nc.vector.scalar_tensor_tensor(row, y_ps[v][n // 2][:, n % 2],
                                                           gates[:, bass.ds(at * E + eb, 1)], row, ALU.mult, ALU.add)
                    m.then_inc(y_added, 1)

            for j in range(R):
                nc.vector.memset(logits[j][:], NEG)
            dve.wait_ge(rms_ready, 1)
            nc.vector.reciprocal(scale[:], rms[:]).then_inc(scale_ready, 1)
            dve.wait_ge(scale_ready, 1)
            dve.wait_ge(w_loaded, 80)
            nc.vector.tensor_scalar(b1[:, :, 1], b1[:, :, 1], 1.0, None, ALU.add).then_inc(filled, 1)
            dve.wait_ge(filled, 1)
            prologue(dve, work)
            dve.wait_ge(b2_added, B)
            dve.wait_ge(g_kept, B)
            experts(dve, unit)
            norm.all_rows(dve, y_added, U)
            norm.vector_part(dve)


def rotary_tables():
    f = np.float32
    inv = (f(1.0) / np.power(f(10000.0), np.arange(0, HD, 2, dtype=f) / f(HD))).astype(f)
    ang = np.arange(P, dtype=f)[:, None] * inv[None, :]
    c, s = np.cos(ang).astype(f), np.sin(ang).astype(f)
    return np.concatenate([c, c], -1), np.concatenate([-s, s], -1)


def band_mask(window):
    i, j = np.arange(P)[:, None], np.arange(P)[None, :]
    return np.where((j <= i) & (j > i - window), 0.0, NEG).astype(np.float32)


def by_feature(w, name):
    if name in "vo":
        return w
    return w.reshape(H, P // H, -1).transpose(1, 0, 2).reshape(w.shape)


def lay_out(t):
    c = np.ascontiguousarray
    t = {k: np.asarray(v) for k, v in t.items()}
    cos, sin = rotary_tables()
    up = [w for w in t["L0_ffn_w13"]]
    g, u = np.split(t["L0_ffn_shared_gate_up_w"], 2)
    for at in range(0, len(g), 256):
        up += [g[at:at + 256], u[at:at + 256]]
    down = np.concatenate([t["L0_ffn_w2"].transpose(0, 2, 1).reshape(-1, D), t["L0_ffn_shared_down_w"].T])
    return {
        "x": c(t["x"].transpose(1, 0, 2)),
        "ident": np.eye(P, dtype=np.float32),
        "cos": cos, "sin": sin, "mask": band_mask(WINDOW),
        "wqkv": c(t["L0_attn_w_qkv"].reshape(3, G, GW, KC, P).transpose(4, 3, 1, 0, 2)),
        "ctx": c(t["ctx_2048"].transpose(1, 0, 2)).reshape(P, B * D),
        "xw": c(np.stack([by_feature(t[f"L0_xattn_W{n}"], n).T for n in "qkvo"], 1)),
        "xbias": c(np.stack([by_feature(t[f"L0_xattn_b{n}"], n) for n in "qkvo"], 1)),
        "causal": band_mask(P),
        "m_norm": c(t["L1_ffn_norm_w"].reshape(KC, P).T),
        "m_gate": c(t["L1_ffn_gate_w"].T.reshape(KC, P, 16).transpose(1, 0, 2)),
        "m_bgate": t["L1_ffn_gate_b"],
        "m_b2": t["L1_ffn_b2"],
        "m_b1": c(t["L1_ffn_b1"].reshape(16, KC, P, 2).transpose(2, 0, 3, 1)),
        "m_w1": c(t["L1_ffn_w1"].reshape(16, KC, P, 2, KC, P).transpose(0, 5, 4, 1, 3, 2)).reshape(16, P, -1),
        "m_w2": c(t["L1_ffn_w2"].reshape(16, D, KC, P).transpose(0, 3, 2, 1)).reshape(16, P, -1),
        "w_wu": c(np.stack([t["L1_xattn_w"], t["L1_xattn_u"]]).reshape(2, KC, P).transpose(2, 0, 1)),
        "r_rank": c(np.stack([t["L1_attn_Ws"], t["L1_attn_Wa"]], 1).reshape(KC, P, 2, 32).transpose(1, 0, 2, 3)),
        "r_wo": c(t["L1_attn_Wo"].T.reshape(KC, P, D).transpose(1, 0, 2)),
        "r_bo": t["L1_attn_bo"],
        "f_router": c(np.concatenate([t["L0_ffn_gate_w"], t["L0_ffn_shared_gate_w"]]).reshape(9, KC, P).transpose(2, 1, 0)),
        "f_up": c(np.concatenate(up, 0).reshape(-1, KC, P).transpose(2, 1, 0)),
        "f_down": c(np.concatenate([down, np.zeros((-len(down) % P, D), np.float32)]).reshape(-1, P, D).transpose(1, 0, 2)),
        "wo": c(t["L0_attn_w_o"].reshape(D, H, P).transpose(2, 1, 0)),
    }


def program(nc, A, out, stages="ABCDEF"):
    with ExitStack() as outer:
        banks = [outer.enter_context(nc.psum_tensor(f"bank{n}", [P, 512], F32)) for n in range(8)]
        room = Room(nc, outer, "all", banks)
        X = room.sb("X", [P, B * D])
        ident = room.sb("ident", [P, P])
        eps = room.sb("eps", [P, 1])
        ctx = room.sb("ctx", [P, B * D])
        start, made, stored, ctx_loaded = room.sems("start made stored ctx_loaded")
        with nc.Block() as block:

            @block.sync
            def _(sp):
                sp.dma_start(ident[:], A["ident"]).then_inc(start, 16)
                sp.wait_ge(start, 16)

            @block.vector
            def _(dve):
                nc.vector.memset(eps[:], EPS).then_inc(made, 1)
                dve.wait_ge(made, 1)

        if stages[0] != "A":
            with nc.Block() as block:

                @block.sync
                def _(sp):
                    sp.dma_start(X[:].rearrange("p (b d) -> p b d", b=B), A["x"]).then_inc(start, 16)
                    sp.wait_ge(start, 32)
                    sp.dma_start(ctx[:], A["ctx"]).then_inc(ctx_loaded, 16)
                    sp.wait_ge(ctx_loaded, 16)
        for letter, stage in (("A", self_attention), ("B", cross_attention), ("C", ffn),
                              ("D", low_rank_attention), ("E", wkv), ("F", mixture)):
            if letter in stages:
                with ExitStack() as stack:
                    own = Room(nc, stack, letter, banks)
                    stage(nc, own, A, X, ident, eps, *((ctx, ctx_loaded) if letter in "AB" else ()))
                    own.close()
        with nc.Block() as block:

            @block.sync
            def _(sp):
                sp.dma_start(out.rearrange("b t d -> t b d"), X[:].rearrange("p (b d) -> p b d", b=B)).then_inc(stored, 16)
                sp.wait_ge(stored, 16)


def kernel(**inputs):
    import concourse.bacc as bacc
    from concourse.bass_utils import run_bass_kernel_spmd

    arrays = lay_out(inputs)
    nc = bacc.Bacc("TRN2", target_bir_lowering=False, num_devices=1)
    A = {n: nc.dram_tensor(f"in_{n}", a.shape, mybir.dt.from_np(a.dtype), kind="ExternalInput").ap()
         for n, a in arrays.items()}
    out = nc.dram_tensor("out", (B, P, D), F32, kind="ExternalOutput").ap()
    program(nc, A, out)
    r = run_bass_kernel_spmd(nc, [{f"in_{n}": a for n, a in arrays.items()}], core_ids=[0])
    return r.results[0]["out"]
```

```python
from contextlib import ExitStack

import concourse.bass as bass
import numpy as np
from concourse import mybir

F32 = mybir.dt.float32
BF16 = mybir.dt.bfloat16
F32R = mybir.dt.float32r
ALU = mybir.AluOpType
ACT = mybir.ActivationFunctionType
AX = mybir.AxisListType

P = 128
B = 16
D = 256
KC = D // P
H = 16
HD = 128
G = 4
HG = H // G
GW = HG * HD
WINDOW = 64
NEG = -3.0e38
EPS = 1e-5


EARLY = {"ctx": [P, B * D], "xw": [P, 4, P], "xbias": [P, 4], "f_router": [P, KC, 9]}
LATER = {
    "r_rank": [P, KC, 2, 32], "r_wo": [P, KC, D], "r_bo": [P, D], "causal": [P, P], "w_wu": [P, 2, KC],
    "m_norm": [P, KC], "m_gate": [P, KC, 16], "m_bgate": [P, 16], "m_b2": [16, D], "m_b1": [P, 16, 2, KC],
}


def load(sp, A, names, early, loaded):
    for name in names:
        src = A[name].partition_broadcast(P) if name in ("r_bo", "m_bgate") else A[name]
        sp.dma_start(early[name][:], src).then_inc(loaded, 16)


def reached(eng, sem, count):
    if not isinstance(count, int) or count > 0:
        eng.wait_ge(sem, count)


class Room:

    def __init__(self, nc, stack, prefix, banks, early=None):
        self.nc, self.stack, self.prefix, self.banks = nc, stack, prefix, list(banks)
        self.early = early or {}
        self.taken = []

    def sb(self, name, shape, dt=F32):
        return self.stack.enter_context(self.nc.sbuf_tensor(f"{self.prefix}_{name}", shape, dt))

    def ps(self, shape):
        bank = self.banks.pop(0)[:]
        return bank if len(shape) == 2 else bank.rearrange("p (a b) -> p a b", a=shape[1])

    def sem(self, name):
        self.taken.append(self.nc.alloc_semaphore(name=f"{self.prefix}_{name}"))
        return self.taken[-1]

    def sems(self, names):
        return [self.sem(n) for n in names.split()]

    def close(self):
        with self.nc.Block() as block:

            @block.gpsimd
            def _(pool):
                self.nc.clear_and_free_semaphores(self.taken)


class RowNorm:
    SHARE = 9

    def __init__(self, nc, room, X, eps):
        self.nc, self.X, self.eps, self.in_loop = nc, X, eps, True
        self.row = room.sb("row", [P, D])
        self.moments = room.sb("moments", [P, 6])
        self.all_moments = room.sb("all_moments", [P, B, 6])
        self.stats = room.sb("stats", [P, B, 2])
        self.root = room.sb("root", [P, B])
        self.rstd = room.sb("rstd", [P, B])
        self.offset = room.sb("offset", [P, B])
        self.row_ready, self.kept, self.bn_ready, self.moments_ready = room.sems(
            "row_ready row_kept bn_ready moments_ready")
        self.stats_ready, self.root_ready, self.rstd_ready, self.offset_ready, self.normed = room.sems(
            "stats_ready root_ready rstd_ready offset_ready normed")

    def put(self, dve, b):
        nc = self.nc
        dve.wait_ge(self.row_ready, b + 1)
        nc.vector.tensor_scalar(self.X[:, bass.ds(b * D, D)], self.row[:], 0.0, None,
                                ALU.add).then_inc(self.kept, 1)
        nc.vector.bn_stats(self.moments[:], self.row[:]).then_inc(self.bn_ready, 1)
        dve.wait_ge(self.bn_ready, b + 1)
        nc.vector.tensor_scalar(self.all_moments[:, bass.ds(b, 1), :].rearrange("p b s -> p (b s)"),
                                self.moments[:], 0.0, None, ALU.add).then_inc(self.moments_ready, 1)

    def all_rows(self, dve, added, count):
        dve.wait_ge(added, count)
        for b in range(B):
            self.moments_of(dve, b)
        self.in_loop = False

    def moments_of(self, dve, b):
        self.nc.vector.bn_stats(self.all_moments[:, b],
                                self.X[:, b * D:(b + 1) * D]).then_inc(self.moments_ready, 1)

    def scalar_part(self, act):
        nc = self.nc
        act.wait_ge(self.stats_ready, B)
        nc.scalar.activation(self.root[:], self.stats[:, :, 1], ACT.Sqrt,
                             bias=self.eps[:]).then_inc(self.root_ready, 1)
        act.wait_ge(self.offset_ready, 1)
        for b in range(self.SHARE, B):
            row = self.X[:, b * D:(b + 1) * D]
            nc.scalar.activation(row, row, ACT.Identity, scale=self.rstd[:, b:b + 1],
                                 bias=self.offset[:, b:b + 1]).then_inc(self.normed, 1)

    def vector_part(self, dve):
        nc = self.nc
        dve.wait_ge(self.moments_ready, B)
        for b in range(B):
            nc.vector.bn_aggr(self.stats[:, b], self.all_moments[:, b]).then_inc(self.stats_ready, 1)
        dve.wait_ge(self.root_ready, 1)
        nc.vector.reciprocal(self.rstd[:], self.root[:]).then_inc(self.rstd_ready, 1)
        dve.wait_ge(self.rstd_ready, 1)
        if self.in_loop:
            dve.wait_ge(self.kept, B)
        nc.vector.scalar_tensor_tensor(self.offset[:], self.stats[:, :, 0], -1.0, self.rstd[:], ALU.mult,
                                       ALU.mult).then_inc(self.offset_ready, 1)
        for b in range(self.SHARE):
            row = self.X[:, b * D:(b + 1) * D]
            nc.vector.tensor_scalar(row, row, self.stats[:, b, 0:1], self.rstd[:, b:b + 1],
                                    ALU.subtract, ALU.mult).then_inc(self.normed, 1)


def split_product(nc, out, stationary, moving, start, stop):
    (s_hi, s_lo), (m_hi, m_lo) = stationary, moving
    nc.tensor.matmul(out, s_hi, m_hi, start=start, stop=False)
    nc.tensor.matmul(out, s_hi, m_lo, start=False, stop=False)
    return nc.tensor.matmul(out, s_lo, m_hi, start=False, stop=stop)


def self_attention(nc, room, A, X, ident, eps):
    wqkv_hi, wqkv_lo = (room.sb(f"wqkv_{n}", [P, KC, G, 3, GW], F32R) for n in ("hi", "lo"))
    NW, SLOTS, PIECE = KC * G, 2, 3 * GW
    staged = [room.early["ctx"][:, n * PIECE:(n + 1) * PIECE] for n in range(SLOTS)]
    WO_PIECES = 4
    HP = H // WO_PIECES
    wo_hi, wo_lo = (room.sb(f"wo_{n}", [P, H, D], F32R) for n in ("hi", "lo"))
    cos = room.sb("cos", [P, HD])
    sin = room.sb("sin", [P, HD])
    mask = room.sb("mask", [P, P])
    xin = room.sb("xin", [P, D])
    xT_hi, xT_lo = (room.sb(f"xT_{n}", [P, KC, P], F32R) for n in ("hi", "lo"))
    t1 = room.sb("t1", [P, 2, GW])
    t2 = room.sb("t2", [P, 2, GW])
    qk = room.sb("qk", [P, 2, GW])
    qkT = room.sb("qkT", [P, 2, GW])
    v = room.sb("v", [P, G, GW])
    s = room.sb("s", [P, HG, P])
    p = room.sb("p", [P, HG, P])
    negmax = room.sb("negmax", [P, HG])
    total = room.sb("total", [P, HG])
    inverse = room.sb("inverse", [P, HG])
    pT = room.sb("pT", [P, HG, P])
    oT_hi, oT_lo = (room.sb(f"oT_{n}", [P, HG, P], F32R) for n in ("hi", "lo"))
    norm = RowNorm(nc, room, X, eps)
    qkv_ps = [room.ps([P, GW]) for n in ("q_ps", "k_ps", "v_ps")]
    turn_ps = room.ps([P, GW])
    y_ps = room.ps([P, GW])
    s_ps = room.ps([P, HG, P])
    pT_ps = room.ps([P, HG, P])
    o_ps = room.ps([P, HG, P])

    x_loaded, ident_loaded, rest_loaded, table_loaded, early_loaded = room.sems(
        "x_loaded ident_loaded rest_loaded table_loaded early_loaded")
    w_loaded = [room.sem(f"w_loaded{n}") for n in range(SLOTS)]
    xin_ready, xT_done, xT_copied = room.sems("xin_ready xT_done xT_copied")
    made = room.sems("q_made k_made v_made")
    taken = room.sems("q_taken k_taken v_taken")
    rotated = room.sems("q_rotated k_rotated")
    turned = room.sems("q_turned k_turned")
    copied = room.sems("qT_copied kT_copied")
    xT_split, oT_split, w_hi, w_split = room.sems("xT_split oT_split w_hi w_split")
    s_made, s_taken, max_ready, e_ready = room.sems("s_made s_taken max_ready e_ready")
    inv_ready, p_ready, pT_made, pT_copied = room.sems("inv_ready p_ready pT_made pT_copied")
    o_made, oT_copied, wo_done = room.sems("o_made oT_copied wo_done")
    SCALE = float(1.0 / np.sqrt(HD))

    def sequences(eng, unit, tail):
        for g in range(G):
            unit(0, g)
        with eng.Fori(1, B - 1) as b:
            for g in range(G):
                unit(b, g)
        for n in range(G + tail):
            unit(B - 1 + n // G, n % G)

    PIECES = [range(g * KC, (g + 1) * KC) for g in range(G)] + [range(NW, NW + WO_PIECES)]

    def piece(wqkv, wo, n):
        if n < NW:
            return wqkv[:, n % KC, n // KC].rearrange("p i e -> p (i e)"), staged[n % SLOTS]
        at = (n - NW) * HP
        return wo[:, at:at + HP].rearrange("p h d -> p (h d)"), staged[n % SLOTS][:, 0:HP * D]

    def live(b, g, back=0):
        return not isinstance(b, int) or 0 <= b * G + g - back < B * G

    def has_next(b):
        return not isinstance(b, int) or b + 1 < B

    with nc.Block() as block:

        @block.sync
        def _(sp):
            sp.dma_start(X[:, 0:D], A["x"][:, 0, :]).then_inc(x_loaded, 16)
            sp.dma_start(ident[:], A["ident"]).then_inc(ident_loaded, 16)
            for n in range(NW + WO_PIECES):
                g, c = n // KC, n % KC
                if n == KC * 2:
                    sp.dma_start(X[:, D:B * D].rearrange("p (b d) -> p b d", b=B - 1),
                                 A["x"][:, 1:B, :]).then_inc(rest_loaded, 16)
                reached(sp, w_split, n - SLOTS + 1)
                if n < NW:
                    sp.dma_start(staged[n % SLOTS], A["wqkv"][:, c, g].rearrange("p i e -> p (i e)")).then_inc(
                        w_loaded[n % SLOTS], 16)
                else:
                    at = (n - NW) * HP
                    sp.dma_start(staged[n % SLOTS][:, 0:HP * D],
                                 A["wo"][:, at:at + HP].rearrange("p h d -> p (h d)")).then_inc(w_loaded[n % SLOTS], 16)
            sp.wait_ge(w_split, NW + WO_PIECES)
            load(sp, A, EARLY, room.early, early_loaded)
            sp.wait_ge(early_loaded, 16 * len(EARLY))

        @block.gpsimd
        def _(pool):
            def unit(b, g):
                u = b * G + g
                for i in range(2):
                    pool.wait_ge(taken[i], u + 1)
                    reached(pool, turned[i], u)
                    nc.gpsimd.tensor_tensor(qk[:, i], t1[:, i], t2[:, i],
                                            ALU.add).then_inc(rotated[i], 1)
                if g == 0 and has_next(b):
                    pool.wait_ge(xT_done, b + 1)
                    if isinstance(b, int) and b == 0:
                        pool.wait_ge(rest_loaded, 16)
                    nc.gpsimd.tensor_copy(xin[:], X[:, bass.ds((b + 1) * D, D)]).then_inc(xin_ready, 1)

            pool.wait_ge(x_loaded, 16)
            nc.gpsimd.tensor_copy(xin[:], X[:, 0:D]).then_inc(xin_ready, 1)
            sequences(pool, unit, 0)

        @block.scalar
        def _(act):
            act.dma_start(cos[:], A["cos"]).then_inc(table_loaded, 16)
            act.dma_start(sin[:], A["sin"]).then_inc(table_loaded, 16)
            act.dma_start(mask[:], A["mask"]).then_inc(table_loaded, 16)

            def split_weights(pieces):
                for n in pieces:
                    act.wait_ge(w_loaded[n % SLOTS], 16 * (n // SLOTS + 1))
                    hi, raw = piece(wqkv_hi, wo_hi, n)
                    nc.scalar.copy(hi, raw).then_inc(w_hi, 1)

            def copy_xT(b):
                act.wait_ge(xT_done, b + 1)
                nc.scalar.copy(xT_hi[:].rearrange("p c t -> p (c t)"), turn_ps[:, 0:D]).then_inc(xT_copied, 1)

            def unit(b, g):
                u = b * G + g
                if live(b, g, 1):
                    for i in range(2):
                        act.wait_ge(turned[i], u)
                        reached(act, s_made, u - 1)
                        nc.scalar.copy(qkT[:, i], turn_ps[:]).then_inc(copied[i], 1)
                if isinstance(b, int) and b == 0 and g + 1 < G:
                    split_weights(PIECES[g + 1])
                if live(b, g, 2):
                    act.wait_ge(pT_made, u - 1)
                    reached(act, o_made, u - 2)
                    nc.scalar.copy(pT[:], pT_ps[:]).then_inc(pT_copied, 1)
                if live(b, g):
                    act.wait_ge(made[2], u + 1)
                    reached(act, o_made, u - 3)
                    nc.scalar.copy(v[:, g], qkv_ps[2][:]).then_inc(taken[2], 1)
                    if g == G - 1 and has_next(b):
                        copy_xT(b + 1)
                if live(b, g, 2):
                    act.wait_ge(o_made, u - 1)
                    reached(act, wo_done, u - 2)
                    nc.scalar.copy(oT_hi[:], o_ps[:]).then_inc(oT_copied, 1)
                if live(b, g, 1):
                    act.wait_ge(max_ready, u)
                    reached(act, pT_made, u - 1)
                    for h in range(HG):
                        e = nc.scalar.activation(p[:, h], s[:, h], ACT.Exp, bias=negmax[:, h:h + 1],
                                                 accum_out=total[:, h:h + 1])
                    e.then_inc(e_ready, 1)
                if isinstance(b, int) and b == 0 and g == G - 2:
                    split_weights(PIECES[G])

            copy_xT(0)
            split_weights(PIECES[0])
            sequences(act, unit, 2)
            norm.scalar_part(act)

        @block.tensor
        def _(pe):
            def turn(i, b, g):
                u = b * G + g
                pe.wait_ge(rotated[i], u)
                if i == 0:
                    reached(pe, copied[1], u - 1)
                    if g == 0 and has_next(b - 1 if isinstance(b, int) else b):
                        pe.wait_ge(xT_split, b + 1)
                else:
                    pe.wait_ge(copied[0], u)
                for h in range(HG):
                    m = nc.tensor.transpose(turn_ps[:, h * HD:(h + 1) * HD],
                                            qk[:, i, h * HD:(h + 1) * HD], ident[:])
                m.then_inc(turned[i], 1)

            def project(i, b, g):
                u = b * G + g
                reached(pe, taken[i], u)
                if i == 0:
                    if g == 0:
                        pe.wait_ge(xT_split, b + 1)
                    if isinstance(b, int) and b == 0:
                        pe.wait_ge(w_split, (g + 1) * KC)
                for c in range(KC):
                    m = split_product(nc, qkv_ps[i][:], (xT_hi[:, c], xT_lo[:, c]),
                                      (wqkv_hi[:, c, g, i], wqkv_lo[:, c, g, i]), c == 0, c == KC - 1)
                m.then_inc(made[i], 1)

            def turn_x(b):
                pe.wait_ge(xin_ready, b + 1)
                for c in range(KC):
                    m = nc.tensor.transpose(turn_ps[:, c * P:(c + 1) * P], xin[:, c * P:(c + 1) * P], ident[:])
                m.then_inc(xT_done, 1)

            def project_heads(b, g):
                u, gh = b * G + g, (g - 3) % G
                pe.wait_ge(oT_split, u - 2)
                if isinstance(b, int) and u == 3:
                    pe.wait_ge(w_split, NW + WO_PIECES)
                if gh == 0:
                    reached(pe, norm.row_ready, (b if g == 3 else b - 1))
                for h in range(HG):
                    at = gh * HG + h
                    m = split_product(nc, y_ps[:, 0:D], (oT_hi[:, h], oT_lo[:, h]), (wo_hi[:, at], wo_lo[:, at]),
                                      at == 0, at == H - 1)
                m.then_inc(wo_done, 1)

            def unit(b, g):
                u = b * G + g
                if live(b, g, 1):
                    turn(0, b, g)
                if live(b, g):
                    project(0, b, g)
                if live(b, g, 3):
                    project_heads(b, g)
                if live(b, g, 1):
                    turn(1, b, g)
                if live(b, g):
                    project(1, b, g)
                if live(b, g, 2):
                    pe.wait_ge(p_ready, u - 1)
                    reached(pe, pT_copied, u - 2)
                    for h in range(HG):
                        m = nc.tensor.transpose(pT_ps[:, h], p[:, h], ident[:])
                    m.then_inc(pT_made, 1)
                if live(b, g):
                    project(2, b, g)
                    if g == G - 1 and has_next(b):
                        pe.wait_ge(copied[1], u)
                        turn_x(b + 1)
                if live(b, g, 1):
                    pe.wait_ge(copied[1], u)
                    reached(pe, s_taken, u - 1)
                    for h in range(HG):
                        m = nc.tensor.matmul(s_ps[:, h], qkT[:, 0, h * HD:(h + 1) * HD],
                                             qkT[:, 1, h * HD:(h + 1) * HD], start=True, stop=True)
                    m.then_inc(s_made, 1)
                if live(b, g, 2):
                    pe.wait_ge(pT_copied, u - 1)
                    reached(pe, oT_split, u - 2)
                    for h in range(HG):
                        m = nc.tensor.matmul(o_ps[:, h], v[:, (g - 2) % G, h * HD:(h + 1) * HD],
                                             pT[:, h], start=True, stop=True)
                    m.then_inc(o_made, 1)

            pe.wait_ge(ident_loaded, 16)
            turn_x(0)
            sequences(pe, unit, 3)

        @block.vector
        def _(dve):
            half = HD // 2

            def rotate(i, b, g):
                u = b * G + g
                src = qkv_ps[i][:].rearrange("p (h e) -> p h e", h=HG)
                a = t1[:, i].rearrange("p (h e) -> p h e", h=HG)
                c = t2[:, i].rearrange("p (h e) -> p h e", h=HG)
                dve.wait_ge(made[i], u + 1)
                reached(dve, rotated[i], u)
                nc.vector.tensor_tensor(a, src, cos[:, None, :].to_broadcast([P, HG, HD]), ALU.mult)
                nc.vector.tensor_tensor(c[:, :, 0:half], src[:, :, half:HD],
                                        sin[:, None, 0:half].to_broadcast([P, HG, half]), ALU.mult)
                nc.vector.tensor_tensor(c[:, :, half:HD], src[:, :, 0:half],
                                        sin[:, None, half:HD].to_broadcast([P, HG, half]),
                                        ALU.mult).then_inc(taken[i], 1)

            def split_weights(pieces):
                for n in pieces:
                    dve.wait_ge(w_hi, n + 1)
                    lo, raw = piece(wqkv_lo, wo_lo, n)
                    hi, _ = piece(wqkv_hi, wo_hi, n)
                    nc.vector.tensor_tensor(lo, raw, hi.bitcast(F32), ALU.subtract).then_inc(w_split, 1)

            def split_xT(b):
                dve.wait_ge(xT_copied, b + 1)
                nc.vector.tensor_tensor(xT_lo[:].rearrange("p c t -> p (c t)"), turn_ps[:, 0:D],
                                        xT_hi[:].rearrange("p c t -> p (c t)").bitcast(F32),
                                        ALU.subtract).then_inc(xT_split, 1)

            def unit(b, g):
                u = b * G + g
                if live(b, g, 3):
                    dve.wait_ge(oT_copied, u - 2)
                    nc.vector.tensor_tensor(oT_lo[:], o_ps[:], oT_hi[:].bitcast(F32), ALU.subtract).then_inc(oT_split, 1)
                if live(b, g, 2):
                    dve.wait_ge(e_ready, u - 1)
                    nc.vector.reciprocal(inverse[:], total[:]).then_inc(inv_ready, 1)
                    dve.wait_ge(inv_ready, u - 1)
                    nc.vector.tensor_tensor(p[:], p[:], inverse[:, :, None].to_broadcast([P, HG, P]),
                                            ALU.mult).then_inc(p_ready, 1)
                if live(b, g):
                    rotate(0, b, g)
                    rotate(1, b, g)
                if isinstance(b, int) and b == 0 and g + 1 < G:
                    split_weights(PIECES[g + 1])
                if g == 2 and live(b, g, 6):
                    dve.wait_ge(wo_done, b * G)
                    nc.vector.tensor_tensor(norm.row[:], X[:, bass.ds((b - 1) * D, D)], y_ps[:, 0:D],
                                            ALU.add).then_inc(norm.row_ready, 1)
                    norm.put(dve, b - 1)
                if g == G - 1 and live(b, g) and has_next(b):
                    split_xT(b + 1)
                if live(b, g, 1):
                    dve.wait_ge(s_made, u)
                    reached(dve, e_ready, u - 1)
                    nc.vector.scalar_tensor_tensor(s[:], s_ps[:], SCALE,
                                                   mask[:, None, :].to_broadcast([P, HG, P]),
                                                   ALU.mult, ALU.add).then_inc(s_taken, 1)
                    dve.wait_ge(s_taken, u)
                    nc.vector.tensor_reduce(negmax[:], s[:], AX.X, ALU.max, negate=True).then_inc(max_ready, 1)
                if isinstance(b, int) and b == 0 and g == G - 2:
                    split_weights(PIECES[G])

            nc.vector.memset(eps[:], EPS)
            split_xT(0)
            split_weights(PIECES[0])
            dve.wait_ge(table_loaded, 48)
            sequences(dve, unit, 3)
            norm.vector_part(dve)


def cross_attention(nc, room, A, X, ident, eps):
    FD = 8
    RUNS = ((0, 3, 0), (3, 2, 1), (5, 1, 2))
    SHIFT = FD * 6
    NPAR = 2
    VW = 32
    SCALE = float(1.0 / np.sqrt(P))
    N_STACK = 2 * len(RUNS)
    R = 4
    up, down = room.early["up"], room.early["down"]
    spread = nc.dram_tensor("spread", [R, 6, P, D], BF16, kind="Internal").ap()

    ctx = room.early["ctx"]
    w = room.early["xw"]
    bias = room.early["xbias"]
    bq = room.sb("bq", [P, 1])
    full = room.sb("full", [P, 2, D])
    rest = room.sb("rest", [P, 2, D])
    part = room.sb("part", [P, 3, 2, D], BF16)
    cin = [room.sb(f"cin{j}", [P, D]) for j in range(2)]
    QS = [room.sb(f"QS{j}", [P, H, D], BF16) for j in range(R)]
    KS = [room.sb(f"KS{j}", [P, H, D], BF16) for j in range(R)]
    zero = room.sb("zero", [NPAR, H * D], BF16)
    V = [room.sb(f"V{j}", [P, KC, H, VW]) for j in range(R)]
    negmax = room.sb("negmax", [P, KC, H])
    high = room.sb("high", [P, KC, H], BF16)
    pair = room.sb("pair", [P, KC, NPAR, H])
    shift = room.sb("shift", [NPAR * H, D], BF16)
    pr = [room.sb(f"pr{j}", [P, KC, D]) for j in range(4)]
    oT = room.sb("oT", [P, 4, D])
    inverse = room.sb("inverse", [P, KC, H])
    o = room.sb("o", [P, KC, H, FD])
    onT = room.sb("onT", [P, D])
    norm = RowNorm(nc, room, X, eps)
    a_ps = room.ps([P, KC, D])
    b_ps = room.ps([P, KC, D])
    m_ps = [room.ps([P, KC, D]) for j in range(2)]
    s_ps = [room.ps([P, KC, D]) for j in range(2)]
    o_ps = [room.ps([P, KC, D]) for j in range(2)]

    cin_ready, next_loaded, early_loaded = room.sems("cin_ready next_loaded early_loaded")
    zero_ready, v_cleared, parts_out, zeroed, stacked, shifted = room.sems(
        "zero_ready v_cleared parts_out zeroed stacked shifted")
    cleared = [room.sem(f"cleared{j}") for j in range(R)]
    qk_made, qk_taken, v_made, v_ready = room.sems("qk_made qk_taken v_made v_ready")
    bq_ready, part0, part1, part2, rest0 = room.sems("bq_ready part0 part1 part2 rest0")
    m_made, max_ready = room.sems("m_made max_ready")
    high_ready, pair_ready, pair_turned, shift_ready = room.sems("high_ready pair_ready pair_turned shift_ready")
    s_made, p_ready, pv_done = room.sems("s_made p_ready pv_done")
    oT_copied, nat_made, inv_ready, o_ready = room.sems("oT_copied nat_made inv_ready o_ready")
    onT_made, onT_copied, y_made = room.sems("onT_made onT_copied y_made")

    def rounds(eng, work):
        for r in range(R - 1):
            work(r, r)
        with eng.Fori(R - 1, B - R, R) as r:
            for n in range(R):
                work(r + n, (R - 1 + n) % R)
        for r in range(B - 1, B + 3):
            work(r, r % R)

    def exists(b):
        return not isinstance(b, int) or 0 <= b < B

    with nc.Block() as block:

        @block.sync
        def _(sp):
            def stack(b, j):
                sp.wait_ge(part2, b + 1)
                sp.dma_start(spread[j].rearrange("n p s -> p n s"),
                             part[:].rearrange("p k i s -> p (k i) s")).then_inc(parts_out, 16)
                reached(sp, s_made, (b - 3) * H)
                if isinstance(b, int) and b < R:
                    sp.wait_ge(cleared[b], 1)
                sp.dma_start(QS[j][SHIFT:SHIFT + NPAR].rearrange("n h s -> n (h s)"), zero[:]).then_inc(zeroed, 16)
                sp.wait_ge(parts_out, 16 * (b + 1))
                src = spread[j].rearrange("(k i) (d h) s -> k i d (h s)", i=2, d=FD)
                for n, m, k in RUNS:
                    rows = slice(n * FD, (n + m) * FD)
                    sp.dma_start(KS[j][rows].rearrange("r h s -> r (h s)"), src[0:m, 1]).then_inc(stacked, 16)
                    sp.dma_start(QS[j][rows].rearrange("r h s -> r (h s)"),
                                 src[k:k + 1, 0].to_broadcast([m, FD, H * D])).then_inc(stacked, 16)

            def work(r, j):
                if exists(r - 1):
                    sp.wait_ge(shift_ready, r)
                    for n in range(NPAR):
                        sp.dma_start(QS[(j - 1) % R][SHIFT + n:SHIFT + n + 1],
                                     shift[n * H:(n + 1) * H]).then_inc(shifted, 16)
                if exists(r + 1):
                    stack(r + 1, (j + 1) % R)

            sp.wait_ge(zero_ready, 1)
            stack(0, 0)
            load(sp, A, LATER, room.early, early_loaded)
            sp.dma_start(up[:], A["f_up"]).then_inc(next_loaded, 16)
            sp.dma_start(down[:], A["f_down"]).then_inc(next_loaded, 16)
            rounds(sp, work)
            sp.wait_ge(next_loaded, 32)
            sp.wait_ge(early_loaded, 16 * len(LATER))

        @block.gpsimd
        def _(pool):
            nc.gpsimd.memset(zero[:], 0.0).then_inc(zero_ready, 1)

            def split(b):
                pool.wait_ge(part0, b + 1)
                nc.gpsimd.tensor_tensor(rest[:], full[:], part[:, 0], ALU.subtract).then_inc(rest0, 1)
                pool.wait_ge(part1, b + 1)
                nc.gpsimd.tensor_tensor(part[:, 2], rest[:], part[:, 1], ALU.subtract).then_inc(part2, 1)

            def work(r, j):
                if isinstance(r, int) and r < R - 1:
                    for n in (0, 1) if r == 0 else (r + 1,):
                        nc.gpsimd.memset(V[n][:, :, :, FD + 1:VW], 0.0)
                        nc.gpsimd.memset(V[n][:, :, :, FD:FD + 1], 1.0).then_inc(v_cleared, 1)
                if exists(r):
                    reached(pool, v_made, r - 1)
                    nc.gpsimd.tensor_copy(cin[j % 2][:], ctx[:, bass.ds(r * D, D)]).then_inc(cin_ready, 1)
                if exists(r + 1):
                    split(r + 1)

            split(0)
            rounds(pool, work)

        @block.scalar
        def _(act):
            def take_qk(b):
                act.wait_ge(qk_made, b + 1)
                reached(act, part2, b)
                nc.scalar.activation(full[:, 0], a_ps[:, 0], ACT.Identity, bias=bq[:], scale=SCALE)
                nc.scalar.activation(full[:, 1], a_ps[:, 1], ACT.Identity,
                                     bias=bias[:, 1:2]).then_inc(qk_taken, 1)
                act.wait_ge(qk_taken, b + 1)
                reached(act, parts_out, b * 16)
                nc.scalar.copy(part[:, 0], full[:]).then_inc(part0, 1)

            def second_part(b):
                act.wait_ge(rest0, b + 1)
                nc.scalar.copy(part[:, 1], rest[:]).then_inc(part1, 1)

            def work(r, j):
                for h in range(H):
                    if exists(r - 2):
                        act.wait_ge(s_made, (r - 2) * H + h + 1)
                        reached(act, pv_done, (r - 2) * H + h - 3)
                        nc.scalar.activation(pr[h % 4][:], s_ps[h % 2][:], ACT.Exp).then_inc(p_ready, 1)
                    if h == 0 and exists(r - 3):
                        act.wait_ge(pv_done, H * (r - 2))
                        nc.scalar.copy(oT[:, 2:4], o_ps[1][:]).then_inc(oT_copied, 1)
                    if h == 1 and exists(r + 1):
                        take_qk(r + 1)
                    if h == 3 and exists(r + 1):
                        second_part(r + 1)
                    if h == 4 and exists(r - 1):
                        act.wait_ge(pair_turned, r)
                        reached(act, shifted, 32 * (r - 1))
                        nc.scalar.copy(shift[:], a_ps[0:NPAR * H, 1]).then_inc(shift_ready, 1)
                    if h == 7 and exists(r - 3):
                        act.wait_ge(onT_made, r - 2)
                        nc.scalar.activation(onT[:], a_ps[:, 0], ACT.Identity,
                                             bias=bias[:, 2:3]).then_inc(onT_copied, 1)
                    if h == 9 and exists(r - 2):
                        act.wait_ge(pv_done, H * (r - 2) + H // 2)
                        nc.scalar.copy(oT[:, 0:2], o_ps[0][:]).then_inc(oT_copied, 1)
                    if h == 13 and exists(r):
                        act.wait_ge(v_made, r + 1)
                        if isinstance(r, int) and r < R - 1:
                            act.wait_ge(v_cleared, r + 2)
                        nc.scalar.copy(V[j][:, :, :, 0:FD],
                                       b_ps[:].rearrange("p c (o e) -> p c o e", o=2)[:, :, 0].rearrange(
                                           "p c (h e) -> p c h e", h=H)).then_inc(v_ready, 1)

            nc.scalar.mul(bq[:], bias[:, 0:1], SCALE).then_inc(bq_ready, 1)
            act.wait_ge(bq_ready, 1)
            take_qk(0)
            second_part(0)
            rounds(act, work)
            norm.scalar_part(act)

        @block.tensor
        def _(pe):
            def project_qk(b):
                nc.tensor.matmul(a_ps[:, 0], w[:, 0], X[:, bass.ds(b * D, D)], start=True, stop=True)
                nc.tensor.matmul(a_ps[:, 1], w[:, 1], ctx[:, bass.ds(b * D, D)], start=True,
                                 stop=True).then_inc(qk_made, 1)

            def attend(r, i, h):
                if h == 0:
                    pe.wait_ge(v_ready, r - 1)
                if h % (H // 2) == 0:
                    half = 2 * h // H
                    reached(pe, oT_copied, 2 * (r - 3) + 1 + half)
                pe.wait_ge(p_ready, (r - 2) * H + h + 1)
                q = h % 4 * VW
                for c in range(KC):
                    m = nc.tensor.matmul(o_ps[h // 8][q:q + VW, h // 4 % 2], V[i][:, c, h], pr[h % 4][:, c],
                                         start=(c == 0), stop=(c == KC - 1))
                m.then_inc(pv_done, 1)

            def work(r, j):
                i = (j - 2) % R
                for h in range(H):
                    if exists(r - 2):
                        if h == 0:
                            pe.wait_ge(shifted, 32 * (r - 1))
                        reached(pe, p_ready, (r - 2) * H + h - 1)
                        for c in range(KC):
                            m = nc.tensor.matmul(s_ps[h % 2][:, c], KS[i][:, h, c * P:(c + 1) * P],
                                                 QS[i][:, h], start=True, stop=True)
                        m.then_inc(s_made, 1)
                    if exists(r):
                        if h == 0:
                            pe.wait_ge(zeroed, 16 * (r + 1))
                            pe.wait_ge(stacked, 16 * N_STACK * (r + 1))
                        reached(pe, max_ready, r * H + h - 1)
                        for c in range(KC):
                            m = nc.tensor.matmul(m_ps[h % 2][:, c], QS[j][:, h, c * P:(c + 1) * P],
                                                 KS[j][:, h], start=True, stop=True)
                        m.then_inc(m_made, 1)
                    if h == 0 and exists(r + 1):
                        reached(pe, onT_copied, r - 3)
                        reached(pe, shift_ready, r - 1)
                        project_qk(r + 1)
                    if h == 3 and exists(r - 3):
                        pe.wait_ge(oT_copied, 2 * (r - 2))
                        if exists(r + 1):
                            pe.wait_ge(qk_taken, r + 2)
                        elif r > B:
                            pe.wait_ge(onT_copied, r - 3)
                            pe.wait_ge(norm.row_ready, r - 3)
                        if exists(r - 1):
                            pe.wait_ge(v_ready, r)
                        for c, to in enumerate((a_ps, b_ps)):
                            for k in range(4):
                                m = nc.tensor.transpose(to[:].rearrange("p c s -> p (c s)")[:, k * P:(k + 1) * P],
                                                        oT[:, k, c * P:(c + 1) * P], ident[:])
                        m.then_inc(nat_made, 1)
                    if h == 4 and exists(r - 1):
                        pe.wait_ge(pair_ready, r)
                        if exists(r - 3):
                            pe.wait_ge(o_ready, r - 2)
                        else:
                            pe.wait_ge(qk_taken, r + 2)
                        for c in range(KC):
                            m = nc.tensor.transpose(a_ps[0:NPAR * H, 1, c * P:(c + 1) * P],
                                                    pair[:, c].rearrange("p n h -> p (n h)"), ident[:])
                        m.then_inc(pair_turned, 1)
                    if h == 6 and exists(r - 3):
                        pe.wait_ge(o_ready, r - 2)
                        if exists(r - 1):
                            pe.wait_ge(shift_ready, r)
                        for c in range(KC):
                            m = nc.tensor.transpose(a_ps[:, 0, c * P:(c + 1) * P],
                                                    o[:, c].rearrange("p h d -> p (h d)"), ident[:])
                        m.then_inc(onT_made, 1)
                    if h == 9 and exists(r - 3):
                        pe.wait_ge(onT_copied, r - 2)
                        nc.tensor.matmul(b_ps[:, 0], w[:, 3], onT[:], start=True, stop=True).then_inc(y_made, 1)
                    if h == 12 and exists(r):
                        reached(pe, norm.row_ready, r - 2)
                        pe.wait_ge(cin_ready, r + 1)
                        for c in range(KC):
                            m = nc.tensor.matmul(b_ps[:, c, 0:P], cin[j % 2][:, c * P:(c + 1) * P], w[:, 2],
                                                 start=True, stop=True)
                        m.then_inc(v_made, 1)
                    if exists(r - 2):
                        if h >= 2:
                            attend(r, i, h - 2)
                        if h == H - 1:
                            attend(r, i, h - 1)
                            attend(r, i, h)

            project_qk(0)
            rounds(pe, work)

        @block.vector
        def _(dve):
            def natural(r, j):
                dve.wait_ge(nat_made, r - 2)
                s4 = [src[:].rearrange("p c s -> p (c s)").rearrange("p (h e) -> p h e", h=H) for src in (a_ps, b_ps)]
                for c in range(KC):
                    nc.vector.reciprocal(inverse[:, c], s4[c][:, :, FD]).then_inc(inv_ready, 1)
                for c in range(KC):
                    dve.wait_ge(inv_ready, 2 * (r - 2) - 1 + c)
                    m = nc.vector.tensor_tensor(o[:, c], s4[c][:, :, 0:FD],
                                                inverse[:, c, :, None].to_broadcast([P, H, FD]), ALU.mult)
                m.then_inc(o_ready, 1)

            def work(r, j):
                for g in range(H):
                    if exists(r):
                        dve.wait_ge(m_made, r * H + g + 1)
                        if g == 0:
                            reached(dve, pair_ready, r)
                        nc.vector.tensor_reduce(negmax[:, :, g], m_ps[g % 2][:], AX.X, ALU.max,
                                                negate=True).then_inc(max_ready, 1)
                    if g == 3 and exists(r - 3):
                        natural(r, j)
                    if g == 10 and exists(r - 3):
                        dve.wait_ge(y_made, r - 2)
                        nc.vector.scalar_tensor_tensor(norm.row[:], b_ps[:, 0], bias[:, 3:4],
                                                       X[:, bass.ds((r - 3) * D, D)], ALU.add,
                                                       ALU.add).then_inc(norm.row_ready, 1)
                        norm.put(dve, r - 3)
                    if isinstance(r, int) and r == 0 and g in (0, 5, 10):
                        clear(g // 5 + 1)
                if exists(r):
                    dve.wait_ge(max_ready, (r + 1) * H)
                    reached(dve, pair_turned, r)
                    nc.vector.tensor_copy(high[:], negmax[:]).then_inc(high_ready, 1)
                    dve.wait_ge(high_ready, r + 1)
                    nc.vector.tensor_copy(pair[:, :, 0], high[:])
                    nc.vector.tensor_tensor(pair[:, :, 1], negmax[:], high[:],
                                            ALU.subtract).then_inc(pair_ready, 1)

            def clear(n):
                nc.vector.memset(QS[n][:].rearrange("p h s -> p (h s)").bitcast(F32), 0.0)
                nc.vector.memset(KS[n][:], 1.0).then_inc(cleared[n], 1)

            clear(0)
            rounds(dve, work)
            norm.vector_part(dve)


def ffn(nc, room, A, X, ident, eps):
    E, W, SW = 8, 176, 704
    GROUPS = [(e * W, W, e) for e in range(E)] + [(E * W + at, min(256, SW - at), E) for at in range(0, SW, 256)]
    NG = len(GROUPS)
    UP = 4
    LAST = [max(p for p in range(-NG, k) if p % NG % UP == k % UP) + 1 for k in range(NG)]
    INNER = E * W + SW
    CHUNKS = list(range(0, INNER, P))
    BUNDLES = [list(range(n, min(n + 4, len(CHUNKS)))) for n in range(0, len(CHUNKS), 4)]
    NB = len(BUNDLES)
    TOP = 2
    PAD = E + 8 - TOP
    R = 2

    up, down = room.early["up"], room.early["down"]
    up_hi, up_lo = (room.sb(f"up_{n}", [P, KC, 2 * INNER], F32R) for n in ("hi", "lo"))
    down_hi, down_lo = (room.sb(f"down_{n}", [P, len(CHUNKS), D], F32R) for n in ("hi", "lo"))
    w_router = room.early["f_router"]
    xin = room.sb("xin", [P, D])
    reuse = room.early["ctx"]
    hid, at = reuse[:, 0:len(CHUNKS) * P], len(CHUNKS) * P
    xT = [reuse[:, at + j * D:at + (j + 1) * D].rearrange("p (c t) -> p c t", c=KC) for j in range(R)]
    th = [reuse[:, at + (R + j) * D:at + (R + j + 1) * D] for j in range(UP)]
    gate = [reuse[:, at + (R + UP) * D:at + (R + UP + 1) * D], room.sb("gate1", [P, D])]
    xT_hi, xT_lo = ([room.sb(f"xT_{n}{j}", [P, KC, P], F32R) for j in range(R)] for n in ("hi", "lo"))
    hT_hi, hT_lo = ([room.sb(f"hT_{n}{j}", [P, 4, P], F32R) for j in range(2)] for n in ("hi", "lo"))
    logits = room.sb("logits", [P, E + 1])
    negmax = room.sb("negmax", [P, 1])
    total = room.sb("total", [P, 1])
    inverse = room.sb("inverse", [P, 1])
    expd = room.sb("expd", [P, E + 1])
    probs = room.sb("probs", [P, PAD])
    best = room.sb("best", [P, 8])
    places = room.sb("places", [P, 8])
    left = room.sb("left", [P, PAD])
    weight = [room.sb(f"weight{j}", [P, E + 1]) for j in range(R)]
    norm = RowNorm(nc, room, X, eps)
    up_ps = [room.ps([P, 512]) for j in range(UP)]
    hT_ps = [room.ps([P, 4, P]) for j in range(2)]
    y_ps = room.ps([P, 512])
    x_ps = room.ps([P, KC, D])
    r_ps = x_ps[:, 1]

    ready = room.sem("ready")
    xT_split, hT_split, w_hi, w_split, down_high, down_split = room.sems(
        "xT_split hT_split w_hi w_split down_high down_split")
    xin_ready, x_turned, xT_copied = room.sems("xin_ready x_turned xT_copied")
    up_made, th_ready, gate_ready, h_ready = room.sems("up_made th_ready gate_ready h_ready")
    hT_made, hT_copied, down_done = room.sems("hT_made hT_copied down_done")
    r_made, r_taken, r_max, e_ready, r_inv, p_ready = room.sems("r_made r_taken r_max e_ready r_inv p_ready")
    best_ready, list_ready, left_ready, weight_ready = room.sems("best_ready list_ready left_ready weight_ready")

    def rounds(eng, work):
        for r in range(R):
            work(r, r)
        with eng.Fori(R, B - R - 1, R) as r:
            for j in range(R):
                work(r + j, j)
        for r in range(B - R, B + 1):
            work(r, r % R)

    def exists(b):
        return not isinstance(b, int) or 0 <= b < B

    TURN = range(1, NB + 1)
    ROUTE = (4, 7, 8, 9, 10)
    AHEAD = 3

    def columns(k):
        at, n, e = GROUPS[k]
        return slice(2 * at, 2 * (at + n))

    with nc.Block() as block:

        @block.gpsimd
        def _(pool):
            def copy(b):
                reached(pool, x_turned, b)
                nc.gpsimd.tensor_copy(xin[:], X[:, bass.ds(b * D, D)]).then_inc(xin_ready, 1)

            def work(r, j):
                if exists(r + 1):
                    copy(r + 1)
                if isinstance(r, int) and r == 0:
                    pool.wait_ge(down_high, 1)
                    nc.gpsimd.tensor_tensor(down_lo[:], down[:], down_hi[:].bitcast(F32),
                                            ALU.subtract).then_inc(down_split, 1)

            copy(0)
            rounds(pool, work)

        @block.scalar
        def _(act):
            def copy_xT(b, j):
                act.wait_ge(x_turned, b + 1)
                for to in (xT, xT_hi):
                    m = nc.scalar.copy(to[j][:], x_ps[:, 0].rearrange("p (c t) -> p c t", c=KC))
                m.then_inc(xT_copied, 1)

            def split_weights(k):
                nc.scalar.copy(up_hi[:, :, columns(k)], up[:, :, columns(k)]).then_inc(w_hi, 1)

            def router_exp(b):
                act.wait_ge(r_max, b + 1)
                nc.scalar.activation(expd[:, 0:E], logits[:, 0:E], ACT.Exp, bias=negmax[:], accum_out=total[:])
                nc.scalar.activation(expd[:, E:E + 1], logits[:, E:E + 1], ACT.Tanh, scale=0.5).then_inc(e_ready, 1)

            def work(r, j):
                for k in range(NG):
                    n = GROUPS[k][1]
                    if exists(r):
                        act.wait_ge(up_made, r * NG + k + 1)
                        reached(act, gate_ready, r * NG + LAST[k])
                        nc.scalar.activation(th[k % UP][:, 0:n], up_ps[k % UP][:, 0:n],
                                             ACT.Tanh, scale=0.5).then_inc(th_ready, 1)
                    if k in TURN and exists(r - 1):
                        n = TURN.index(k)
                        act.wait_ge(hT_made, (r - 1) * NB + n + 1)
                        reached(act, down_done, (r - 1) * NB + n - 1)
                        m = len(BUNDLES[n])
                        nc.scalar.copy(hT_hi[n % 2][:, 0:m], hT_ps[n % 2][:, 0:m]).then_inc(hT_copied, 1)
                    if k == 1 and exists(r + 1):
                        copy_xT(r + 1, 1 - j)
                    if k == 5 and exists(r + 1):
                        router_exp(r + 1)
                    if isinstance(r, int) and r == 0:
                        if k + AHEAD < NG:
                            split_weights(k + AHEAD)
                        elif k + AHEAD == NG:
                            nc.scalar.copy(down_hi[:], down[:]).then_inc(down_high, 1)

            copy_xT(0, 0)
            for k in range(AHEAD):
                split_weights(k)
            router_exp(0)
            rounds(act, work)
            norm.scalar_part(act)

        @block.tensor
        def _(pe):
            def turn_x(b):
                pe.wait_ge(xin_ready, b + 1)
                for c in range(KC):
                    m = nc.tensor.transpose(x_ps[:, 0, c * P:(c + 1) * P], xin[:, c * P:(c + 1) * P], ident[:])
                m.then_inc(x_turned, 1)

            def router(b, j):
                pe.wait_ge(xT_copied, b + 1)
                for c in range(KC):
                    m = nc.tensor.matmul(r_ps[:, 0:E + 1], xT[j][:, c], w_router[:, c],
                                         start=(c == 0), stop=(c == KC - 1))
                m.then_inc(r_made, 1)

            def down(b, k):
                pe.wait_ge(hT_split, b * NB + k + 1)
                if k == 0:
                    reached(pe, norm.row_ready, b)
                for n, c in enumerate(BUNDLES[k]):
                    m = split_product(nc, y_ps[:, 0:D], (hT_hi[k % 2][:, n], hT_lo[k % 2][:, n]),
                                      (down_hi[:, c], down_lo[:, c]), c == 0, c == len(CHUNKS) - 1)
                m.then_inc(down_done, 1)

            def work(r, j):
                for k in range(NG):
                    if exists(r):
                        at, n, e = GROUPS[k]
                        reached(pe, h_ready, r * NG + LAST[k])
                        if k == 0:
                            pe.wait_ge(xT_split, r + 1)
                        if isinstance(r, int) and r == 0:
                            pe.wait_ge(w_split, k + 1)
                        for c in range(KC):
                            m = split_product(nc, up_ps[k % UP][:, 0:2 * n], (xT_hi[j][:, c], xT_lo[j][:, c]),
                                              (up_hi[:, c, columns(k)], up_lo[:, c, columns(k)]), c == 0, c == KC - 1)
                        m.then_inc(up_made, 1)
                    if k in TURN and exists(r - 1):
                        n = TURN.index(k)
                        if n == 0:
                            pe.wait_ge(h_ready, r * NG)
                        reached(pe, hT_split, (r - 1) * NB + n - 1)
                        for q, c in enumerate(BUNDLES[n]):
                            at = CHUNKS[c]
                            m = nc.tensor.transpose(hT_ps[n % 2][:, q], hid[:, at:at + P], ident[:])
                        m.then_inc(hT_made, 1)
                    if k - 1 in TURN and exists(r - 1):
                        down(r - 1, TURN.index(k - 1))
                    if k == 1 and exists(r + 1):
                        pe.wait_ge(r_taken, r + 1)
                        turn_x(r + 1)
                    if k == NG - 1 and isinstance(r, int) and r == 0:
                        pe.wait_ge(down_split, 1)
                    if k == 3 and exists(r + 1):
                        pe.wait_ge(xT_split, r + 2)
                        router(r + 1, 1 - j)

            turn_x(0)
            pe.wait_ge(xT_split, 1)
            router(0, 0)
            rounds(pe, work)

        @block.vector
        def _(dve):
            def route(b, j, step):
                if step == 0:
                    dve.wait_ge(r_made, b + 1)
                    nc.vector.tensor_copy(logits[:], r_ps[:, 0:E + 1]).then_inc(r_taken, 1)
                    dve.wait_ge(r_taken, b + 1)
                    nc.vector.tensor_reduce(negmax[:], logits[:, 0:E], AX.X, ALU.max, negate=True).then_inc(r_max, 1)
                if step == 1:
                    dve.wait_ge(e_ready, b + 1)
                    nc.vector.reciprocal(inverse[:], total[:]).then_inc(r_inv, 1)
                    dve.wait_ge(r_inv, b + 1)
                    nc.vector.tensor_scalar(probs[:, 0:E], expd[:, 0:E], inverse[:], None, ALU.mult).then_inc(p_ready, 1)
                if step == 2:
                    dve.wait_ge(p_ready, b + 1)
                    nc.vector.memset(places[:], -1.0)
                    nc.vector.max(best[:], probs[:]).then_inc(best_ready, 1)
                    dve.wait_ge(best_ready, b + 1)
                    nc.vector.tensor_copy(places[:, 0:TOP], best[:, 0:TOP]).then_inc(list_ready, 1)
                if step == 3:
                    dve.wait_ge(list_ready, b + 1)
                    nc.vector.tensor_scalar(weight[j][:, E:E + 1], expd[:, E:E + 1], 1.0, 0.25, ALU.add,
                                            ALU.mult).then_inc(weight_ready, 1)
                    nc.vector.match_replace(left[:], places[:], probs[:], -2.0).then_inc(left_ready, 1)
                if step == 4:
                    dve.wait_ge(left_ready, b + 1)
                    nc.vector.tensor_scalar(left[:, 0:E], left[:, 0:E], -2.0, 0.5, ALU.is_equal,
                                            ALU.mult).then_inc(weight_ready, 1)
                    dve.wait_ge(weight_ready, 3 * b + 2)
                    nc.vector.tensor_tensor(weight[j][:, 0:E], left[:, 0:E], probs[:, 0:E],
                                            ALU.mult).then_inc(weight_ready, 1)

            def split_xT(b, j):
                dve.wait_ge(xT_copied, b + 1)
                nc.vector.tensor_tensor(xT_lo[j][:], x_ps[:, 0].rearrange("p (c t) -> p c t", c=KC),
                                        xT_hi[j][:].bitcast(F32), ALU.subtract).then_inc(xT_split, 1)

            def split_weights(k):
                dve.wait_ge(w_hi, k + 1)
                nc.vector.tensor_tensor(up_lo[:, :, columns(k)], up[:, :, columns(k)],
                                        up_hi[:, :, columns(k)].bitcast(F32), ALU.subtract).then_inc(w_split, 1)

            def work(r, j):
                for k in range(NG):
                    if exists(r):
                        at, n, e = GROUPS[k]
                        dve.wait_ge(th_ready, r * NG + k + 1)
                        reached(dve, h_ready, r * NG + (k - 1 if k != 0 else 0))
                        nc.vector.scalar_tensor_tensor(gate[k % 2][:, 0:n], th[k % UP][:, 0:n], 1.0,
                                                       up_ps[k % UP][:, 0:n], ALU.add, ALU.mult).then_inc(gate_ready, 1)
                        dve.wait_ge(gate_ready, r * NG + k + 1)
                        if exists(r - 1):
                            dve.wait_ge(hT_made, (r - 1) * NB + 1 + (at + n - 1) // (4 * P))
                        if k == 0:
                            dve.wait_ge(weight_ready, 3 * (r + 1))
                        nc.vector.scalar_tensor_tensor(hid[:, at:at + n], gate[k % 2][:, 0:n], weight[j][:, e:e + 1],
                                                       up_ps[k % UP][:, n:2 * n], ALU.mult, ALU.mult).then_inc(h_ready, 1)
                    if k in TURN and exists(r - 1):
                        n = TURN.index(k)
                        dve.wait_ge(hT_copied, (r - 1) * NB + n + 1)
                        m = len(BUNDLES[n])
                        nc.vector.tensor_tensor(hT_lo[n % 2][:, 0:m], hT_ps[n % 2][:, 0:m],
                                                hT_hi[n % 2][:, 0:m].bitcast(F32), ALU.subtract).then_inc(hT_split, 1)
                    if k == 1 and exists(r + 1):
                        split_xT(r + 1, 1 - j)
                    if k in ROUTE and exists(r + 1):
                        route(r + 1, 1 - j, ROUTE.index(k))
                    if isinstance(r, int) and r == 0 and k + AHEAD < NG:
                        split_weights(k + AHEAD)
                    if k == 6 and exists(r - 1):
                        dve.wait_ge(down_done, r * NB)
                        nc.vector.tensor_tensor(norm.row[:], X[:, bass.ds((r - 1) * D, D)], y_ps[:, 0:D],
                                                ALU.add).then_inc(norm.row_ready, 1)
                        norm.put(dve, r - 1)

            nc.vector.memset(hid[:, INNER:], 0.0)
            nc.vector.memset(probs[:], -1.0).then_inc(ready, 1)
            dve.wait_ge(ready, 1)
            split_xT(0, 0)
            for k in range(AHEAD):
                split_weights(k)
            for step in range(len(ROUTE)):
                route(0, 0, step)
            rounds(dve, work)
            norm.vector_part(dve)


def low_rank_attention(nc, room, A, X, ident, eps):
    RANK = 32
    SCALE = float(1.0 / np.sqrt(np.float32(RANK)))
    R = 4

    w_rank, wo, bo, mask = (room.early[n] for n in ("r_rank", "r_wo", "r_bo", "causal"))
    xin = [room.sb(f"xin{j}", [P, D]) for j in range(R)]
    xT = [room.sb(f"xT{j}", [P, KC, P]) for j in range(2)]
    sa = [room.sb(f"sa{j}", [RANK, 2, P]) for j in range(2)]
    sc = [room.sb(f"sc{j}", [P, P]) for j in range(2)]
    p = [room.sb(f"p{j}", [P, P]) for j in range(2)]
    negmax = [room.sb(f"negmax{j}", [P, 1]) for j in range(2)]
    total = [room.sb(f"total{j}", [P, 1]) for j in range(2)]
    inverse = room.sb("inverse", [P, 1])
    pT = [room.sb(f"pT{j}", [P, P]) for j in range(2)]
    oT = [room.sb(f"oT{j}", [P, KC, P]) for j in range(2)]
    xb = [room.sb(f"xb{j}", [P, D]) for j in range(R)]
    norm = RowNorm(nc, room, X, eps)
    x_ps = room.ps([P, 512])
    sa_ps = room.ps([P, 512])
    s_ps = room.ps([P, 512])
    pT_ps = room.ps([P, 512])
    o_ps = room.ps([P, 512])
    y_ps = room.ps([P, 512])

    ctx_loaded = room.sem("ctx_loaded")
    xin_ready, x_turned, xT_copied, sa_made, sa_copied = room.sems(
        "xin_ready x_turned xT_copied sa_made sa_copied")
    s_made, s_taken, max_ready, e_ready, inv_ready, p_ready = room.sems(
        "s_made s_taken max_ready e_ready inv_ready p_ready")
    pT_made, pT_copied, o_made, oT_copied, y_made, xb_ready = room.sems(
        "pT_made pT_copied o_made oT_copied y_made xb_ready")

    def rounds(eng, work, last):
        n = 2 * R
        for r in range(n):
            work(r, r % R)
        with eng.Fori(n, B - R + 1, R) as r:
            for j in range(R):
                work(r + j, j)
        for r in range(B, B + last):
            work(r, r % R)

    def exists(b):
        return not isinstance(b, int) or 0 <= b < B

    with nc.Block() as block:

        @block.sync
        def _(sp):
            sp.dma_start(room.early["ctx"][:], A["ctx"]).then_inc(ctx_loaded, 16)
            sp.wait_ge(ctx_loaded, 16)

        @block.gpsimd
        def _(pool):
            def work(r, j):
                if exists(r):
                    reached(pool, norm.row_ready, r - 5)
                    reached(pool, o_made, r - R + 1)
                    nc.gpsimd.tensor_copy(xin[j][:], X[:, bass.ds(r * D, D)]).then_inc(xin_ready, 1)
                if exists(r - 2):
                    if not exists(r):
                        pool.wait_ge(norm.row_ready, r - 5)
                    nc.gpsimd.tensor_tensor(xb[(j - 2) % R][:], X[:, bass.ds((r - 2) * D, D)], bo[:],
                                            ALU.add).then_inc(xb_ready, 1)

            rounds(pool, work, 2)

        @block.scalar
        def _(act):
            def work(r, j):
                i, k = j % 2, (j - 1) % 2
                if exists(r - 1):
                    act.wait_ge(sa_made, r)
                    reached(act, s_made, r - 2)
                    nc.scalar.copy(sa[k][:], sa_ps[0:RANK, 0:2 * P].rearrange("p (c t) -> p c t", c=2)).then_inc(sa_copied, 1)
                if exists(r - 3):
                    act.wait_ge(o_made, r - 2)
                    reached(act, y_made, r - 4)
                    nc.scalar.copy(oT[k][:], o_ps[:, 0:D].rearrange("p (c t) -> p c t", c=KC)).then_inc(oT_copied, 1)
                if exists(r):
                    act.wait_ge(x_turned, r + 1)
                    reached(act, sa_made, r - 1)
                    nc.scalar.copy(xT[i][:], x_ps[:, 0:D].rearrange("p (c t) -> p c t", c=KC)).then_inc(xT_copied, 1)
                if exists(r - 2):
                    act.wait_ge(pT_made, r - 1)
                    reached(act, o_made, r - 3)
                    nc.scalar.copy(pT[i][:], pT_ps[:, 0:P]).then_inc(pT_copied, 1)
                if exists(r - 1):
                    act.wait_ge(max_ready, r)
                    reached(act, pT_made, r - 2)
                    nc.scalar.activation(p[k][:], sc[k][:], ACT.Exp, bias=negmax[k][:],
                                         accum_out=total[k][:]).then_inc(e_ready, 1)

            rounds(act, work, 3)
            norm.scalar_part(act)

        @block.tensor
        def _(pe):
            def work(r, j):
                i, k = j % 2, (j - 1) % 2
                if exists(r):
                    pe.wait_ge(xin_ready, r + 1)
                    reached(pe, xT_copied, r)
                    for c in range(KC):
                        m = nc.tensor.transpose(x_ps[:, c * P:(c + 1) * P], xin[j][:, c * P:(c + 1) * P], ident[:])
                    m.then_inc(x_turned, 1)
                if exists(r - 1):
                    pe.wait_ge(sa_copied, r)
                    reached(pe, s_taken, r - 1)
                    nc.tensor.matmul(s_ps[:, 0:P], sa[k][:, 0], sa[k][:, 1], start=True, stop=True).then_inc(s_made, 1)
                if exists(r - 2):
                    pe.wait_ge(p_ready, r - 1)
                    reached(pe, pT_copied, r - 2)
                    nc.tensor.transpose(pT_ps[:, 0:P], p[i][:], ident[:]).then_inc(pT_made, 1)
                if exists(r - 3):
                    pe.wait_ge(oT_copied, r - 2)
                    reached(pe, norm.row_ready, r - 3)
                    for c in range(KC):
                        m = nc.tensor.matmul(y_ps[:, 0:D], oT[k][:, c], wo[:, c],
                                             start=(c == 0), stop=(c == KC - 1))
                    m.then_inc(y_made, 1)
                if exists(r - 2):
                    pe.wait_ge(pT_copied, r - 1)
                    reached(pe, oT_copied, r - 2)
                    for c in range(KC):
                        m = nc.tensor.matmul(o_ps[:, c * P:(c + 1) * P], xin[(j - 2) % R][:, c * P:(c + 1) * P],
                                             pT[i][:], start=True, stop=True)
                    m.then_inc(o_made, 1)
                if exists(r):
                    pe.wait_ge(xT_copied, r + 1)
                    reached(pe, sa_copied, r)
                    for n in range(2):
                        for c in range(KC):
                            m = nc.tensor.matmul(sa_ps[0:RANK, n * P:(n + 1) * P], w_rank[:, c, n], xT[i][:, c],
                                                 start=(c == 0), stop=(c == KC - 1))
                    m.then_inc(sa_made, 1)

            rounds(pe, work, 3)

        @block.vector
        def _(dve):
            def work(r, j):
                k = (j - 1) % 2
                if exists(r - 1):
                    dve.wait_ge(s_made, r)
                    reached(dve, e_ready, r - 2)
                    nc.vector.scalar_tensor_tensor(sc[k][:], s_ps[:, 0:P], SCALE, mask[:], ALU.mult,
                                                   ALU.add).then_inc(s_taken, 1)
                    dve.wait_ge(s_taken, r)
                    nc.vector.tensor_reduce(negmax[k][:], sc[k][:], AX.X, ALU.max, negate=True).then_inc(max_ready, 1)
                if exists(r - 3):
                    dve.wait_ge(y_made, r - 2)
                    dve.wait_ge(xb_ready, r - 2)
                    nc.vector.tensor_tensor(norm.row[:], xb[(j - 3) % R][:], y_ps[:, 0:D], ALU.add).then_inc(norm.row_ready, 1)
                    norm.put(dve, r - 3)
                if exists(r - 1):
                    dve.wait_ge(e_ready, r)
                    nc.vector.reciprocal(inverse[:], total[k][:]).then_inc(inv_ready, 1)
                    dve.wait_ge(inv_ready, r)
                    nc.vector.tensor_scalar(p[k][:], p[k][:], inverse[:], None, ALU.mult).then_inc(p_ready, 1)

            rounds(dve, work, 3)
            norm.vector_part(dve)


def wkv(nc, room, A, X, ident, eps):
    BG = 4
    NG = B // BG
    T1 = P + 1
    LOW = -1.0e38
    U = NG * KC
    OLD, NEW, CARRY, ENTER = range(4)

    wu = room.early["w_wu"]
    zeros = room.sb("zeros", [P, BG, T1])
    decay = [room.sb(f"decay{c}", [P, BG, T1]) for c in range(KC)]
    ctx = room.early["ctx"]
    k = [room.sb(f"k{j}", [P, BG, T1]) for j in range(2)]
    v = [room.sb(f"v{j}", [P, BG, P]) for j in range(2)]
    o = [room.sb(f"o{j}", [P, BG, T1]) for j in range(2)]
    no = room.sb("no", [P, BG, P])
    arg = [room.sb(f"arg{j}", [P, 4, BG, P]) for j in range(2)]
    ex = [room.sb(f"ex{j}", [P, 4, BG, T1]) for j in range(2)]
    ev = room.sb("ev", [P, BG, T1])
    ps = room.sb("ps", [P, BG, T1])
    qs = room.sb("qs", [P, BG, T1])
    enter = room.sb("enter", [P, BG, P])
    old = room.sb("old", [P, BG, P])
    num = room.sb("num", [P, BG, P])
    den1 = room.sb("den1", [P, BG, P])
    den = room.sb("den", [P, BG, P])
    inv = room.sb("inv", [P, BG, P])
    y = [room.sb(f"y{j}", [P, BG, P]) for j in range(2)]
    norm = RowNorm(nc, room, X, eps)
    k_ps = [room.ps([P, BG, P]) for j in range(2)]
    v_ps = [room.ps([P, BG, P]) for j in range(2)]
    y_ps = [room.ps([P, BG, P]) for j in range(2)]

    cleared, ready = room.sems("cleared ready")
    turned, kv_copied = room.sems("turned kv_copied")
    o_ready, no_ready, arg_dve, arg_pool, ex_ready = room.sems("o_ready no_ready arg_dve arg_pool ex_ready")
    ev_ready, p_ready, q_ready, enter_ready, old_ready = room.sems("ev_ready p_ready q_ready enter_ready old_ready")
    num_ready, den1_ready, den_ready, inv_ready, y_ready = room.sems("num_ready den1_ready den_ready inv_ready y_ready")
    y_turned, added = room.sems("y_turned added")

    def rounds(eng, work):
        for r in range(-1, U + 2):
            work(r, r % 2, r // 2)

    def exists(u):
        return 0 <= u < U

    def part(t, g, c):
        return t[:, g * BG * D:(g + 1) * BG * D].rearrange("p (b d) -> p b d", b=BG)[:, :, c * P:(c + 1) * P]

    def flat(t):
        return t[:].rearrange("p b t -> p (b t)")

    with nc.Block() as block:

        @block.gpsimd
        def _(pool):
            def work(r, c, g):
                i = 1 - c
                if exists(r - 1):
                    pool.wait_ge(ex_ready, r)
                    reached(pool, p_ready, r - 1)
                    nc.gpsimd.tensor_tensor(ev[:, :, 1:], ex[i][:, ENTER, :, 1:], v[i][:], ALU.mult).then_inc(ev_ready, 1)
                    reached(pool, num_ready, r - 1)
                    nc.gpsimd.tensor_tensor(enter[:], ex[i][:, NEW, :, 1:], v[i][:], ALU.mult).then_inc(enter_ready, 1)
                    pool.wait_ge(q_ready, r)
                    nc.gpsimd.tensor_tensor(den1[:], ex[i][:, OLD, :, 1:], qs[:, :, 0:P], ALU.mult).then_inc(den1_ready, 1)
                    pool.wait_ge(den1_ready, r)
                    reached(pool, inv_ready, r - 1)
                    nc.gpsimd.tensor_tensor(den[:], den1[:], ex[i][:, NEW, :, 1:], ALU.add).then_inc(den_ready, 1)
                if exists(r):
                    pool.wait_ge(o_ready, r + 1)
                    reached(pool, ex_ready, r - 1)
                    nc.gpsimd.tensor_tensor(arg[c][:, ENTER], k[c][:, :, 1:], o[c][:, :, 1:], ALU.subtract)
                    pool.wait_ge(no_ready, r + 1)
                    nc.gpsimd.tensor_tensor(arg[c][:, OLD], o[c][:, :, 0:P], no[:], ALU.subtract).then_inc(arg_pool, 1)

            nc.gpsimd.memset(zeros[:], 0.0)
            nc.gpsimd.memset(ev[:], 0.0)
            for j in range(2):
                nc.gpsimd.memset(k[j][:], LOW)
                m = nc.gpsimd.memset(ex[j][:], 0.0)
            m.then_inc(cleared, 1)
            pool.wait_ge(cleared, 1)
            rounds(pool, work)

        @block.scalar
        def _(act):
            def work(r, c, g):
                if exists(r + 1):
                    i = 1 - c
                    act.wait_ge(turned, r + 2)
                    nc.scalar.copy(k[i][:, :, 1:], k_ps[i][:])
                    reached(act, enter_ready, r)
                    nc.scalar.copy(v[i][:], v_ps[i][:]).then_inc(kv_copied, 1)
                if exists(r):
                    act.wait_ge(arg_dve, r + 1)
                    act.wait_ge(arg_pool, r + 1)
                    reached(act, num_ready, r - 1)
                    reached(act, den_ready, r - 1)
                    nc.scalar.activation(ex[c][:, :, :, 1:].rearrange("p k b t -> p (k b) t"),
                                         arg[c][:].rearrange("p k b t -> p (k b) t"), ACT.Exp).then_inc(ex_ready, 1)

            act.wait_ge(cleared, 1)
            rounds(act, work)
            norm.scalar_part(act)

        @block.tensor
        def _(pe):
            def work(r, c, g):
                if exists(r + 1):
                    i, h = 1 - c, (r + 1) // 2
                    reached(pe, kv_copied, r)
                    for n in range(BG):
                        nc.tensor.transpose(k_ps[i][:, n], part(X, h, i)[:, n], ident[:])
                        m = nc.tensor.transpose(v_ps[i][:, n], part(ctx, h, i)[:, n], ident[:])
                    m.then_inc(turned, 1)
                if exists(r - 2):
                    pe.wait_ge(y_ready, r - 1)
                    reached(pe, added, r - 3)
                    for n in range(BG):
                        m = nc.tensor.transpose(y_ps[c][:, n], y[c][:, n], ident[:])
                    m.then_inc(y_turned, 1)

            rounds(pe, work)

        @block.vector
        def _(dve):
            def work(r, c, g):
                if exists(r):
                    w, u = wu[:, 0, c:c + 1], wu[:, 1, c:c + 1]
                    dve.wait_ge(kv_copied, r + 1)
                    reached(dve, arg_pool, r - 1)
                    nc.vector.tensor_tensor_scan(flat(o[c]), flat(decay[c]), flat(k[c]), LOW, ALU.add,
                                                 ALU.max).then_inc(o_ready, 1)
                    dve.wait_ge(o_ready, r + 1)
                    reached(dve, arg_pool, r)
                    nc.vector.scalar_tensor_tensor(no[:], k[c][:, :, 1:], u, o[c][:, :, 0:P], ALU.add,
                                                   ALU.max).then_inc(no_ready, 1)
                    reached(dve, ex_ready, r - 1)
                    nc.vector.scalar_tensor_tensor(arg[c][:, CARRY], o[c][:, :, 0:P], w, o[c][:, :, 1:], ALU.add,
                                                   ALU.subtract)
                    dve.wait_ge(no_ready, r + 1)
                    nc.vector.scalar_tensor_tensor(arg[c][:, NEW], k[c][:, :, 1:], u, no[:], ALU.add,
                                                   ALU.subtract).then_inc(arg_dve, 1)
                i = 1 - c
                if exists(r - 1):
                    dve.wait_ge(ex_ready, r)
                    reached(dve, den1_ready, r - 1)
                    nc.vector.tensor_tensor_scan(flat(qs), ex[i][:, CARRY].rearrange("p b t -> p (b t)"),
                                                 ex[i][:, ENTER].rearrange("p b t -> p (b t)"), 0.0, ALU.mult,
                                                 ALU.add).then_inc(q_ready, 1)
                    dve.wait_ge(ev_ready, r)
                    nc.vector.tensor_tensor_scan(flat(ps), ex[i][:, CARRY].rearrange("p b t -> p (b t)"), flat(ev),
                                                 0.0, ALU.mult, ALU.add).then_inc(p_ready, 1)
                    dve.wait_ge(p_ready, r)
                    nc.vector.tensor_tensor(old[:], ex[i][:, OLD, :, 1:], ps[:, :, 0:P], ALU.mult).then_inc(old_ready, 1)
                    dve.wait_ge(old_ready, r)
                    dve.wait_ge(enter_ready, r)
                    nc.vector.tensor_tensor(num[:], old[:], enter[:], ALU.add).then_inc(num_ready, 1)
                    dve.wait_ge(den_ready, r)
                    nc.vector.reciprocal(inv[:], den[:]).then_inc(inv_ready, 1)
                    dve.wait_ge(inv_ready, r)
                    reached(dve, y_turned, r - 2)
                    nc.vector.tensor_tensor(y[i][:], num[:], inv[:], ALU.mult).then_inc(y_ready, 1)
                if exists(r - 2):
                    dve.wait_ge(y_turned, r - 1)
                    nc.vector.tensor_tensor(part(X, g - 1, c), part(X, g - 1, c), y_ps[c][:], ALU.add).then_inc(added, 1)

            dve.wait_ge(cleared, 1)
            for c in range(KC):
                nc.vector.memset(decay[c][:], LOW).then_inc(ready, 1)
                dve.wait_ge(ready, 2 * c + 1)
                nc.vector.tensor_scalar(decay[c][:, :, 1:], zeros[:, :, 1:], wu[:, 0, c:c + 1], None,
                                        ALU.add).then_inc(ready, 1)
            dve.wait_ge(ready, 2 * KC)
            rounds(dve, work)
            norm.all_rows(dve, added, U)
            norm.vector_part(dve)


def mixture(nc, room, A, X, ident, eps):
    E, I, TOP = 16, 256, 4
    IC = I // P
    LIMIT, ALPHA = 7.0, 1.702
    PAD = E + 8 - TOP
    NT = 512
    TT = B * P // NT
    TB = NT // P
    R = 2

    norm_w, w_gate, b_gate, b2, b1 = (room.early[n] for n in ("m_norm", "m_gate", "m_bgate", "m_b2", "m_b1"))
    w1 = [room.sb(f"w1_{j}", [P, KC, IC, 2, P]) for j in range(R)]
    w2 = [room.sb(f"w2_{j}", [P, IC, D]) for j in range(R)]
    w1_hi, w1_lo = ([room.sb(f"w1_{n}{j}", [P, KC, IC, 2, P], F32R) for j in range(R)] for n in ("hi", "lo"))
    w2_hi, w2_lo = ([room.sb(f"w2_{n}{j}", [P, IC, D], F32R) for j in range(R)] for n in ("hi", "lo"))
    ss = room.sb("ss", [P, B])
    rms = room.sb("rms", [P, B])
    scale = room.sb("scale", [P, B])
    tin = [room.sb(f"tin{j}", [P, 2, D]) for j in range(R)]
    tT = room.sb("tT", [P, KC * B * P])
    tT_hi, tT_lo = (room.sb(f"tT_{n}", [P, KC * B * P], F32R) for n in ("hi", "lo"))
    logits = room.sb("logits", [P, B, PAD])
    best = room.sb("best", [P, B, 8])
    places = room.sb("places", [P, B, 8])
    left = room.sb("left", [P, B, PAD])
    below = room.sb("below", [P, B, E])
    chosen = room.sb("chosen", [P, B, E])
    expd = room.sb("expd", [P, B, E])
    kept = room.sb("kept", [P, B, E])
    total = room.sb("total", [P, B])
    inverse = room.sb("inverse", [P, B])
    gates = room.sb("gates", [P, B * E])
    gT = room.sb("gT", [E, 4, TB * P])
    a = [room.sb(f"a{j}", [P, NT]) for j in range(2)]
    sg = [room.sb(f"sg{j}", [P, NT]) for j in range(2)]
    ag = [room.sb(f"ag{j}", [P, NT]) for j in range(2)]
    bb = [room.sb(f"bb{j}", [P, NT]) for j in range(2)]
    act_ = [room.sb(f"act{j}", [P, IC, NT]) for j in range(2)]
    act_hi, act_lo = ([room.sb(f"act_{n}{j}", [P, IC, NT], F32R) for j in range(2)] for n in ("hi", "lo"))
    norm = RowNorm(nc, room, X, eps)
    norm.in_loop = False
    up_ps = [[room.ps([P, NT]) for h in range(2)] for ic in range(IC)]
    y_ps = [[room.ps([P, 2, D]) for h in range(2)] for j in range(2)]
    x_ps = up_ps[0] + up_ps[1]
    l_ps = y_ps[0][0].rearrange("p c d -> p (c d)")[:, 0:B * E]
    g_ps, b_ps = y_ps[0] + y_ps[1], up_ps[0] + up_ps[1]

    ready, filled, squared, rms_ready, scale_ready = room.sems("ready filled squared rms_ready scale_ready")
    w1_loaded = room.sems("w1_loaded0 w1_loaded1")
    w2_loaded = room.sems("w2_loaded0 w2_loaded1")
    tin_ready, t_turned, t_copied = room.sems("tin_ready t_turned t_copied")
    l_made, l_ready, best_ready, list_ready, left_ready, below_ready = room.sems(
        "l_made l_ready best_ready list_ready left_ready below_ready")
    chosen_ready, e_ready, kept_ready, total_ready, inv_ready, g_ready = room.sems(
        "chosen_ready e_ready kept_ready total_ready inv_ready g_ready")
    g_turned, g_copied, b2_made, b2_added = room.sems("g_turned g_copied b2_made b2_added")
    up_made, a_ready, b_ready, sg_ready, ag_ready, act_ready = room.sems(
        "up_made a_ready b_ready sg_ready ag_ready act_ready")
    t_hi, t_lo, w_hi, w_lo, a_hi, a_lo = room.sems("t_hi t_lo w_hi w_lo a_hi a_lo")
    down_done, y_added = room.sems("down_done y_added")

    PAIRS = B // 2

    def tile_part(n):
        at = (n % KC * TT + n // KC) * NT
        return slice(at, at + NT)

    U = E * TT

    def experts(eng, work):
        for e in range(R):
            for tt in range(TT):
                work(e, tt, e)
        with eng.Fori(R, E - R - 1, R) as e:
            for j in range(R):
                for tt in range(TT):
                    work(e + j, tt, j)
        for e in range(E - R, E):
            for tt in range(TT):
                work(e, tt, e % R)
        work(E, 0, 0)

    def loads(e, j):
        return 16 * (e // R + 1) if isinstance(e, int) else (e - j) * (16 // R) + 16

    def following(e, j):
        return None if isinstance(e, int) and e + 1 >= E else (e + 1, 1 - j)

    def live(e, tt, back=0):
        return not isinstance(e, int) or 0 <= e * TT + tt - back < U

    with nc.Block() as block:

        @block.sync
        def _(sp):
            def load(e, j):
                sp.dma_start(w1[j][:].rearrange("p c i h n -> p (c i h n)"),
                             A["m_w1"][bass.ds(e, 1)].rearrange("o p n -> (o p) n")).then_inc(w1_loaded[j], 16)
                sp.dma_start(w2[j][:].rearrange("p c n -> p (c n)"),
                             A["m_w2"][bass.ds(e, 1)].rearrange("o p n -> (o p) n")).then_inc(w2_loaded[j], 16)

            for e in range(R):
                load(e, e)
            with sp.Fori(R, E - 1, R) as e:
                for j in range(R):
                    sp.wait_ge(w_lo, 2 * (e + j - 1))
                    load(e + j, j)
            for j in range(R):
                sp.wait_ge(w1_loaded[j], 16 * E // R)
                sp.wait_ge(w2_loaded[j], 16 * E // R)

        @block.gpsimd
        def _(pool):
            def split_weights(e, j):
                for n, (raw, hi, lo) in enumerate(((w1, w1_hi, w1_lo), (w2, w2_hi, w2_lo))):
                    pool.wait_ge(w_hi, 2 * e + n + 1)
                    nc.gpsimd.tensor_tensor(lo[j][:], raw[j][:], hi[j][:].bitcast(F32), ALU.subtract).then_inc(w_lo, 1)

            def unit(e, tt, j):
                if live(e, tt):
                    u = (e * TT + tt) * IC
                    for ic in range(IC):
                        pool.wait_ge(sg_ready, u + ic + 1)
                        reached(pool, act_ready, u + ic - 1)
                        nc.gpsimd.tensor_tensor(ag[ic][:], a[ic][:], sg[ic][:], ALU.mult).then_inc(ag_ready, 1)
                    for ic in range(IC):
                        pool.wait_ge(a_hi, u + ic + 1)
                        nc.gpsimd.tensor_tensor(act_lo[tt % 2][:, ic], act_[tt % 2][:, ic],
                                                act_hi[tt % 2][:, ic].bitcast(F32), ALU.subtract).then_inc(a_lo, 1)
                    if tt == 1 and following(e, j):
                        split_weights(*following(e, j))

            split_weights(0, 0)
            for n in range(KC * TT):
                pool.wait_ge(t_hi, n + 1)
                at = tile_part(n)
                nc.gpsimd.tensor_tensor(tT_lo[:, at], tT[:, at], tT_hi[:, at].bitcast(F32),
                                        ALU.subtract).then_inc(t_lo, 1)
            experts(pool, unit)

        @block.scalar
        def _(act):
            def split_weights(e, j):
                for n, (raw, hi, loaded) in enumerate(((w1, w1_hi, w1_loaded), (w2, w2_hi, w2_loaded))):
                    act.wait_ge(loaded[j], loads(e, j))
                    reached(act, down_done, (e - 1) * TT)
                    nc.scalar.copy(hi[j][:], raw[j][:]).then_inc(w_hi, 1)

            def unit(e, tt, j):
                if live(e, tt):
                    u = (e * TT + tt) * IC
                    for ic in range(IC):
                        act.wait_ge(a_ready, u + ic + 1)
                        reached(act, ag_ready, u + ic - 1)
                        nc.scalar.activation(sg[ic][:], a[ic][:], ACT.Sigmoid, scale=ALPHA).then_inc(sg_ready, 1)
                    for ic in range(IC):
                        act.wait_ge(act_ready, u + ic + 1)
                        reached(act, down_done, e * TT + tt - 1)
                        nc.scalar.copy(act_hi[tt % 2][:, ic], act_[tt % 2][:, ic]).then_inc(a_hi, 1)
                    if tt == 1 and following(e, j):
                        split_weights(*following(e, j))

            for b in range(B):
                m = nc.scalar.activation(tT[:, b * D:(b + 1) * D], X[:, b * D:(b + 1) * D], ACT.Square,
                                         accum_out=ss[:, b:b + 1])
            m.then_inc(squared, 1)
            act.wait_ge(squared, 1)
            nc.scalar.activation(rms[:], ss[:], ACT.Sqrt, scale=1.0 / D, bias=eps[:]).then_inc(rms_ready, 1)
            split_weights(0, 0)
            for n in range(PAIRS):
                act.wait_ge(t_turned, n + 1)
                for c in range(KC):
                    at = (c * B + 2 * n) * P
                    m = nc.scalar.mul(tT[:, at:at + 2 * P], x_ps[n % 4][:, c * 2 * P:(c + 1) * 2 * P], norm_w[:, c:c + 1])
                m.then_inc(t_copied, 1)
            act.wait_ge(below_ready, 1)
            nc.scalar.activation(expd[:], below[:], ACT.Exp).then_inc(e_ready, 1)
            for n in range(4):
                act.wait_ge(g_turned, n + 1)
                nc.scalar.copy(gT[:, n], g_ps[n][0:E].rearrange("p c d -> p (c d)")).then_inc(g_copied, 1)
            experts(act, unit)
            norm.scalar_part(act)

        @block.tensor
        def _(pe):
            def unit(e, tt, j):
                u = e * TT + tt
                if live(e, tt):
                    if tt == 0:
                        pe.wait_ge(w_lo, 2 * (e + 1))
                    if isinstance(e, int) and e == 0:
                        pe.wait_ge(t_lo, (tt + 1) * KC)
                    for ic in range(IC):
                        reached(pe, b_ready, (u - 1) * IC + ic + 1)
                        reached(pe, a_ready, (u - 1) * IC + ic + 1)
                        for h in range(2):
                            for c in range(KC):
                                at = c * B * P + tt * NT
                                m = split_product(nc, up_ps[ic][h][:], (w1_hi[j][:, c, ic, h], w1_lo[j][:, c, ic, h]),
                                                  (tT_hi[:, at:at + NT], tT_lo[:, at:at + NT]), c == 0, c == KC - 1)
                            m.then_inc(up_made, 1)
                if live(e, tt, 1):
                    i = j if tt else 1 - j
                    v = (tt - 1) % 2
                    pe.wait_ge(a_lo, u * IC)
                    reached(pe, y_added, u - 2)
                    for n in range(TB):
                        for c in range(IC):
                            cols = slice(n * P, (n + 1) * P)
                            m = split_product(nc, y_ps[v][n // 2][:, n % 2], (act_hi[v][:, c, cols], act_lo[v][:, c, cols]),
                                              (w2_hi[i][:, c], w2_lo[i][:, c]), c == 0, c == IC - 1)
                    m.then_inc(down_done, 1)

            for n in range(PAIRS + 1):
                if n < PAIRS:
                    pe.wait_ge(tin_ready, n + 1)
                    reached(pe, t_copied, n - 3)
                    for q in range(2):
                        for c in range(KC):
                            m = nc.tensor.transpose(x_ps[n % 4][:, (2 * c + q) * P:(2 * c + q + 1) * P],
                                                    tin[n % R][:, q, c * P:(c + 1) * P], ident[:])
                    m.then_inc(t_turned, 1)
                if n >= 1:
                    pe.wait_ge(t_copied, n)
                    for b in (2 * n - 2, 2 * n - 1):
                        for c in range(KC):
                            m = nc.tensor.matmul(l_ps[:, b * E:(b + 1) * E], tT[:, (c * B + b) * P:(c * B + b + 1) * P],
                                                 w_gate[:, c], start=(c == 0), stop=(c == KC - 1))
                    m.then_inc(l_made, 1)
            pe.wait_ge(g_ready, 1)
            for n in range(4):
                for q in range(TB):
                    at = (n * TB + q) * E
                    m = nc.tensor.transpose(g_ps[n][0:E].rearrange("p c d -> p (c d)")[:, q * P:(q + 1) * P],
                                            gates[:, at:at + E], ident[:])
                m.then_inc(g_turned, 1)
            for n in range(B // 2):
                pe.wait_ge(g_copied, n // 2 + 1)
                reached(pe, b2_added, n - 3)
                for q in range(2):
                    b = 2 * n + q
                    m = nc.tensor.matmul(b_ps[n % 4][:, q * D:(q + 1) * D], gT[:, b // TB, b % TB * P:(b % TB + 1) * P],
                                         b2[:], start=True, stop=True)
                m.then_inc(b2_made, 1)
            pe.wait_ge(b2_added, B // 2)
            experts(pe, unit)

        @block.vector
        def _(dve):
            def route():
                dve.wait_ge(l_made, PAIRS)
                nc.vector.tensor_tensor(logits[:, :, 0:E], l_ps.rearrange("p (b e) -> p b e", b=B),
                                        b_gate[:, None, :].to_broadcast([P, B, E]), ALU.add).then_inc(l_ready, 1)
                dve.wait_ge(l_ready, 1)
                for b in range(B):
                    nc.vector.max(best[:, b], logits[:, b]).then_inc(best_ready, 1)
                dve.wait_ge(best_ready, B)
                nc.vector.tensor_copy(places[:, :, 0:TOP], best[:, :, 0:TOP]).then_inc(list_ready, 1)
                nc.vector.tensor_tensor(below[:], logits[:, :, 0:E], best[:, :, 0:1].to_broadcast([P, B, E]),
                                        ALU.subtract).then_inc(below_ready, 1)
                dve.wait_ge(list_ready, 1)
                for b in range(B):
                    nc.vector.match_replace(left[:, b], places[:, b], logits[:, b], NEG).then_inc(left_ready, 1)
                dve.wait_ge(left_ready, B)
                nc.vector.tensor_tensor(chosen[:], left[:, :, 0:E], logits[:, :, 0:E], ALU.not_equal).then_inc(chosen_ready, 1)
                dve.wait_ge(chosen_ready, 1)
                dve.wait_ge(e_ready, 1)
                nc.vector.tensor_tensor(kept[:], expd[:], chosen[:], ALU.mult).then_inc(kept_ready, 1)
                dve.wait_ge(kept_ready, 1)
                nc.vector.tensor_reduce(total[:], kept[:], AX.X, ALU.add).then_inc(total_ready, 1)
                dve.wait_ge(total_ready, 1)
                nc.vector.reciprocal(inverse[:], total[:]).then_inc(inv_ready, 1)
                dve.wait_ge(inv_ready, 1)
                nc.vector.tensor_tensor(gates[:].rearrange("p (b e) -> p b e", b=B), kept[:],
                                        inverse[:, :, None].to_broadcast([P, B, E]), ALU.mult).then_inc(g_ready, 1)

            def unit(e, tt, j):
                u = e * TT + tt
                if live(e, tt):
                    for ic in range(IC):
                        n = u * IC + ic
                        dve.wait_ge(up_made, 2 * n + 1)
                        reached(dve, ag_ready, n - 1)
                        nc.vector.tensor_scalar(a[ic][:], up_ps[ic][0][:], b1[:, bass.ds(e, 1), 0, ic],
                                                LIMIT, ALU.add, ALU.min).then_inc(a_ready, 1)
                        dve.wait_ge(up_made, 2 * n + 2)
                        reached(dve, act_ready, n - 1)
                        nc.vector.tensor_scalar(bb[ic][:], up_ps[ic][1][:], b1[:, bass.ds(e, 1), 1, ic],
                                                LIMIT + 1.0, ALU.add, ALU.min).then_inc(b_ready, 1)
                    dve.wait_ge(b_ready, (u + 1) * IC)
                    for ic in range(IC):
                        n = u * IC + ic
                        dve.wait_ge(ag_ready, n + 1)
                        reached(dve, a_lo, (u - 1) * IC)
                        nc.vector.scalar_tensor_tensor(act_[tt % 2][:, ic], bb[ic][:], 1.0 - LIMIT, ag[ic][:],
                                                       ALU.max, ALU.mult).then_inc(act_ready, 1)
                if live(e, tt, 1):
                    v = (tt - 1) % 2
                    dve.wait_ge(down_done, u)
                    for n in range(TB):
                        at = (tt - 1) % TT * TB + n
                        eb = e if tt else e - 1
                        row = X[:, at * D:(at + 1) * D]
                        m = nc.vector.scalar_tensor_tensor(row, y_ps[v][n // 2][:, n % 2],
                                                           gates[:, bass.ds(at * E + eb, 1)], row, ALU.mult, ALU.add)
                    m.then_inc(y_added, 1)
                    if isinstance(e, int) and u - 1 >= (E - 1) * TT:
                        dve.wait_ge(y_added, u)
                        for n in range(TB):
                            norm.moments_of(dve, (tt - 1) % TT * TB + n)

            nc.vector.memset(logits[:], NEG)
            nc.vector.memset(places[:], NEG).then_inc(ready, 1)
            dve.wait_ge(ready, 1)
            dve.wait_ge(rms_ready, 1)
            nc.vector.reciprocal(scale[:], rms[:]).then_inc(scale_ready, 1)
            dve.wait_ge(scale_ready, 1)
            nc.vector.tensor_scalar(b1[:, :, 1], b1[:, :, 1], 1.0, None, ALU.add).then_inc(filled, 1)
            dve.wait_ge(filled, 1)
            def high(tt):
                dve.wait_ge(t_copied, (tt + 1) * TB // 2)
                for n in range(tt * KC, (tt + 1) * KC):
                    nc.vector.tensor_copy(tT_hi[:, tile_part(n)], tT[:, tile_part(n)]).then_inc(t_hi, 1)

            for n in range(PAIRS):
                reached(dve, t_turned, n - 1)
                for q in range(2):
                    b = 2 * n + q
                    m = nc.vector.tensor_scalar(tin[n % R][:, q], X[:, b * D:(b + 1) * D], scale[:, b:b + 1], None,
                                                ALU.mult)
                m.then_inc(tin_ready, 1)
                if n % 2 and n >= 3:
                    high(n // 2 - 1)
            high(TT - 1)
            route()
            for n in range(B // 2):
                dve.wait_ge(b2_made, n + 1)
                rows = X[:, n * 2 * D:(n + 1) * 2 * D]
                nc.vector.scalar_tensor_tensor(rows, rows, 2.0, b_ps[n % 4][:], ALU.mult, ALU.add).then_inc(b2_added, 1)
            dve.wait_ge(b2_added, B // 2)
            experts(dve, unit)
            norm.vector_part(dve)


def rotary_tables():
    f = np.float32
    inv = (f(1.0) / np.power(f(10000.0), np.arange(0, HD, 2, dtype=f) / f(HD))).astype(f)
    ang = np.arange(P, dtype=f)[:, None] * inv[None, :]
    c, s = np.cos(ang).astype(f), np.sin(ang).astype(f)
    return np.concatenate([c, c], -1), np.concatenate([-s, s], -1)


def band_mask(window):
    i, j = np.arange(P)[:, None], np.arange(P)[None, :]
    return np.where((j <= i) & (j > i - window), 0.0, NEG).astype(np.float32)


def by_feature(w, name):
    if name in "vo":
        return w
    return w.reshape(H, P // H, -1).transpose(1, 0, 2).reshape(w.shape)


def lay_out(t):
    c = np.ascontiguousarray
    t = {k: np.asarray(v) for k, v in t.items()}
    cos, sin = rotary_tables()
    up = [w for w in t["L0_ffn_w13"]]
    g, u = np.split(t["L0_ffn_shared_gate_up_w"], 2)
    for at in range(0, len(g), 256):
        up += [g[at:at + 256], u[at:at + 256]]
    down = np.concatenate([t["L0_ffn_w2"].transpose(0, 2, 1).reshape(-1, D), t["L0_ffn_shared_down_w"].T])
    return {
        "x": c(t["x"].transpose(1, 0, 2)),
        "ident": np.eye(P, dtype=np.float32),
        "cos": cos, "sin": sin, "mask": band_mask(WINDOW),
        "wqkv": c(t["L0_attn_w_qkv"].reshape(3, G, GW, KC, P).transpose(4, 3, 1, 0, 2)),
        "ctx": c(t["ctx_2048"].transpose(1, 0, 2)).reshape(P, B * D),
        "xw": c(np.stack([by_feature(t[f"L0_xattn_W{n}"], n).T for n in "qkvo"], 1)),
        "xbias": c(np.stack([by_feature(t[f"L0_xattn_b{n}"], n) for n in "qkvo"], 1)),
        "causal": band_mask(P),
        "m_norm": c(t["L1_ffn_norm_w"].reshape(KC, P).T),
        "m_gate": c(t["L1_ffn_gate_w"].T.reshape(KC, P, 16).transpose(1, 0, 2)),
        "m_bgate": t["L1_ffn_gate_b"],
        "m_b2": t["L1_ffn_b2"],
        "m_b1": c(t["L1_ffn_b1"].reshape(16, KC, P, 2).transpose(2, 0, 3, 1)),
        "m_w1": c(t["L1_ffn_w1"].reshape(16, KC, P, 2, KC, P).transpose(0, 5, 4, 1, 3, 2)).reshape(16, P, -1),
        "m_w2": c(t["L1_ffn_w2"].reshape(16, D, KC, P).transpose(0, 3, 2, 1)).reshape(16, P, -1),
        "w_wu": c(np.stack([t["L1_xattn_w"], t["L1_xattn_u"]]).reshape(2, KC, P).transpose(2, 0, 1)),
        "r_rank": c(np.stack([t["L1_attn_Ws"], t["L1_attn_Wa"]], 1).reshape(KC, P, 2, 32).transpose(1, 0, 2, 3)),
        "r_wo": c(t["L1_attn_Wo"].T.reshape(KC, P, D).transpose(1, 0, 2)),
        "r_bo": t["L1_attn_bo"],
        "f_router": c(np.concatenate([t["L0_ffn_gate_w"], t["L0_ffn_shared_gate_w"]]).reshape(9, KC, P).transpose(2, 1, 0)),
        "f_up": c(np.concatenate(up, 0).reshape(-1, KC, P).transpose(2, 1, 0)),
        "f_down": c(np.concatenate([down, np.zeros((-len(down) % P, D), np.float32)]).reshape(-1, P, D).transpose(1, 0, 2)),
        "wo": c(t["L0_attn_w_o"].reshape(D, H, P).transpose(2, 1, 0)),
    }


def program(nc, A, out):
    with ExitStack() as outer:
        banks = [outer.enter_context(nc.psum_tensor(f"bank{n}", [P, 512], F32)) for n in range(8)]
        room = Room(nc, outer, "all", banks)
        X = room.sb("X", [P, B * D])
        ident = room.sb("ident", [P, P])
        eps = room.sb("eps", [P, 1])
        early = {name: room.sb(name, shape) for name, shape in EARLY.items()}
        stored = room.sem("stored")

        def run(stage, letter):
            with ExitStack() as stack:
                own = Room(nc, stack, letter, banks, early)
                stage(nc, own, A, X, ident, eps)
                own.close()

        run(self_attention, "A")
        early.update((name, room.sb(name, shape)) for name, shape in LATER.items())
        with ExitStack() as both:
            for name in ("up", "down"):
                early[name] = Room(nc, both, "BC", banks).sb(name, A[f"f_{name}"].shape)
            run(cross_attention, "B")
            run(ffn, "C")
        run(low_rank_attention, "D")
        run(wkv, "E")
        run(mixture, "F")
        with nc.Block() as block:

            @block.sync
            def _(sp):
                sp.dma_start(out.rearrange("b t d -> t b d"), X[:].rearrange("p (b d) -> p b d", b=B)).then_inc(stored, 16)
                sp.wait_ge(stored, 16)


def kernel(**inputs):
    import concourse.bacc as bacc
    from concourse.bass_utils import run_bass_kernel_spmd

    arrays = lay_out(inputs)
    nc = bacc.Bacc("TRN2", target_bir_lowering=False, num_devices=1)
    A = {n: nc.dram_tensor(f"in_{n}", a.shape, mybir.dt.from_np(a.dtype), kind="ExternalInput").ap()
         for n, a in arrays.items()}
    out = nc.dram_tensor("out", (B, P, D), F32, kind="ExternalOutput").ap()
    program(nc, A, out)
    r = run_bass_kernel_spmd(nc, [{f"in_{n}": a for n, a in arrays.items()}], core_ids=[0])
    return r.results[0]["out"]
```
